# Optimizing a Trainium2 kernel written in Bass

```python
import numpy as np
import jax
import jax.numpy as jnp

def _softmax(x, axis=-1):
    return jax.nn.softmax(x, axis=axis)

def _gelu(x):
    return jax.nn.gelu(x, approximate=True)

def _silu(x):
    return jax.nn.silu(x)

def _sigmoid(x):
    return jax.nn.sigmoid(x)

def _layernorm(x, axis=-1, eps=1e-05):
    m = jnp.mean(x, axis=axis, keepdims=True)
    v = jnp.var(x, axis=axis, keepdims=True)
    return (x - m) / jnp.sqrt(v + eps)

def _scatter_add(tgt, idx, src, axis=0):
    return tgt.at[idx].add(src)

def _segment_sum(src, seg, n):
    return jax.ops.segment_sum(src, seg, n)
kernel_name = 'mk_hybrid_d2_jaxref_r8_330d3e'

def setup_inputs(seed: int=0):
    np.random.seed(seed)
    _w = jnp.asarray

    def _L0_attn_a_setup():
        import jax, jax.numpy as jnp
        import numpy as np
        B, S, D_IN, D_OUT = (4, 512, 128, 128)
        key = jax.random.key(seed)
        kx, kq, kk, kv = jax.random.split(key, 4)
        scale = 1.0 / np.sqrt(D_IN)
        return {'x': jax.random.normal(kx, (B, S, D_IN), dtype=jnp.float32), 'W_query': jax.random.uniform(kq, (D_OUT, D_IN), jnp.float32, -scale, scale), 'W_key': jax.random.uniform(kk, (D_OUT, D_IN), jnp.float32, -scale, scale), 'W_value': jax.random.uniform(kv, (D_OUT, D_IN), jnp.float32, -scale, scale)}
    _L0_attn_a_in = _L0_attn_a_setup()

    def _L0_attn_b_setup():
        import jax, jax.numpy as jnp
        import numpy as np
        HEADS = 16
        DIM_HEAD = 64
        DIM = 128
        INNER = HEADS * DIM_HEAD
        SCALE = DIM_HEAD ** (-0.5)
        key = jax.random.key(seed)
        k1, k2, k3 = jax.random.split(key, 3)
        x = jax.random.normal(k1, (4, 1024, DIM), dtype=jnp.float32)
        Wqkv = jax.random.normal(k2, (DIM, INNER * 3), dtype=jnp.float32) * DIM ** (-0.5)
        Wout = jax.random.normal(k3, (INNER, DIM), dtype=jnp.float32) * INNER ** (-0.5)
        bout = jnp.zeros((DIM,), dtype=jnp.float32)
        return {'x': x, 'Wqkv': Wqkv, 'Wout': Wout, 'bout': bout}
    _L0_attn_b_in = _L0_attn_b_setup()

    def _L0_ffn_setup():
        import jax, jax.numpy as jnp
        import numpy as np
        EPS = 1e-08

        def _ternary_linear(x, w):
            alpha = jnp.mean(jnp.abs(w))
            w_t = jnp.sign(w) * (jnp.abs(w) > 0.5 * alpha).astype(w.dtype)
            w_q = w + jax.lax.stop_gradient(w_t - w)
            d = x.shape[-1]
            rms = jnp.sqrt(jnp.sum(x * x, axis=-1, keepdims=True)) / jnp.sqrt(jnp.asarray(d, x.dtype))
            x_norm = x / (rms + EPS)
            return jnp.einsum('bsd,fd->bsf', x_norm, w_q)
        key = jax.random.key(seed)
        k1, k2, k3 = jax.random.split(key, 3)
        d_model, d_ff = (128, 512)
        B, S = (4, 512)
        x = jax.random.normal(k1, (B, S, d_model), dtype=jnp.float32)
        w_up = jax.random.normal(k2, (d_ff, d_model), dtype=jnp.float32) * 0.02
        w_down = jax.random.normal(k3, (d_model, d_ff), dtype=jnp.float32) * 0.02
        return {'x': x, 'w_up': w_up, 'w_down': w_down}
    _L0_ffn_in = _L0_ffn_setup()

    def _L1_attn_a_setup():
        import jax, jax.numpy as jnp
        import numpy as np
        import math
        D_MODEL = 128
        N_HEADS = 16
        HEAD_DIM = D_MODEL // N_HEADS
        FEAT = 16
        WINDOW = 64
        EPS_NORM = 1e-06
        EPS_LIN = 1e-06
        CHUNK = 128

        def rmsnorm(x, w):
            return x * jax.lax.rsqrt(jnp.mean(x * x, axis=-1, keepdims=True) + EPS_NORM) * w

        def taylor_feature_map(x):
            d = x.shape[-1]
            iu, ju = jnp.triu_indices(d)
            scale = jnp.where(iu == ju, 0.5, 1.0 / math.sqrt(2.0)).astype(x.dtype)
            quad = x[..., iu] * x[..., ju] * scale
            ones = jnp.ones(x.shape[:-1] + (1,), dtype=x.dtype)
            return jnp.concatenate([ones, x, quad], axis=-1)

        def linear_attention_causal(q_phi, k_phi, v):
            B, T, H, F = q_phi.shape
            D = v.shape[-1]
            Nc = T // CHUNK
            qc = q_phi.reshape(B, Nc, CHUNK, H, F).transpose(1, 0, 2, 3, 4)
            kc = k_phi.reshape(B, Nc, CHUNK, H, F).transpose(1, 0, 2, 3, 4)
            vc = v.reshape(B, Nc, CHUNK, H, D).transpose(1, 0, 2, 3, 4)
            causal = jnp.tril(jnp.ones((CHUNK, CHUNK), dtype=q_phi.dtype))

            def step(carry, inp):
                kv, ksum = carry
                qb, kb, vb = inp
                A = jnp.einsum('bchf,bshf->bhcs', qb, kb) * causal
                y = jnp.einsum('bhcs,bshd->bchd', A, vb) + jnp.einsum('bchf,bhfd->bchd', qb, kv)
                z = jnp.einsum('bhcs->bch', A) + jnp.einsum('bchf,bhf->bch', qb, ksum)
                kv = kv + jnp.einsum('bshf,bshd->bhfd', kb, vb)
                ksum = ksum + kb.sum(axis=1)
                return ((kv, ksum), y / (z[..., None] + EPS_LIN))
            kv0 = jnp.zeros((B, H, F, D), dtype=q_phi.dtype)
            ks0 = jnp.zeros((B, H, F), dtype=q_phi.dtype)
            _, ys = jax.lax.scan(step, (kv0, ks0), (qc, kc, vc))
            return ys.transpose(1, 0, 2, 3, 4).reshape(B, T, H, D)

        def sliding_window_attention(q, k, v):
            B, T, H, D = q.shape
            scale = 1.0 / math.sqrt(D)
            t = jnp.arange(T)
            allowed = (t[None, :] <= t[:, None]) & (t[None, :] >= t[:, None] - WINDOW)
            scores = jnp.einsum('bqhd,bkhd->bhqk', q, k) * scale
            scores = jnp.where(allowed[None, None], scores, -jnp.inf)
            attn = jax.nn.softmax(scores, axis=-1)
            out = jnp.einsum('bhqk,bkhd->bqhd', attn, v)
            return out.reshape(B, T, H * D)
        key = jax.random.key(seed)
        ks = jax.random.split(key, 7)
        B, T = (2, 256)
        s = 0.02
        return {'x': jax.random.normal(ks[0], (B, T, D_MODEL), jnp.float32), 'norm_w': jnp.ones((D_MODEL,), jnp.float32), 'Wq': jax.random.normal(ks[1], (D_MODEL, D_MODEL), jnp.float32) * s, 'Wk': jax.random.normal(ks[2], (D_MODEL, D_MODEL), jnp.float32) * s, 'Wv': jax.random.normal(ks[3], (D_MODEL, D_MODEL), jnp.float32) * s, 'Wqf': jax.random.normal(ks[4], (HEAD_DIM, FEAT), jnp.float32) * s, 'Wkf': jax.random.normal(ks[5], (HEAD_DIM, FEAT), jnp.float32) * s, 'Wout': jax.random.normal(ks[6], (2 * D_MODEL, D_MODEL), jnp.float32) * s}
    _L1_attn_a_in = _L1_attn_a_setup()

    def _L1_attn_b_setup():
        import jax, jax.numpy as jnp
        import numpy as np
        DIM = 128
        DEPTH = 6
        HEADS = 8
        FF_MULT = 4
        LN_EPS = 1e-05
        LEAKY_SLOPE = 0.01

        def _layernorm(x, w, b):
            m = jnp.mean(x, axis=-1, keepdims=True)
            v = jnp.mean(jnp.square(x - m), axis=-1, keepdims=True)
            return (x - m) * jax.lax.rsqrt(v + LN_EPS) * w + b

        def _linear_attn(q, k, v):
            q = jax.nn.softmax(q, axis=-1)
            k = jax.nn.softmax(k, axis=-2)
            context = jnp.einsum('bhnd,bhne->bhde', k, v)
            return jnp.einsum('bhnd,bhde->bhne', q, context)
        key = jax.random.key(seed)
        ks = jax.random.split(key, 12)
        b, t = (2, 512)
        s = 0.02
        return {'x': jax.random.normal(ks[0], (b, t, DIM), dtype=jnp.float32), 'ln1_w': jnp.ones((DEPTH, DIM), jnp.float32), 'ln1_b': jnp.zeros((DEPTH, DIM), jnp.float32), 'wq': jax.random.normal(ks[1], (DEPTH, DIM, DIM), jnp.float32) * s, 'wk': jax.random.normal(ks[2], (DEPTH, DIM, DIM), jnp.float32) * s, 'wv': jax.random.normal(ks[3], (DEPTH, DIM, DIM), jnp.float32) * s, 'wo': jax.random.normal(ks[4], (DEPTH, DIM, DIM), jnp.float32) * s, 'bo': jnp.zeros((DEPTH, DIM), jnp.float32), 'ln2_w': jnp.ones((DEPTH, DIM), jnp.float32), 'ln2_b': jnp.zeros((DEPTH, DIM), jnp.float32), 'w1': jax.random.normal(ks[5], (DEPTH, DIM, FF_MULT * DIM), jnp.float32) * s, 'w2': jax.random.normal(ks[6], (DEPTH, FF_MULT * DIM, DIM), jnp.float32) * s}
    _L1_attn_b_in = _L1_attn_b_setup()

    def _L1_ffn_setup():
        import jax, jax.numpy as jnp
        import numpy as np
        DIM = 128
        LATENT = 64
        INTER = 64
        SHARED = 512
        E = 8
        TOPK = 2
        NGROUP = 2
        TOPKG = 1
        NORM_TOPK = True
        SCALE = 1.0
        B, S = (2, 128)

        def relu2(x):
            r = jnp.maximum(x, 0.0)
            return r * r
        key = jax.random.key(seed)
        ks = jax.random.split(key, 8)

        def w(k, shape, std=0.02):
            return jax.random.normal(k, shape, dtype=jnp.float32) * std
        return {'x': jax.random.normal(ks[0], (B, S, DIM), dtype=jnp.float32), 'gate': w(ks[1], (E, DIM)), 'corr_bias': jnp.zeros((E,), jnp.float32), 'w1': w(ks[2], (E, INTER, LATENT)), 'w2': w(ks[3], (E, LATENT, INTER)), 'fc1_w': w(ks[4], (LATENT, DIM)), 'fc2_w': w(ks[5], (DIM, LATENT)), 'up_w': w(ks[6], (SHARED, DIM)), 'down_w': w(ks[7], (DIM, SHARED))}
    _L1_ffn_in = _L1_ffn_setup()
    _d = {'L0_attn_a_x': _L0_attn_a_in['x'], 'L0_attn_a_W_query': _L0_attn_a_in['W_query'], 'L0_attn_a_W_key': _L0_attn_a_in['W_key'], 'L0_attn_a_W_value': _L0_attn_a_in['W_value'], 'L0_attn_b_Wqkv': _L0_attn_b_in['Wqkv'], 'L0_attn_b_Wout': _L0_attn_b_in['Wout'], 'L0_attn_b_bout': _L0_attn_b_in['bout'], 'L0_ffn_w_up': _L0_ffn_in['w_up'], 'L0_ffn_w_down': _L0_ffn_in['w_down'], 'L1_attn_a_norm_w': _L1_attn_a_in['norm_w'], 'L1_attn_a_Wq': _L1_attn_a_in['Wq'], 'L1_attn_a_Wk': _L1_attn_a_in['Wk'], 'L1_attn_a_Wv': _L1_attn_a_in['Wv'], 'L1_attn_a_Wqf': _L1_attn_a_in['Wqf'], 'L1_attn_a_Wkf': _L1_attn_a_in['Wkf'], 'L1_attn_a_Wout': _L1_attn_a_in['Wout'], 'L1_attn_b_ln1_w': _L1_attn_b_in['ln1_w'], 'L1_attn_b_ln1_b': _L1_attn_b_in['ln1_b'], 'L1_attn_b_wq': _L1_attn_b_in['wq'], 'L1_attn_b_wk': _L1_attn_b_in['wk'], 'L1_attn_b_wv': _L1_attn_b_in['wv'], 'L1_attn_b_wo': _L1_attn_b_in['wo'], 'L1_attn_b_bo': _L1_attn_b_in['bo'], 'L1_attn_b_ln2_w': _L1_attn_b_in['ln2_w'], 'L1_attn_b_ln2_b': _L1_attn_b_in['ln2_b'], 'L1_attn_b_w1': _L1_attn_b_in['w1'], 'L1_attn_b_w2': _L1_attn_b_in['w2'], 'L1_ffn_gate': _L1_ffn_in['gate'], 'L1_ffn_corr_bias': _L1_ffn_in['corr_bias'], 'L1_ffn_w1': _L1_ffn_in['w1'], 'L1_ffn_w2': _L1_ffn_in['w2'], 'L1_ffn_fc1_w': _L1_ffn_in['fc1_w'], 'L1_ffn_fc2_w': _L1_ffn_in['fc2_w'], 'L1_ffn_up_w': _L1_ffn_in['up_w'], 'L1_ffn_down_w': _L1_ffn_in['down_w']}
    _x0 = _d['L0_attn_a_x']
    _d['L0_attn_a_x'] = jax.random.normal(jax.random.fold_in(jax.random.key(seed), 1), (8, 256, 128), dtype=_x0.dtype)
    del _x0
    return _d

def reference(L0_attn_a_x, L0_attn_a_W_query, L0_attn_a_W_key, L0_attn_a_W_value, L0_attn_b_Wqkv, L0_attn_b_Wout, L0_attn_b_bout, L0_ffn_w_up, L0_ffn_w_down, L1_attn_a_norm_w, L1_attn_a_Wq, L1_attn_a_Wk, L1_attn_a_Wv, L1_attn_a_Wqf, L1_attn_a_Wkf, L1_attn_a_Wout, L1_attn_b_ln1_w, L1_attn_b_ln1_b, L1_attn_b_wq, L1_attn_b_wk, L1_attn_b_wv, L1_attn_b_wo, L1_attn_b_bo, L1_attn_b_ln2_w, L1_attn_b_ln2_b, L1_attn_b_w1, L1_attn_b_w2, L1_ffn_gate, L1_ffn_corr_bias, L1_ffn_w1, L1_ffn_w2, L1_ffn_fc1_w, L1_ffn_fc2_w, L1_ffn_up_w, L1_ffn_down_w):

    def _L0_attn_a_ref(x, W_query, W_key, W_value):
        import jax, jax.numpy as jnp
        import numpy as np
        B, S, D_IN, D_OUT = (4, 512, 128, 128)
        q = jnp.einsum('bsd,od->bso', x, W_query)
        k = jnp.einsum('bsd,od->bso', x, W_key)
        v = jnp.einsum('bsd,od->bso', x, W_value)
        scores = jnp.einsum('bqo,bko->bqk', q, k)
        causal = jnp.tril(jnp.ones((x.shape[1], x.shape[1]), dtype=bool))
        scores = jnp.where(causal[None, :, :], scores, -jnp.inf)
        attn = jax.nn.softmax(scores / jnp.sqrt(jnp.float32(k.shape[-1])), axis=-1)
        return jnp.einsum('bqk,bko->bqo', attn, v)

    def _L0_attn_b_ref(x, Wqkv, Wout, bout):
        import jax, jax.numpy as jnp
        import numpy as np
        HEADS = 16
        DIM_HEAD = 64
        DIM = 128
        INNER = HEADS * DIM_HEAD
        SCALE = DIM_HEAD ** (-0.5)
        B, N, D = x.shape
        qkv = x @ Wqkv
        q, k, v = jnp.split(qkv, 3, axis=-1)

        def to_heads(t):
            return t.reshape(B, N, HEADS, DIM_HEAD).transpose(0, 2, 1, 3)
        q, k, v = (to_heads(q), to_heads(k), to_heads(v))
        q = jax.nn.softmax(q * SCALE, axis=-1)
        k = jax.nn.softmax(k, axis=-2)
        context = jnp.einsum('bhnd,bhne->bhde', q, k)
        out = jnp.einsum('bhde,bhnd->bhne', context, v)
        out = out.transpose(0, 2, 1, 3).reshape(B, N, INNER)
        return out @ Wout + bout

    def _L0_ffn_ref(x, w_up, w_down):
        import jax, jax.numpy as jnp
        import numpy as np
        EPS = 1e-08

        def _ternary_linear(x, w):
            alpha = jnp.mean(jnp.abs(w))
            w_t = jnp.sign(w) * (jnp.abs(w) > 0.5 * alpha).astype(w.dtype)
            w_q = w + jax.lax.stop_gradient(w_t - w)
            d = x.shape[-1]
            rms = jnp.sqrt(jnp.sum(x * x, axis=-1, keepdims=True)) / jnp.sqrt(jnp.asarray(d, x.dtype))
            x_norm = x / (rms + EPS)
            return jnp.einsum('bsd,fd->bsf', x_norm, w_q)
        h = jax.nn.gelu(_ternary_linear(x, w_up), approximate=False)
        return _ternary_linear(h, w_down)

    def _L1_attn_a_ref(x, norm_w, Wq, Wk, Wv, Wqf, Wkf, Wout):
        import jax, jax.numpy as jnp
        import numpy as np
        import math
        D_MODEL = 128
        N_HEADS = 16
        HEAD_DIM = D_MODEL // N_HEADS
        FEAT = 16
        WINDOW = 64
        EPS_NORM = 1e-06
        EPS_LIN = 1e-06
        CHUNK = 128

        def rmsnorm(x, w):
            return x * jax.lax.rsqrt(jnp.mean(x * x, axis=-1, keepdims=True) + EPS_NORM) * w

        def taylor_feature_map(x):
            d = x.shape[-1]
            iu, ju = jnp.triu_indices(d)
            scale = jnp.where(iu == ju, 0.5, 1.0 / math.sqrt(2.0)).astype(x.dtype)
            quad = x[..., iu] * x[..., ju] * scale
            ones = jnp.ones(x.shape[:-1] + (1,), dtype=x.dtype)
            return jnp.concatenate([ones, x, quad], axis=-1)

        def linear_attention_causal(q_phi, k_phi, v):
            B, T, H, F = q_phi.shape
            D = v.shape[-1]
            Nc = T // CHUNK
            qc = q_phi.reshape(B, Nc, CHUNK, H, F).transpose(1, 0, 2, 3, 4)
            kc = k_phi.reshape(B, Nc, CHUNK, H, F).transpose(1, 0, 2, 3, 4)
            vc = v.reshape(B, Nc, CHUNK, H, D).transpose(1, 0, 2, 3, 4)
            causal = jnp.tril(jnp.ones((CHUNK, CHUNK), dtype=q_phi.dtype))

            def step(carry, inp):
                kv, ksum = carry
                qb, kb, vb = inp
                A = jnp.einsum('bchf,bshf->bhcs', qb, kb) * causal
                y = jnp.einsum('bhcs,bshd->bchd', A, vb) + jnp.einsum('bchf,bhfd->bchd', qb, kv)
                z = jnp.einsum('bhcs->bch', A) + jnp.einsum('bchf,bhf->bch', qb, ksum)
                kv = kv + jnp.einsum('bshf,bshd->bhfd', kb, vb)
                ksum = ksum + kb.sum(axis=1)
                return ((kv, ksum), y / (z[..., None] + EPS_LIN))
            kv0 = jnp.zeros((B, H, F, D), dtype=q_phi.dtype)
            ks0 = jnp.zeros((B, H, F), dtype=q_phi.dtype)
            _, ys = jax.lax.scan(step, (kv0, ks0), (qc, kc, vc))
            return ys.transpose(1, 0, 2, 3, 4).reshape(B, T, H, D)

        def sliding_window_attention(q, k, v):
            B, T, H, D = q.shape
            scale = 1.0 / math.sqrt(D)
            t = jnp.arange(T)
            allowed = (t[None, :] <= t[:, None]) & (t[None, :] >= t[:, None] - WINDOW)
            scores = jnp.einsum('bqhd,bkhd->bhqk', q, k) * scale
            scores = jnp.where(allowed[None, None], scores, -jnp.inf)
            attn = jax.nn.softmax(scores, axis=-1)
            out = jnp.einsum('bhqk,bkhd->bqhd', attn, v)
            return out.reshape(B, T, H * D)
        B, T, _ = x.shape
        h = rmsnorm(x, norm_w)
        q = (h @ Wq).reshape(B, T, N_HEADS, HEAD_DIM)
        k = (h @ Wk).reshape(B, T, N_HEADS, HEAD_DIM)
        v = (h @ Wv).reshape(B, T, N_HEADS, HEAD_DIM)
        q_phi = taylor_feature_map(q @ Wqf)
        k_phi = taylor_feature_map(k @ Wkf)
        lin = linear_attention_causal(q_phi, k_phi, v).reshape(B, T, D_MODEL)
        win = sliding_window_attention(q, k, v)
        out = jnp.concatenate([lin, win], axis=-1) @ Wout
        return x + out

    def _L1_attn_b_ref(x, ln1_w, ln1_b, wq, wk, wv, wo, bo, ln2_w, ln2_b, w1, w2):
        import jax, jax.numpy as jnp
        import numpy as np
        DIM = 128
        DEPTH = 6
        HEADS = 8
        FF_MULT = 4
        LN_EPS = 1e-05
        LEAKY_SLOPE = 0.01

        def _layernorm(x, w, b):
            m = jnp.mean(x, axis=-1, keepdims=True)
            v = jnp.mean(jnp.square(x - m), axis=-1, keepdims=True)
            return (x - m) * jax.lax.rsqrt(v + LN_EPS) * w + b

        def _linear_attn(q, k, v):
            q = jax.nn.softmax(q, axis=-1)
            k = jax.nn.softmax(k, axis=-2)
            context = jnp.einsum('bhnd,bhne->bhde', k, v)
            return jnp.einsum('bhnd,bhde->bhne', q, context)
        b, t, e = x.shape
        h, dh = (HEADS, e // HEADS)
        for i in range(DEPTH):
            xn = _layernorm(x, ln1_w[i], ln1_b[i])
            q = (xn @ wq[i]).reshape(b, t, h, dh).transpose(0, 2, 1, 3)
            k = (xn @ wk[i]).reshape(b, t, h, dh).transpose(0, 2, 1, 3)
            v = (xn @ wv[i]).reshape(b, t, h, dh).transpose(0, 2, 1, 3)
            attn = _linear_attn(q, k, v)
            attn = attn.transpose(0, 2, 1, 3).reshape(b, t, e)
            x = attn @ wo[i] + bo[i] + x
            xn = _layernorm(x, ln2_w[i], ln2_b[i])
            hdn = xn @ w1[i]
            hdn = jnp.where(hdn >= 0, hdn, LEAKY_SLOPE * hdn)
            x = hdn @ w2[i] + x
        return x

    def _L1_ffn_ref(x, gate, corr_bias, w1, w2, fc1_w, fc2_w, up_w, down_w):
        import jax, jax.numpy as jnp
        import numpy as np
        DIM = 128
        LATENT = 64
        INTER = 64
        SHARED = 512
        E = 8
        TOPK = 2
        NGROUP = 2
        TOPKG = 1
        NORM_TOPK = True
        SCALE = 1.0
        B, S = (2, 128)

        def relu2(x):
            r = jnp.maximum(x, 0.0)
            return r * r
        Bv, Sv, D = x.shape
        xf = x.reshape(-1, D)
        N = xf.shape[0]
        scores = jax.nn.sigmoid(xf.astype(jnp.float32) @ gate.T)
        sfc = scores + corr_bias
        gs = E // NGROUP
        if NGROUP > 1:
            group_scores = jax.lax.top_k(sfc.reshape(N, NGROUP, gs), 2)[0].sum(-1)
            gidx = jax.lax.top_k(group_scores, TOPKG)[1]
            gmask = jnp.zeros((N, NGROUP), sfc.dtype).at[jnp.arange(N)[:, None], gidx].set(1.0)
            smask = jnp.repeat(gmask, gs, axis=1)
            sfc = jnp.where(smask > 0, sfc, 0.0)
        sel = jax.lax.top_k(sfc, TOPK)[1]
        top_scores = jnp.take_along_axis(scores, sel, axis=1)
        if NORM_TOPK:
            top_scores = top_scores / (top_scores.sum(-1, keepdims=True) + 1e-20)
        flat = sel.reshape(-1)
        perm = jnp.argsort(flat, stable=True)
        sorted_eid = flat[perm]
        scores_sorted = top_scores.reshape(-1)[perm]
        tok = perm // TOPK
        lat = xf @ fc1_w.T
        xs = lat[tok]
        out = jnp.zeros_like(xs)
        for e in range(E):
            he = relu2(xs @ w1[e].T) @ w2[e].T
            out = jnp.where((sorted_eid == e)[:, None], he, out)
        out = out * scores_sorted[:, None]
        comb = jnp.zeros((N, LATENT), out.dtype).at[tok].add(out)
        routed = comb @ fc2_w.T * SCALE
        shared = relu2(xf @ up_w.T) @ down_w.T
        return (routed + shared).reshape(Bv, Sv, D)
    x = L0_attn_a_x
    x = x + _L0_attn_a_ref(_layernorm(x, axis=-1), L0_attn_a_W_query, L0_attn_a_W_key, L0_attn_a_W_value)
    x = x + _L0_ffn_ref(_layernorm(x, axis=-1), L0_ffn_w_up, L0_ffn_w_down)
    x = x + _L0_attn_b_ref(_layernorm(x, axis=-1), L0_attn_b_Wqkv, L0_attn_b_Wout, L0_attn_b_bout)
    x = x + _L0_ffn_ref(_layernorm(x, axis=-1), L0_ffn_w_up, L0_ffn_w_down)
    x = x + _L1_attn_a_ref(_layernorm(x, axis=-1), L1_attn_a_norm_w, L1_attn_a_Wq, L1_attn_a_Wk, L1_attn_a_Wv, L1_attn_a_Wqf, L1_attn_a_Wkf, L1_attn_a_Wout)
    x = x + _L1_ffn_ref(_layernorm(x, axis=-1), L1_ffn_gate, L1_ffn_corr_bias, L1_ffn_w1, L1_ffn_w2, L1_ffn_fc1_w, L1_ffn_fc2_w, L1_ffn_up_w, L1_ffn_down_w)
    x = x + _L1_attn_b_ref(_layernorm(x, axis=-1), L1_attn_b_ln1_w, L1_attn_b_ln1_b, L1_attn_b_wq, L1_attn_b_wk, L1_attn_b_wv, L1_attn_b_wo, L1_attn_b_bo, L1_attn_b_ln2_w, L1_attn_b_ln2_b, L1_attn_b_w1, L1_attn_b_w2)
    x = x + _L1_ffn_ref(_layernorm(x, axis=-1), L1_ffn_gate, L1_ffn_corr_bias, L1_ffn_w1, L1_ffn_w2, L1_ffn_fc1_w, L1_ffn_fc2_w, L1_ffn_up_w, L1_ffn_down_w)
    return x

_drawn_inputs = setup_inputs


def setup_inputs(seed=0):
    import zlib

    import numpy as np

    out = dict(_drawn_inputs(seed))
    spreads = {'L0_attn_b_bout': (0.0, 0.8),
     'L1_attn_a_norm_w': (1.0, 0.6),
     'L1_attn_b_ln1_w': (1.0, 0.6),
     'L1_attn_b_ln1_b': (0.0, 0.8),
     'L1_attn_b_bo': (0.0, 0.8),
     'L1_attn_b_ln2_w': (1.0, 0.6),
     'L1_attn_b_ln2_b': (0.0, 0.8),
     'L1_ffn_corr_bias': (0.0, 0.8)}
    factors = {'L0_attn_b_Wqkv': 8.0,
     'L0_attn_b_Wout': 8.0,
     'L1_attn_a_Wq': 8.0,
     'L1_attn_a_Wk': 8.0,
     'L1_attn_a_Wv': 8.0,
     'L1_attn_a_Wqf': 8.0,
     'L1_attn_a_Wkf': 8.0,
     'L1_attn_a_Wout': 8.0,
     'L1_attn_b_wq': 8.0,
     'L1_attn_b_wk': 8.0,
     'L1_attn_b_wv': 8.0,
     'L1_attn_b_wo': 8.0,
     'L1_attn_b_w1': 8.0,
     'L1_attn_b_w2': 8.0,
     'L1_ffn_gate': 8.0,
     'L1_ffn_w1': 8.0,
     'L1_ffn_w2': 8.0,
     'L1_ffn_fc1_w': 8.0,
     'L1_ffn_fc2_w': 8.0,
     'L1_ffn_up_w': 8.0,
     'L1_ffn_down_w': 8.0}
    for name, (base, spread) in spreads.items():
        noise = np.random.default_rng([zlib.crc32(name.encode()), seed]).standard_normal(out[name].shape)
        drawn = base * np.exp(spread * noise) if base else spread * noise
        out[name] = jnp.asarray(drawn.astype(out[name].dtype))
    for name, factor in factors.items():
        out[name] = (out[name] * factor).astype(out[name].dtype)
    return out
```

```python
from contextlib import ExitStack

import concourse.bass as bass
from concourse import mybir

F32 = mybir.dt.float32
BF16 = mybir.dt.bfloat16
ALU = mybir.AluOpType
ACT = mybir.ActivationFunctionType
X = mybir.AxisListType.X

P = 128
SEQ = 256
NEG = -1.0e30


def skew(stages, n):
    for t in range(n + len(stages) - 1):
        for d, stage in enumerate(stages):
            if stage is not None and 0 <= t - d < n:
                stage(t - d)


def hybrid_program(nc, w, out):
    x_dram = w["L0_attn_a_x"].rearrange("b (t p) d -> p (b t) d", p=P)
    out_dram = out.rearrange("b (t p) d -> p (b t) d", p=P)
    NT = x_dram.shape[1]
    TG = 4
    G = NT // TG
    TOK = TG * P
    NB = TG * P // SEQ
    DEPTH = w["L1_attn_b_wq"].shape[0]
    QH, QD = 16, 64
    INNER = QH * QD
    NC_ = INNER // P
    HC, DC = 16, 8
    HE, DE = 8, 16
    NE = w["L1_ffn_gate"].shape[0]
    FF = 512
    NF = FF // P
    VA = P + HC

    with ExitStack() as ctx:
        def sb(name, shape, dt=F32):
            return ctx.enter_context(nc.sbuf_tensor(name, shape, dt))

        x = sb("x", [P, NT, P])
        z = sb("z", [P, NT, P])
        xn = sb("xn", [P, NT, P])
        xnT = sb("xnT", [P, G, TOK])
        st = sb("st", [P, NT, 6])
        mv = sb("mv", [P, NT, 2])
        var_eps = sb("var_eps", [P, NT])
        rstd = sb("rstd", [P, NT])
        second = sb("second", [P, 3, NT])
        neg_half = sb("neg_half", [P, TG])
        pos_half = sb("pos_half", [P, TG])

        ident = sb("ident", [P, P])
        ident_bf = sb("ident_bf", [P, P], BF16)
        ones = sb("ones", [P, P])
        window_bf = sb("window_bf", [P, P + 192], BF16)
        head8 = sb("head8", [P, HC])
        head16 = sb("head16", [P, HE])
        bd16 = sb("bd16", [P, HE, DE])
        lower = sb("lower", [P, NE, NE])
        a_w = sb("a_w", [P, 2 * P])
        wupT = sb("wupT", [P, FF])
        wdnT = sb("wdnT", [P, NF, P])
        wqkv = sb("wqkv", [P, 3 * INNER])
        wvT = sb("wvT", [P, NC_, P])
        wout_b = sb("wout_b", [P, NC_, P])
        bout_bc = sb("bout_bc", [P, P])
        c_w = sb("c_w", [P, 4, P])
        wout_c = sb("wout_c", [P, 2, P])
        cols = sb("cols", [P, 25])
        gateT = sb("gateT", [P, NE])
        bias_bc = sb("bias_bc", [P, NE])
        gate_sel = sb("gate_sel", [P, NF, P], BF16)
        moe_up = sb("moe_up", [P, 2 * FF])
        moe_dn = sb("moe_dn", [P, 2 * NF, P])
        e_w4 = [sb(f"e_w4_{i}", [P, 4, P]) for i in range(2)]
        e_w1 = [sb(f"e_w1_{i}", [P, FF]) for i in range(2)]
        e_w2 = [sb(f"e_w2_{i}", [P, NF, P]) for i in range(2)]
        bo_bc = sb("bo_bc", [P, DEPTH, P])

        ARENA = 30436
        arena = sb("arena", [P, ARENA])

        def carve():
            used = [0]

            def take(*dims):
                n = 1
                for d in dims:
                    n *= d
                a = arena[:, used[0]:used[0] + n]
                used[0] += n
                assert used[0] <= ARENA, used
                if len(dims) == 1:
                    return a
                names = "abcd"[:len(dims)]
                return a.rearrange(f"p ({' '.join(names)}) -> p {' '.join(names)}",
                                   **{c: d for c, d in zip(names[1:], dims[1:])})
            return take

        ps = ctx.enter_context(nc.psum_tensor("ps", [P, 8, 512], F32))
        sems = {}

        def S(name):
            if name not in sems:
                sems[name] = ctx.enter_context(nc.semaphore(name))
            return sems[name]

        ring = {"next": 0, "banks": list(range(8))}
        freed_by = {}
        where = {}

        def claim(pe, name, idx, sem, value):
            b = ring["banks"][ring["next"] % len(ring["banks"])]
            ring["next"] += 1
            if b in freed_by:
                pe.wait_ge(*freed_by[b])
            freed_by[b] = (S(sem), value)
            where[(name, idx)] = b
            return ps[:, b, :]

        def bank(name, idx):
            return ps[:, where[(name, idx)], :]

        def tiles(g):
            return range(TG * g, TG * g + TG)

        block = ctx.enter_context(nc.Block())

        take = carve()
        bd8 = take(HC, DC)
        s_aw = take(3, P)
        s_up0 = take(NF, P)
        s_dn0 = take(FF)
        s_gate = take(P)
        s_w1 = take(4, 64)
        s_w2 = take(8, 64)
        s_fc1 = take(P)
        s_fc2 = take(64)
        s_upw = take(NF, P)
        s_dnw = take(FF)
        s_cf = take(2, 16)
        s_rows = take(P)
        s_absum = take(2)
        s_thr = take(4)
        s_tern = take(2, FF)
        s_wt = take(2, FF)
        s_cfT = take(2, P)
        s_bd = take(P)
        s_wqT = take(P)
        s_w1T = take(FF)
        s_fc2T = take(P)

        causal_bf = arena[:, ARENA - 192:ARENA].bitcast(BF16)

        take = carve()
        a_uT = take(2, TOK)
        a_v = take(4, TG, P)
        a_p = take(2, NB, 384)
        a_pT = take(2, NB, 384)
        a_nmax = take(2, NT)
        a_sum = take(2, NT)

        take = carve()
        f_hT = take(3, NF * TOK)
        f_sq = take(2, NF * TOK)
        f_ssq = take(2, TOK)
        f_r = take(3, NT)

        take = carve()
        b_q = take(2, TG, INNER)
        b_k = take(2, TG, INNER)
        b_kTe = take(4, TOK)
        b_ctx = take(4, NC_, P)
        b_m = take(2, NC_, P)
        b_g = take(4, P)
        b_qmax = take(4, QH)
        b_qsum = take(4, QH)
        b_qrec = take(4, QH)
        b_kmax = take(NC_ * 4, NB)
        b_ksum = take(2, NB, NC_)
        b_krec = take(2, NB, NC_)

        take = carve()
        c_km = take(2, HC, SEQ)
        c_kT = take(2, SEQ)
        c_qT = take(2, 2, SEQ)
        c_vm = take(4, HC * (VA + DC + 1))
        c_p0 = take(2, 4, P)
        c_p1 = take(2, 4, SEQ)
        c_pT = take(2, 3, 512)
        c_a0 = take(2, 4, SEQ)
        c_a1 = take(2, 4, P)
        c_max = take(4, 8)
        c_rec = take(4, 2, HC)
        c_cat = take(2, 2, SEQ)
        c_catT = take(2, SEQ)

        take = carve()
        d_r2 = take(3, 2 * NF, TOK)
        d_r = take(4, TOK)
        d_sc = take(G, 2, TG * NE)
        d_e = take(G, TG * NE)
        d_sfc = take(G, TG * NE)
        d_top = take(G, 8, TG * 2)
        d_cmp = take(2, 2, TG * NE * NE)
        d_rank = take(G, TG * NE)
        d_w = take(G, TG * NE)
        d_den = take(G, 2, TG)
        d_gate = take(G, TG * NE)
        d_rest = take(2, 2, TG * NE)
        d_parts = take(2, TG * 96 // 2).bitcast(BF16).rearrange("p r (t k) -> p r t k", k=96)
        d_partsT = take(2, TOK // 2).bitcast(BF16)

        take = carve()
        e_qe = take(2, TOK)
        e_qm = take(G, 3, TG * HE)
        e_qT = take(4, TOK)
        e_kTe = take(2, TOK)
        e_km = take(G, NB)
        e_ks = take(G, NB)
        e_kr = take(G, NB)
        e_k = take(2, TOK)
        e_v = take(3, TOK)
        e_ctx = take(2, NB, P)
        e_m = take(2, NB, P)
        e_h = take(3, NF * TOK)

        def value_blocks(i):
            return c_vm[:, i, 0:HC * VA].rearrange("p (h v) -> p h v", v=VA)

        def own_columns(i):
            return c_vm[:, i, 0:HC * (VA + DC)].rearrange("p (h v) -> p h v", v=VA + DC)[:, :, 0:DC]

        def own_sums(i):
            return c_vm[:, i, P:P + HC * (VA + 1)].rearrange("p (h v) -> p h v", v=VA + 1)[:, :, 0:1]

        WQP, WQ, WK, WV = range(4)

        def col(kind, l):
            c = kind * DEPTH + l
            return cols[:, c:c + 1]

        A_IN, F_IN, B_IN, C_IN, D_IN, E_IN = 3 * 16, 2 * 16, 3 * 16, (4 + 2 * HC + 5) * 16, 8 * 16, 6 * 16
        LN_A, LN_F0, LN_B, LN_F1, LN_C, LN_D0, LN_Z, LN_E = 0, 1, 2, 3, 4, 5, 6, 7
        LN_D1 = LN_E + 2 * DEPTH

        def turned(u):
            return u if u < LN_Z else u - 1

        PH = PHASES
        LAST = len(PH) - 1

        @block.sync
        def _(sp):
            def load(dst, src, name):
                sp.dma_start(dst, src).then_inc(S(name), 16)

            for g in range(G):
                load(x[:, TG * g:TG * g + TG, :], x_dram[:, TG * g:TG * g + TG, :], f"x_in{g}")
            for i, n in enumerate(("W_query", "W_key", "W_value")):
                load(s_aw[:, i, :], w[f"L0_attn_a_{n}"], "a_in")
            load(s_up0, w["L0_ffn_w_up"].rearrange("(c p) d -> p c d", p=P), "f_in")
            load(s_dn0, w["L0_ffn_w_down"], "f_in")
            load(wqkv[:, :], w["L0_attn_b_Wqkv"], "b_in")
            load(wout_b[:, :, :], w["L0_attn_b_Wout"].rearrange("(c p) f -> p c f", p=P), "b_in")
            load(bout_bc[:, :], w["L0_attn_b_bout"].rearrange("(a d) -> a d", a=1).broadcast_to([P, P]), "b_in")
            load(c_w[:, WQ, :], w["L1_attn_a_Wq"], "c_in")
            load(c_w[:, WK, :], w["L1_attn_a_Wk"], "c_in")
            load(c_w[:, WV, :], w["L1_attn_a_Wv"], "c_in")
            load(wout_c[:, :, :], w["L1_attn_a_Wout"].rearrange("(c p) f -> p c f", p=P), "c_in")
            for i, n in enumerate(("Wqf", "Wkf")):
                for h in range(HC):
                    load(s_cf[h * DC:(h + 1) * DC, i, :], w[f"L1_attn_a_{n}"], "c_in")
            for i, n in enumerate(("ln1_w", "ln1_b", "ln2_w", "ln2_b")):
                load(s_rows[i * DEPTH:(i + 1) * DEPTH, :], w[f"L1_attn_b_{n}"], "c_in")
            load(s_rows[4 * DEPTH:4 * DEPTH + 1, :], w["L1_attn_a_norm_w"].rearrange("(a d) -> a d", a=1), "c_in")
            load(s_gate[0:NE, :], w["L1_ffn_gate"], "d_in")
            load(s_w1, w["L1_ffn_w1"].rearrange("e i l -> (e i) l").rearrange("(c p) l -> p c l", p=P), "d_in")
            load(s_w2[0:64, :, :], w["L1_ffn_w2"].rearrange("e l i -> l e i"), "d_in")
            load(s_fc1[0:64, :], w["L1_ffn_fc1_w"], "d_in")
            load(s_fc2, w["L1_ffn_fc2_w"], "d_in")
            load(s_upw, w["L1_ffn_up_w"].rearrange("(c p) d -> p c d", p=P), "d_in")
            load(s_dnw, w["L1_ffn_down_w"], "d_in")
            load(bias_bc[:, :], w["L1_ffn_corr_bias"].rearrange("(a d) -> a d", a=1).broadcast_to([P, NE]), "d_in")
            load(bo_bc[:, :, :], w["L1_attn_b_bo"].rearrange("(a l) d -> a l d", a=1).broadcast_to([P, DEPTH, P]), "e_bo_in")
            for l in range(DEPTH if "E" in PH else 0):
                if l >= 2:
                    sp.wait_ge(S("e_z2"), (l - 1) * G)
                for i, n in enumerate(("wq", "wk", "wv", "wo")):
                    load(e_w4[l % 2][:, i, :], w[f"L1_attn_b_{n}"][l], f"e_in{l % 2}")
                load(e_w1[l % 2][:, :], w["L1_attn_b_w1"][l], f"e_in{l % 2}")
                load(e_w2[l % 2][:, :, :], w["L1_attn_b_w2"][l].rearrange("(c p) f -> p c f", p=P), f"e_in{l % 2}")
            for g in range(G):
                sp.wait_ge(S("x_sum"), LAST * G + g + 1)
                sp.dma_start(out_dram[:, TG * g:TG * g + TG, :], x[:, TG * g:TG * g + TG, :]).then_inc(S("stored"), 16)
            sp.wait_ge(S("stored"), 16 * G)

        @block.tensor
        def _(pe):
            def mm(o, lhsT, rhs, start=True, stop=True):
                return pe.matmul(o, lhsT, rhs, start=start, stop=stop, skip_group_check=True)

            pe.wait_ge(S("masks"), 1)
            prep = [0]

            def prep_bank():
                prep[0] += 1
                return claim(pe, "prep", prep[0] - 1, "prep_out", PREP_OUT[prep[0] - 1])

            pe.wait_ge(S("a_in"), A_IN)
            o = prep_bank()
            mm(o[:, 0:P], s_aw[:, 0, :], s_aw[:, 1, :])
            pe.transpose(o[:, P:2 * P], s_aw[:, 2, :], ident[:, :]).then_inc(S("prep_mm"), 1)
            o = prep_bank()
            pe.wait_ge(S("f_abs"), 2)
            mm(o[:, 0:2], ones[:, :], s_absum).then_inc(S("prep_mm"), 1)
            pe.wait_ge(S("f_tern"), 2)
            for i in range(2):
                o = prep_bank()
                for c in range(NF):
                    last = pe.transpose(o[:, c * P:(c + 1) * P], s_wt[:, i, c * P:(c + 1) * P], ident[:, :])
                last.then_inc(S("prep_mm"), 1)
            pe.wait_ge(S("b_in"), B_IN)
            for i in range(2):
                o = prep_bank()
                for c in range(4):
                    v0 = 2 * INNER + (4 * i + c) * P
                    last = pe.transpose(o[:, c * P:(c + 1) * P], wqkv[:, v0:v0 + P], ident[:, :])
                last.then_inc(S("prep_mm"), 1)
            pe.wait_ge(S("c_in"), C_IN)
            o = prep_bank()
            pe.transpose(o[0:16, 0:P], s_cf[:, 0, :], ident[:, :])
            pe.transpose(o[0:16, P:2 * P], s_cf[:, 1, :], ident[:, :])
            pe.transpose(o[:, 2 * P:2 * P + 25], s_rows[0:25, :], ident[0:25, 0:25]).then_inc(S("prep_mm"), 1)
            o = prep_bank()
            pe.wait_ge(S("prep_out"), PREP_OUT[6])
            mm(o[:, 0:P], s_cfT[0:16, 0, :], s_cfT[0:16, 1, :]).then_inc(S("prep_mm"), 1)
            o = prep_bank()
            pe.wait_ge(S("c_scaled"), 3)
            pe.transpose(o[:, 0:P], c_w[:, WQ, :], ident[:, :]).then_inc(S("prep_mm"), 1)
            o = prep_bank()
            pe.wait_ge(S("prep_out"), PREP_OUT[8])
            mm(o[:, 0:P], s_wqT, s_bd).then_inc(S("prep_mm"), 1)
            pe.wait_ge(S("d_in"), D_IN)
            o = prep_bank()
            for c in range(4):
                last = pe.transpose(o[0:64, c * P:(c + 1) * P], s_w1[:, c, :], ident[:, :])
            last.then_inc(S("prep_mm"), 1)
            o = prep_bank()
            pe.transpose(o[0:64, 0:P], s_fc2, ident[:, :])
            pe.transpose(o[:, P:P + NE], s_gate[0:NE, :], ident[0:NE, 0:NE]).then_inc(S("prep_mm"), 1)
            o = prep_bank()
            pe.wait_ge(S("prep_out"), PREP_OUT[11])
            mm(o, s_fc1[0:64, :], s_w1T[0:64, :]).then_inc(S("prep_mm"), 1)
            o = prep_bank()
            for c in range(NF):
                last = pe.transpose(o[:, c * P:(c + 1) * P], s_upw[:, c, :], ident[:, :])
            last.then_inc(S("prep_mm"), 1)
            o = prep_bank()
            w2f = s_w2.rearrange("p e i -> p (e i)")
            for c in range(NF):
                last = mm(o[:, c * P:(c + 1) * P], w2f[0:64, c * P:(c + 1) * P], s_fc2T[0:64, :])
            last.then_inc(S("prep_mm"), 1)
            o = prep_bank()
            for c in range(NF):
                last = pe.transpose(o[:, c * P:(c + 1) * P], s_dnw[:, c * P:(c + 1) * P], ident[:, :])
            last.then_inc(S("prep_mm"), 1)

            def ln_transpose(u):
                def stage(g):
                    o = claim(pe, f"ln{u}", g, "ln_xT", turned(u) * G + g + 1)
                    pe.wait_ge(S("ln_xn"), turned(u) * G + g + 1)
                    for j, t in enumerate(tiles(g)):
                        last = pe.transpose(o[:, j * P:(j + 1) * P], xn[:, t, :], ident[:, :])
                    last.then_inc(S("ln_T"), 1)
                return stage

            def a_proj(g):
                o = claim(pe, "a_u", g, "a_uT", g + 1)
                pe.wait_ge(S("ln_xT"), LN_A * G + g + 1)
                if g == 0:
                    pe.wait_ge(S("prep_out"), PREP_OUT[-1])
                mm(o, a_w[:, 0:P], xnT[:, g, :]).then_inc(S("a_u_mm"), 1)
                o = claim(pe, "a_v", g, "a_v", g + 1)
                for j in range(TG):
                    last = mm(o[:, j * P:(j + 1) * P], xnT[:, g, j * P:(j + 1) * P], a_w[:, P:2 * P])
                last.then_inc(S("a_v_mm"), 1)

            def a_scores(g):
                for b in range(NB):
                    o = claim(pe, "a_s", NB * g + b, "a_exp", TG * g + 2 * b + 2)
                    mm(o[:, 0:384], ident_bf[:, :], causal_bf, True, False)
                    if b == 0:
                        pe.wait_ge(S("a_uT"), g + 1)
                    q0 = b * SEQ
                    mm(o[:, 0:P], a_uT[:, g % 2, q0:q0 + P], xnT[:, g, q0:q0 + P], False, False)
                    mm(o[:, P:384], a_uT[:, g % 2, q0 + P:q0 + SEQ], xnT[:, g, q0:q0 + SEQ],
                       False, True).then_inc(S("a_s_mm"), 1)

            def a_ptrans(g):
                for b in range(NB):
                    o = claim(pe, "a_pT", NB * g + b, f"a_pT{b}", g + 1)
                    pe.wait_ge(S("a_exp"), TG * g + 2 * b + 2)
                    for c in range(3):
                        last = pe.transpose(o[:, c * P:(c + 1) * P], a_p[:, g % 2, b, c * P:(c + 1) * P], ident[:, :])
                    last.then_inc(S("a_pT_mm"), 1)

            def a_out(g):
                o = claim(pe, "a_o", g, "x_sum", G * PH.index("A") + g + 1)
                pe.wait_ge(S("a_v"), g + 1)
                for b in range(NB):
                    pe.wait_ge(S(f"a_pT{b}"), g + 1)
                    v0, v1 = a_v[:, g, 2 * b, :], a_v[:, g, 2 * b + 1, :]
                    pT = a_pT[:, g % 2, b, :]
                    mm(o[:, 2 * b * P:(2 * b + 1) * P], pT[:, 0:P], v0)
                    mm(o[:, (2 * b + 1) * P:(2 * b + 2) * P], pT[:, P:2 * P], v0, True, False)
                    last = mm(o[:, (2 * b + 1) * P:(2 * b + 2) * P], pT[:, 2 * P:3 * P], v1, False, True)
                last.then_inc(S("a_o_mm"), 1)

            if "A" in PH:
                skew([None, ln_transpose(LN_A), a_proj, a_scores, a_ptrans, a_out], G)

            def ffn(n, u, key):
                def up(g):
                    for c in range(NF):
                        o = claim(pe, f"f_h{n}", NF * g + c, "f_gelu", n * NF * G + NF * g + c + 1)
                        if c == 0:
                            pe.wait_ge(S("ln_xT"), turned(u) * G + g + 1)
                        mm(o, wupT[:, c * P:(c + 1) * P], xnT[:, g, :]).then_inc(S("f_h_mm"), 1)

                def down(g):
                    o = claim(pe, f"f_ss{n}", g, "f_ms", n * G + g + 1)
                    pe.wait_ge(S("f_ssq"), n * G + g + 1)
                    for j in range(TG):
                        last = mm(o[:, j:j + 1], f_ssq[:, g % 2, j * P:(j + 1) * P], ones[:, 0:1])
                    last.then_inc(S("f_ss_mm"), 1)
                    o = claim(pe, f"f_y{n}", g, "x_sum", G * PH.index(key) + g + 1)
                    for j in range(TG):
                        for c in range(NF):
                            h0 = c * TOK + j * P
                            last = mm(o[:, j * P:(j + 1) * P], f_hT[:, g % 3, h0:h0 + P], wdnT[:, c, :],
                                      c == 0, c == NF - 1)
                    last.then_inc(S("f_y_mm"), 1)
                skew([None, None, ln_transpose(u), up, None, down, None], G)

            if "F" in PH:
                ffn(0, LN_F0, "F")

            def b_qk(g):
                pe.wait_ge(S("ln_xT"), LN_B * G + g + 1)

                def q_tile(j):
                    for half in range(2):
                        o = claim(pe, "b_q", (TG * g + j) * 2 + half, "b_qsub", (TG * g + j) * 2 + half + 1)
                        mm(o, xnT[:, g, j * P:(j + 1) * P], wqkv[:, half * 512:half * 512 + 512]).then_inc(S("b_q_mm"), 1)

                def k_chunk(c):
                    n = NC_ * g + c
                    o = claim(pe, "b_k", n, "b_kexp", NB * (n + 1))
                    mm(o, wqkv[:, INNER + c * P:INNER + (c + 1) * P], xnT[:, g, :]).then_inc(S("b_k_mm"), 1)

                def k_turn(c):
                    n = NC_ * g + c
                    o = claim(pe, "b_kT", n, "b_k", n + 1)
                    pe.wait_ge(S("b_kexp"), NB * (n + 1))
                    for j in range(TG):
                        last = pe.transpose(o[:, j * P:(j + 1) * P], b_kTe[:, n % 4, j * P:(j + 1) * P], ident[:, :])
                    last.then_inc(S("b_kT_mm"), 1)

                for c in range(NC_ + 2):
                    if c < NC_:
                        k_chunk(c)
                        if c % 2 == 0:
                            q_tile(c // 2)
                    if c >= 2:
                        k_turn(c - 2)

            def b_context(g):
                for b in range(NB):
                    for half in range(2):
                        o = claim(pe, "b_c", (NB * g + b) * 2 + half, "b_ctx", (NB * g + b) * 4 + 2 * half + 2)
                        if b == 0 and half == 0:
                            pe.wait_ge(S("b_k"), NC_ * (g + 1))
                            pe.wait_ge(S("b_qn"), TG * (g + 1))
                        for c in range(4):
                            cc = (4 * half + c) * P
                            for s in range(2):
                                j = 2 * b + s
                                last = mm(o[:, c * P:(c + 1) * P], b_k[:, g % 2, j, cc:cc + P],
                                          b_q[:, g % 2, j, cc:cc + P], s == 0, s == 1)
                        last.then_inc(S("b_c_mm"), 1)

            def b_fold(g):
                for b in range(NB):
                    n = NB * g + b
                    for half in range(2):
                        o = claim(pe, "b_m", 2 * n + half, "b_m", 2 * n + half + 1)
                        pe.wait_ge(S("b_ctx"), 4 * n + 2 * half + 2)
                        for c in range(4):
                            cc = 4 * half + c
                            last = mm(o[:, c * P:(c + 1) * P], b_ctx[:, n % 4, cc, :], wout_b[:, cc, :])
                        last.then_inc(S("b_m_mm"), 1)
                for b in range(NB):
                    n = NB * g + b
                    o = claim(pe, "b_g", n, "b_g", n + 1)
                    pe.wait_ge(S("b_m"), 2 * n + 2)
                    for c in range(NC_):
                        last = mm(o[:, 0:P], wvT[:, c, :], b_m[:, n % 2, c, :], c == 0, c == NC_ - 1)
                    last.then_inc(S("b_g_mm"), 1)

            def b_out(g):
                o = claim(pe, "b_y", g, "x_sum", G * PH.index("B") + g + 1)
                pe.wait_ge(S("b_g"), NB * (g + 1))
                for j in range(TG):
                    last = mm(o[:, j * P:(j + 1) * P], xnT[:, g, j * P:(j + 1) * P], b_g[:, (NB * g + j // 2) % 4, :])
                last.then_inc(S("b_y_mm"), 1)

            if "B" in PH:
                skew([None, ln_transpose(LN_B), b_qk, b_context, b_fold, b_out], G)
            if "f" in PH:
                ffn(1, LN_F1, "f")

            def c_turn(g):
                ln_transpose(LN_C)(g)

            def c_proj(n):
                g, s0 = n // NB, (n % NB) * SEQ
                o = claim(pe, "c_q", n, "c_qT", n + 1)
                pe.wait_ge(S("ln_xT"), LN_C * G + g + 1)
                mm(o[:, 0:SEQ], c_w[:, WQP, :], xnT[:, g, s0:s0 + SEQ])
                mm(o[:, SEQ:2 * SEQ], c_w[:, WQ, :], xnT[:, g, s0:s0 + SEQ]).then_inc(S("c_q_mm"), 1)
                o = claim(pe, "c_k", n, "c_kT", n + 1)
                mm(o[:, 0:SEQ], c_w[:, WK, :], xnT[:, g, s0:s0 + SEQ]).then_inc(S("c_k_mm"), 1)
                o = claim(pe, "c_v", n, "c_vm", n + 1)
                for s in range(2):
                    last = mm(o[:, s * P:(s + 1) * P], xnT[:, g, s0 + s * P:s0 + (s + 1) * P], c_w[:, WV, :])
                last.then_inc(S("c_v_mm"), 1)

            def c_heads(n):
                km, qp, q = c_km[:, n % 2], c_qT[:, n % 2, 0, :], c_qT[:, n % 2, 1, :]

                def scores(i):
                    m = 4 * n + i
                    h0 = 4 * i
                    if i == 0:
                        pe.wait_ge(S("c_km"), n + 1)
                        pe.wait_ge(S("c_qT"), n + 1)
                    o = claim(pe, "c_s0", m, "c_sub", 3 * m + 1)
                    mm(o, ident_bf[:, :], window_bf[:, 0:P].unsqueeze(1).to_broadcast([P, 4, P]), True, False)
                    mm(o, q[:, 0:P], km[:, h0:h0 + 4, 0:P], False, True).then_inc(S("c_s_mm"), 1)
                    for r in range(2):
                        o = claim(pe, "c_s1", 2 * m + r, "c_sub", 3 * m + 2 + r)
                        mm(o[:, 0:384], ident_bf[:, :], window_bf[:, P:320].unsqueeze(1).to_broadcast([P, 2, 192]), True, False)
                        mm(o[:, 0:384], q[:, P:SEQ], km[:, h0 + 2 * r:h0 + 2 * r + 2, 64:SEQ], False, True)\
                            .then_inc(S("c_s_mm"), 1)
                    for r in range(2):
                        o = claim(pe, "c_l0", 2 * m + r, "c_sqr", 3 * m + 1 + r)
                        for k in range(2):
                            last = mm(o[:, k * SEQ:(k + 1) * SEQ], km[:, h0 + 2 * r + k, 0:P], qp)
                        last.then_inc(S("c_l_mm"), 1)
                    o = claim(pe, "c_l1", m, "c_sqr", 3 * m + 3)
                    for k in range(4):
                        last = mm(o[:, k * P:(k + 1) * P], km[:, h0 + k, P:SEQ], qp[:, P:SEQ])
                    last.then_inc(S("c_l_mm"), 1)

                def turn(i):
                    m = 4 * n + i
                    o = claim(pe, "c_t0", 3 * m, "c_pT_dve", m + 1)
                    pe.wait_ge(S("c_exp"), 2 * m + 2)
                    for k in range(4):
                        last = pe.transpose(o[:, k * P:(k + 1) * P], c_p0[:, m % 2, k, :], ident[:, :])
                    last.then_inc(S("c_t_mm"), 1)
                    for r in range(2):
                        o = claim(pe, "c_t0", 3 * m + 1 + r, "c_pT_act", 2 * m + r + 1)
                        for k in range(2):
                            for s in range(2):
                                last = pe.transpose(o[:, (2 * k + s) * P:(2 * k + s + 1) * P],
                                                    c_p1[:, m % 2, 2 * r + k, s * P:(s + 1) * P], ident[:, :])
                        last.then_inc(S("c_t_mm"), 1)

                lin, win = ps[:, 6, :], ps[:, 7, :]

                def values(i):
                    m = 4 * n + i
                    if i == 0 and n > 0:
                        pe.wait_ge(S("c_cat"), 2 * n)
                    v = [value_blocks((2 * n + s) % 4) for s in range(2)]
                    pe.wait_ge(S("c_mask"), 2 * m + 2)
                    pe.wait_ge(S("c_sqr"), 3 * m + 3)
                    for k in range(4):
                        h = 4 * i + k
                        first, end = h == 0, h == HC - 1
                        mm(lin[:, 0:VA], c_a0[:, m % 2, k, 0:P], v[0][:, h, :], first, end)
                        mm(lin[:, VA:2 * VA], c_a0[:, m % 2, k, P:SEQ], v[0][:, h, :], False, False)
                        last = mm(lin[:, VA:2 * VA], c_a1[:, m % 2, k, :], v[1][:, h, :], False, end)
                    last.then_inc(S("c_lin_mm"), 1)
                    pe.wait_ge(S("c_pT_dve"), m + 1)
                    pe.wait_ge(S("c_pT_act"), 2 * m + 2)
                    for k in range(4):
                        h = 4 * i + k
                        first, end = h == 0, h == HC - 1
                        pT = c_pT[:, m % 2]
                        mm(win[:, 0:VA], pT[:, 0, k * P:(k + 1) * P], v[0][:, h, :], first, end)
                        c1 = (k % 2) * SEQ
                        mm(win[:, VA:2 * VA], pT[:, 1 + k // 2, c1:c1 + P], v[0][:, h, :], False, False)
                        last = mm(win[:, VA:2 * VA], pT[:, 1 + k // 2, c1 + P:c1 + SEQ], v[1][:, h, :], False, end)
                    last.then_inc(S("c_win_mm"), 1)

                for i in range(4 + 1):
                    if i < 4:
                        scores(i)
                    if i >= 1:
                        turn(i - 1)
                        values(i - 1)

            def c_out(n):
                o = claim(pe, "c_cT", n, "c_catT", n + 1)
                pe.wait_ge(S("c_cat"), 2 * n + 2)
                for s in range(2):
                    for f in range(2):
                        last = pe.transpose(o[:, (2 * f + s) * P:(2 * f + s + 1) * P],
                                            c_cat[:, n % 2, s, f * P:(f + 1) * P], ident[:, :])
                last.then_inc(S("c_cT_mm"), 1)
                if n % NB < NB - 1:
                    o = claim(pe, "c_y", n, "c_xsum", n // NB + 1)
                else:
                    o = claim(pe, "c_y", n, "x_sum", G * PH.index("C") + n // NB + 1)
                pe.wait_ge(S("c_catT"), n + 1)
                for s in range(2):
                    for f in range(2):
                        last = mm(o[:, s * P:(s + 1) * P], c_catT[:, f, s * P:(s + 1) * P], wout_c[:, f, :],
                                  f == 0, f == 1)
                last.then_inc(S("c_y_mm"), 1)

            if "C" in PH:
                for g in range(G):
                    c_turn(g)
                for b in (6, 7):
                    pe.wait_ge(*freed_by[b])
                ring["banks"] = list(range(6))
                skew([c_proj, c_heads, c_out], NB * G)
                ring["banks"] = list(range(8))
                for b in (6, 7):
                    freed_by[b] = (S("c_cat"), 2 * NB * G)

            def moe(n, u, key):
                def up(g):
                    pe.wait_ge(S("ln_xT"), turned(u) * G + g + 1)
                    o = claim(pe, f"d_g{n}", g, "d_exp", n * G + g + 1)
                    for j in range(TG):
                        last = mm(o[:, j * NE:(j + 1) * NE], xnT[:, g, j * P:(j + 1) * P], gateT[:, :])
                    last.then_inc(S("d_g_mm"), 1)
                    for c in range(NF):
                        k = n * G * NF + NF * g + c
                        o = claim(pe, "d_s", k, "d_srelu", k + 1)
                        mm(o, moe_up[:, FF + c * P:FF + (c + 1) * P], xnT[:, g, :]).then_inc(S("d_s_mm"), 1)

                def turn_gate(g):
                    k = n * G + g
                    o = claim(pe, "d_pT", k, "d_partsT", k + 1).bitcast(BF16)
                    pe.wait_ge(S("d_gate"), k + 1)
                    for j in range(TG):
                        last = pe.transpose(o[0:96, j * P:(j + 1) * P], d_parts[:, g % 2, j, :], ident_bf[:, :])
                    last.then_inc(S("d_pT_mm"), 1)

                def experts(g):
                    turn_gate(g)
                    for c in range(NF):
                        k = n * G * NF + NF * g + c
                        o = claim(pe, "d_u", k, "d_relu", k + 1)
                        mm(o, moe_up[:, c * P:(c + 1) * P], xnT[:, g, :]).then_inc(S("d_u_mm"), 1)
                        o = claim(pe, "d_b", k, "d_gated", k + 1)
                        if c == 0:
                            pe.wait_ge(S("d_partsT"), n * G + g + 1)
                        mm(o, gate_sel[0:96, c, :], d_partsT[0:96, g % 2, :]).then_inc(S("d_b_mm"), 1)

                def down(g):
                    o = claim(pe, f"d_y{n}", g, "x_sum", G * PH.index(key) + g + 1)
                    pe.wait_ge(S("d_sq"), (n * G + g + 1) * NF)
                    pe.wait_ge(S("d_r2"), (n * G + g + 1) * NF)
                    for j in range(TG):
                        for c in range(2 * NF):
                            last = mm(o[:, j * P:(j + 1) * P], d_r2[:, g % 3, c, j * P:(j + 1) * P], moe_dn[:, c, :],
                                      c == 0, c == 2 * NF - 1)
                    last.then_inc(S("d_y_mm"), 1)
                skew([None, ln_transpose(u), up, experts, down], G)

            if "D" in PH:
                moe(0, LN_D0, "D")

            def e_layer(l):
                w4, w1, w2 = e_w4[l % 2], e_w1[l % 2], e_w2[l % 2]

                def qkv(g):
                    n = l * G + g
                    if g == 0:
                        pe.wait_ge(S(f"e_in{l % 2}"), E_IN * (l // 2 + 1))
                    pe.wait_ge(S("ln_xT"), turned(LN_E + 2 * l) * G + g + 1)
                    o = claim(pe, "e_k", n, "e_kexp", NB * (n + 1))
                    mm(o, w4[:, 1, :], xnT[:, g, :]).then_inc(S("e_k_mm"), 1)
                    o = claim(pe, "e_q", n, "e_qsub", n + 1)
                    for j in range(TG):
                        last = mm(o[:, j * P:(j + 1) * P], xnT[:, g, j * P:(j + 1) * P], w4[:, 0, :])
                    last.then_inc(S("e_q_mm"), 1)
                    o = claim(pe, "e_v", n, "e_v", n + 1)
                    for j in range(TG):
                        last = mm(o[:, j * P:(j + 1) * P], xnT[:, g, j * P:(j + 1) * P], w4[:, 2, :])
                    last.then_inc(S("e_v_mm"), 1)

                def turn(g):
                    n = l * G + g
                    o = claim(pe, "e_kT", n, "e_k", n + 1)
                    pe.wait_ge(S("e_kexp"), NB * (n + 1))
                    for j in range(TG):
                        last = pe.transpose(o[:, j * P:(j + 1) * P], e_kTe[:, g % 2, j * P:(j + 1) * P], ident[:, :])
                    last.then_inc(S("e_kT_mm"), 1)
                    o = claim(pe, "e_qT", n, "e_qT", n + 1)
                    pe.wait_ge(S("e_qn"), n + 1)
                    for j in range(TG):
                        last = pe.transpose(o[:, j * P:(j + 1) * P], e_qe[:, g % 2, j * P:(j + 1) * P], ident[:, :])
                    last.then_inc(S("e_qT_mm"), 1)

                def context(g):
                    n = l * G + g
                    o = claim(pe, "e_c", n, "e_ctx", n + 1)
                    pe.wait_ge(S("e_k"), n + 1)
                    pe.wait_ge(S("e_v"), n + 1)
                    for b in range(NB):
                        for s in range(2):
                            j = (2 * b + s) * P
                            last = mm(o[:, b * P:(b + 1) * P], e_v[:, g % 3, j:j + P], e_k[:, g % 2, j:j + P], s == 0, s == 1)
                    last.then_inc(S("e_c_mm"), 1)

                def fold(g):
                    n = l * G + g
                    o = claim(pe, "e_m", n, "e_m", n + 1)
                    pe.wait_ge(S("e_ctx"), n + 1)
                    for b in range(NB):
                        last = mm(o[:, b * P:(b + 1) * P], e_ctx[:, g % 2, b, :], w4[:, 3, :])
                    last.then_inc(S("e_m_mm"), 1)

                def out_(g):
                    n = l * G + g
                    o = claim(pe, "e_y", n, "e_z1", n + 1)
                    pe.wait_ge(S("e_m"), n + 1)
                    pe.wait_ge(S("e_qT"), n + 1)
                    for j in range(TG):
                        last = mm(o[:, j * P:(j + 1) * P], e_qT[:, g, j * P:(j + 1) * P], e_m[:, g % 2, j // 2, :])
                    last.then_inc(S("e_y_mm"), 1)

                def up(g):
                    n = l * G + g
                    pe.wait_ge(S("ln_xT"), turned(LN_E + 2 * l + 1) * G + g + 1)
                    for c in range(NF):
                        o = claim(pe, "e_u", NF * n + c, "e_h", NF * n + c + 1)
                        mm(o, w1[:, c * P:(c + 1) * P], xnT[:, g, :]).then_inc(S("e_u_mm"), 1)

                def down(g):
                    n = l * G + g
                    o = claim(pe, "e_d", n, "e_z2", n + 1)
                    pe.wait_ge(S("e_h"), NF * (n + 1))
                    for j in range(TG):
                        for c in range(NF):
                            h0 = c * TOK + j * P
                            last = mm(o[:, j * P:(j + 1) * P], e_h[:, g % 3, h0:h0 + P], w2[:, c, :], c == 0, c == NF - 1)
                    last.then_inc(S("e_d_mm"), 1)

                skew([None, ln_transpose(LN_E + 2 * l), qkv, turn, context, fold, out_,
                      None, ln_transpose(LN_E + 2 * l + 1), up, down], G)

            if "E" in PH:
                for l in range(DEPTH):
                    e_layer(l)
            if "d" in PH:
                moe(1, LN_D1, "d")

        @block.vector
        def _(dve):
            def tt(o, a, b, op):
                return dve.tensor_tensor(o, a, b, op)

            def ln_stats(u, src):
                def stage(g):
                    if src is x and u == 0:
                        dve.wait_ge(S(f"x_in{g}"), 16)
                    if src is x and u > 0:
                        dve.wait_ge(S("x_sum"), G * LN_PH[u] + g + 1)
                    if src is z:
                        if (u - LN_E) % 2 == 1:
                            dve.wait_ge(S("e_z1"), ((u - LN_E) // 2) * G + g + 1)
                        elif u > LN_E:
                            dve.wait_ge(S("e_z2"), ((u - LN_E) // 2 - 1) * G + g + 1)
                        else:
                            dve.wait_ge(S("z_in"), g + 1)
                    for t in tiles(g):
                        last = dve.bn_stats(st[:, t, :], src[:, t, :])
                    last.then_inc(S("ln_st"), 1)
                    dve.wait_ge(S("ln_st"), u * G + g + 1)
                    for t in tiles(g):
                        last = dve.bn_aggr(mv[:, t, :], st[:, t, :])
                    last.then_inc(S("ln_mv"), 1)
                    dve.wait_ge(S("ln_mv"), u * G + g + 1)
                    dve.tensor_scalar(var_eps[:, TG * g:TG * g + TG], mv[:, TG * g:TG * g + TG, 1], 1e-5, None,
                                      ALU.add).then_inc(S("ln_ve"), 1)
                return stage

            def normalise(u, src, g, dst, scale):
                for t in tiles(g):
                    last = dve.tensor_scalar(dst[:, t, :], src[:, t, :], mv[:, t, 0:1], scale[:, t:t + 1],
                                             ALU.subtract, ALU.mult)
                return last

            def ln_apply(u, src):
                def stage(g):
                    dve.wait_ge(S("ln_rs"), u * G + g + 1)
                    normalise(u, src, g, xn, rstd).then_inc(S("ln_xn"), 1)
                return stage

            dve.wait_ge(S("masks"), 1)
            dve.tensor_copy(ident_bf[:, :], ident[:, :]).then_inc(S("dve_const"), 1)
            dve.tensor_copy(bd8, head8[:, :].unsqueeze(2).to_broadcast([P, HC, DC])).then_inc(S("dve_const"), 1)
            dve.tensor_copy(bd16[:, :, :], head16[:, :].unsqueeze(2).to_broadcast([P, HE, DE])).then_inc(S("dve_const"), 1)
            dve.wait_ge(S("dve_const"), 3)
            n_out = [0]

            def evac(dst, src):
                n_out[0] += 1
                dve.tensor_copy(dst, src).then_inc(S("prep_out"), 1)

            def prep(i):
                dve.wait_ge(S("prep_mm"), i + 1)
                return bank("prep", i)

            o = prep(0)
            evac(a_w[:, :], o[:, 0:2 * P])
            dve.wait_ge(S("f_in"), F_IN)
            flat_up = s_up0.rearrange("p c d -> p (c d)")
            dve.tensor_reduce(s_absum[:, 0:1], flat_up, X, ALU.add, apply_absolute_value=True).then_inc(S("f_abs"), 1)
            dve.tensor_reduce(s_absum[:, 1:2], s_dn0, X, ALU.add, apply_absolute_value=True).then_inc(S("f_abs"), 1)
            o = prep(1)
            half_mean = 0.5 / (P * FF)
            dve.tensor_scalar(s_thr[:, 0:2], o[:, 0:2], half_mean, None, ALU.mult).then_inc(S("prep_out"), 1)
            dve.tensor_scalar(s_thr[:, 2:4], o[:, 0:2], -half_mean, None, ALU.mult).then_inc(S("prep_out"), 1)
            n_out[0] += 2
            dve.wait_ge(S("prep_out"), n_out[0])
            for i, src in enumerate((flat_up, s_dn0)):
                dve.tensor_scalar(s_tern[:, i, :], src, s_thr[:, 2 + i:3 + i], None, ALU.is_lt).then_inc(S("f_neg"), 1)
                dve.wait_ge(S("f_neg"), i + 1)
                dve.scalar_tensor_tensor(out=s_wt[:, i, :], in0=src, scalar=s_thr[:, i:i + 1], in1=s_tern[:, i, :],
                                         op0=ALU.is_gt, op1=ALU.subtract).then_inc(S("f_tern"), 1)
            o = prep(2)
            evac(wupT[:, :], o)
            o = prep(3)
            evac(wdnT[:, :, :].rearrange("p c f -> p (c f)"), o)
            for i in range(2):
                o = prep(4 + i)
                evac(wvT[:, 4 * i:4 * i + 4, :].rearrange("p c f -> p (c f)"), o)
            o = prep(6)
            evac(s_cfT[0:16, :, :].rearrange("p c f -> p (c f)"), o[0:16, 0:2 * P])
            evac(cols[:, :], o[:, 2 * P:2 * P + 25])
            dve.wait_ge(S("prep_out"), n_out[0])
            for i in (WQ, WK, WV):
                dve.tensor_scalar(c_w[:, i, :], c_w[:, i, :], cols[:, 24:25], None, ALU.mult).then_inc(S("c_scaled"), 1)
            o = prep(7)
            tt(s_bd, o[:, 0:P], bd8.rearrange("p h d -> p (h d)"), ALU.mult).then_inc(S("prep_out"), 1)
            n_out[0] += 1
            o = prep(8)
            evac(s_wqT, o[:, 0:P])
            o = prep(9)
            evac(c_w[:, WQP, :], o[:, 0:P])
            o = prep(10)
            evac(s_w1T[0:64, :], o[0:64, :])
            o = prep(11)
            evac(s_fc2T[0:64, :], o[0:64, 0:P])
            evac(gateT[:, :], o[:, P:P + NE])
            o = prep(12)
            evac(moe_up[:, 0:FF], o)
            o = prep(13)
            evac(moe_up[:, FF:2 * FF], o)
            o = prep(14)
            evac(moe_dn[:, 0:NF, :].rearrange("p c f -> p (c f)"), o)
            o = prep(15)
            evac(moe_dn[:, NF:2 * NF, :].rearrange("p c f -> p (c f)"), o)
            assert n_out[0] == PREP_OUT[-1], n_out

            def a_values(g):
                dve.wait_ge(S("a_v_mm"), g + 1)
                dve.tensor_copy(a_v[:, g, :, :].rearrange("p t f -> p (t f)"), bank("a_v", g)).then_inc(S("a_v"), 1)

            def a_max(g):
                for b in range(NB):
                    n = NB * g + b
                    dve.wait_ge(S("a_s_mm"), n + 1)
                    o = bank("a_s", n)
                    dve.tensor_reduce(a_nmax[:, 0, 2 * n:2 * n + 1], o[:, 0:P], X, ALU.max).then_inc(S("a_max"), 1)
                    dve.tensor_reduce(a_nmax[:, 0, 2 * n + 1:2 * n + 2], o[:, P:384], X, ALU.max).then_inc(S("a_max"), 1)
                    dve.wait_ge(S("a_max"), 2 * n + 2)
                    dve.tensor_scalar(a_nmax[:, 1, 2 * n:2 * n + 2], a_nmax[:, 0, 2 * n:2 * n + 2], -P ** -0.5, None,
                                      ALU.mult).then_inc(S("a_nmax"), 1)

            def a_turned(g):
                dve.wait_ge(S("a_exp"), TG * (g + 1))
                dve.reciprocal(a_sum[:, 1, TG * g:TG * g + TG], a_sum[:, 0, TG * g:TG * g + TG]).then_inc(S("a_rec"), 1)
                dve.wait_ge(S("a_pT_mm"), NB * g + 2)
                dve.tensor_copy(a_pT[:, g % 2, 1, :], bank("a_pT", NB * g + 1)[:, 0:384]).then_inc(S("a_pT1"), 1)

            def a_add(g):
                dve.wait_ge(S("a_o_mm"), g + 1)
                dve.wait_ge(S("a_rec"), g + 1)
                o = bank("a_o", g)
                for j, t in enumerate(tiles(g)):
                    last = dve.scalar_tensor_tensor(out=x[:, t, :], in0=o[:, j * P:(j + 1) * P], scalar=a_sum[:, 1, t:t + 1],
                                                    in1=x[:, t, :], op0=ALU.mult, op1=ALU.add)
                last.then_inc(S("x_sum"), 1)

            if "A" in PH:
                skew([ln_stats(LN_A, x), ln_apply(LN_A, x), a_values, a_max, a_turned, a_add], G)

            def ffn(n, u, key):
                def rms_in(g):
                    ts = slice(TG * g, TG * g + TG)
                    dve.wait_ge(S("ln_rs"), u * G + g + 1)
                    tt(second[:, 0, ts], mv[:, ts, 1], rstd[:, ts], ALU.mult).then_inc(S("s2_a"), 1)
                    dve.wait_ge(S("s2_a"), S2[u] * G + g + 1)
                    tt(second[:, 1, ts], second[:, 0, ts], rstd[:, ts], ALU.mult).then_inc(S("s2_b"), 1)

                def apply(g):
                    ts = slice(TG * g, TG * g + TG)
                    dve.wait_ge(S("s2_pow"), S2[u] * G + g + 1)
                    dve.tensor_scalar(second[:, 0, ts], second[:, 2, ts], 1e-8, None, ALU.add).then_inc(S("s2_c"), 1)
                    dve.wait_ge(S("s2_c"), 3 * (n * G + g) + 1)
                    dve.reciprocal(second[:, 1, ts], second[:, 0, ts]).then_inc(S("s2_c"), 1)
                    dve.wait_ge(S("s2_c"), 3 * (n * G + g) + 2)
                    tt(second[:, 0, ts], second[:, 1, ts], rstd[:, ts], ALU.mult).then_inc(S("s2_c"), 1)
                    dve.wait_ge(S("s2_c"), 3 * (n * G + g) + 3)
                    normalise(u, x, g, xn, second[:, 0, :]).then_inc(S("ln_xn"), 1)

                def squares(g):
                    k = n * G + g
                    dve.wait_ge(S("f_sq"), k + 1)
                    dve.tensor_reduce(f_ssq[:, g % 2, :], f_sq[:, g % 2, :].rearrange("p (c t) -> p t c", c=NF), X,
                                      ALU.add).then_inc(S("f_ssq"), 1)

                def mean_square(g):
                    k = n * G + g
                    dve.wait_ge(S("f_ss_mm"), k + 1)
                    dve.tensor_scalar(f_r[:, 0, TG * g:TG * g + TG], bank(f"f_ss{n}", g)[:, 0:TG], 1.0 / FF, None,
                                      ALU.mult).then_inc(S("f_ms"), 1)

                def add(g):
                    k = n * G + g
                    ts = slice(TG * g, TG * g + TG)
                    dve.wait_ge(S("f_pow"), k + 1)
                    dve.tensor_scalar(f_r[:, 0, ts], f_r[:, 1, ts], 1e-8, None, ALU.add).then_inc(S("f_rc"), 1)
                    dve.wait_ge(S("f_rc"), 2 * k + 1)
                    dve.reciprocal(f_r[:, 2, ts], f_r[:, 0, ts]).then_inc(S("f_rc"), 1)
                    dve.wait_ge(S("f_rc"), 2 * k + 2)
                    dve.wait_ge(S("f_y_mm"), k + 1)
                    o = bank(f"f_y{n}", g)
                    for j, t in enumerate(tiles(g)):
                        last = dve.scalar_tensor_tensor(out=x[:, t, :], in0=o[:, j * P:(j + 1) * P],
                                                        scalar=f_r[:, 2, t:t + 1], in1=x[:, t, :],
                                                        op0=ALU.mult, op1=ALU.add)
                    last.then_inc(S("x_sum"), 1)
                skew([ln_stats(u, x), rms_in, apply, None, squares, mean_square, add], G)

            if "F" in PH:
                ffn(0, LN_F0, "F")

            def b_softmax(g):
                if g == 0:
                    dve.memset(b_ctx, 0.0).then_inc(S("b_zero"), 1)
                    dve.wait_ge(S("b_zero"), 1)

                def q_tile(j):
                    n = TG * g + j
                    r = n % 4
                    if g >= 2 and j == 0:
                        dve.wait_ge(S("b_c_mm"), 2 * NB * (g - 1))
                    for half in range(2):
                        hs = slice(half * 8, half * 8 + 8)
                        dve.wait_ge(S("b_q_mm"), 2 * n + half + 1)
                        o = bank("b_q", 2 * n + half).rearrange("p (h d) -> p h d", d=QD)
                        dve.tensor_reduce(b_qmax[:, r, hs], o, X, ALU.max).then_inc(S("b_qmax"), 1)
                        dve.wait_ge(S("b_qmax"), 2 * n + half + 1)
                        tt(b_q[:, g % 2, j, half * 512:half * 512 + 512].rearrange("p (h d) -> p h d", d=QD), o,
                           b_qmax[:, r, hs].unsqueeze(2).to_broadcast([P, 8, QD]), ALU.subtract).then_inc(S("b_qsub"), 1)

                def q_sum(j):
                    n = TG * g + j
                    r = n % 4
                    dve.wait_ge(S("b_qexp"), n + 1)
                    dve.tensor_reduce(b_qsum[:, r, :], b_q[:, g % 2, j, :].rearrange("p (h d) -> p h d", d=QD), X,
                                      ALU.add).then_inc(S("b_qsum"), 1)
                    dve.wait_ge(S("b_qsum"), n + 1)
                    if n >= 4:
                        dve.wait_ge(S("b_qn"), n - 3)
                    dve.reciprocal(b_qrec[:, r, :], b_qsum[:, r, :]).then_inc(S("b_qrec"), 1)

                def k_max(c):
                    n = NC_ * g + c
                    dve.wait_ge(S("b_k_mm"), n + 1)
                    dve.tensor_reduce(b_kmax[:, n, :], bank("b_k", n).rearrange("p (b t) -> p b t", b=NB), X, ALU.max,
                                      negate=True).then_inc(S("b_kmax"), 1)

                def k_turned(c):
                    n = NC_ * g + c
                    if g >= 2 and c == 0:
                        dve.wait_ge(S("b_c_mm"), 2 * NB * (g - 1))
                    dve.wait_ge(S("b_kT_mm"), n + 1)
                    dve.tensor_copy(b_k[:, g % 2, :, c * P:(c + 1) * P],
                                    bank("b_kT", n).rearrange("p (t f) -> p t f", f=P)).then_inc(S("b_k"), 1)

                for c in range(NC_ + 2):
                    if c < NC_:
                        k_max(c)
                        if c % 2 == 0:
                            q_tile(c // 2)
                    if c >= 2:
                        k_turned(c - 2)
                        if c % 2 == 0:
                            q_sum(c // 2 - 1)
                dve.wait_ge(S("b_kexp"), NB * NC_ * (g + 1))
                dve.reciprocal(b_krec[:, g % 2, :, :], b_ksum[:, g % 2, :, :]).then_inc(S("b_krec"), 1)

            def b_context(g):
                dve.wait_ge(S("b_krec"), g + 1)
                for b in range(NB):
                    n = NB * g + b
                    if n >= 4:
                        dve.wait_ge(S("b_m_mm"), 2 * (n - 3))
                    for half in range(2):
                        dve.wait_ge(S("b_c_mm"), 2 * n + half + 1)
                        cs = slice(4 * half, 4 * half + 4)
                        for q in range(2):
                            r = slice(64 * q, 64 * q + 64)
                            src = bank("b_c", 2 * n + half).rearrange("p (c d) -> p c d", d=P)
                            tt(b_ctx[r, n % 4, cs, r], src[r, :, r],
                               b_krec[r, g % 2, b, cs].unsqueeze(2).to_broadcast([64, 4, 64]),
                               ALU.mult).then_inc(S("b_ctx"), 1)

            def b_fold(g):
                for b in range(NB):
                    n = NB * g + b
                    dve.wait_ge(S("b_g_mm"), n + 1)
                    dve.tensor_copy(b_g[:, n % 4, :], bank("b_g", n)[:, 0:P]).then_inc(S("b_g"), 1)

            def b_add(g):
                dve.wait_ge(S("b_xb"), g + 1)
                dve.wait_ge(S("b_y_mm"), g + 1)
                xg = x[:, TG * g:TG * g + TG, :].rearrange("p t f -> p (t f)")
                tt(xg, bank("b_y", g), xg, ALU.add).then_inc(S("x_sum"), 1)

            if "B" in PH:
                skew([ln_stats(LN_B, x), ln_apply(LN_B, x), b_softmax, b_context, b_fold, b_add], G)
            if "f" in PH:
                ffn(1, LN_F1, "f")

            def c_rms(g):
                ts = slice(TG * g, TG * g + TG)
                k = S2[LN_C] * G + g
                dve.wait_ge(S("ln_rs"), LN_C * G + g + 1)
                tt(second[:, 0, ts], mv[:, ts, 1], rstd[:, ts], ALU.mult).then_inc(S("s2_a"), 1)
                dve.wait_ge(S("s2_a"), k + 1)
                tt(second[:, 1, ts], second[:, 0, ts], rstd[:, ts], ALU.mult).then_inc(S("s2_b"), 1)
                dve.wait_ge(S("s2_b"), k + 1)
                dve.tensor_scalar(second[:, 0, ts], second[:, 1, ts], 1e-6, None, ALU.add).then_inc(S("c_ms"), 1)
                normalise(LN_C, x, g, z, rstd).then_inc(S("c_ln"), 1)

            def c_apply(g):
                dve.wait_ge(S("s2_pow"), S2[LN_C] * G + g + 1)
                dve.wait_ge(S("c_ln"), g + 1)
                for t in tiles(g):
                    last = dve.tensor_scalar(xn[:, t, :], z[:, t, :], second[:, 2, t:t + 1], None, ALU.mult)
                last.then_inc(S("ln_xn"), 1)

            def c_proj(n):
                if n >= 2:
                    dve.wait_ge(S("c_l_mm"), 3 * 4 * (n - 1))
                dve.wait_ge(S("c_kT"), n + 1)
                for h in range(HC):
                    last = dve.tensor_scalar(c_km[:, n % 2, h, :], c_kT[:, n % 2, :], head8[:, h:h + 1], None, ALU.mult)
                last.then_inc(S("c_km"), 1)
                dve.wait_ge(S("c_v_mm"), n + 1)
                if n == 0:
                    dve.wait_ge(S("c_zero"), 8)
                if n >= 2:
                    dve.wait_ge(S("c_win_mm"), 4 * (n - 1))
                for s in range(2):
                    last = dve.tensor_copy(own_columns((2 * n + s) % 4),
                                           bank("c_v", n)[:, s * P:(s + 1) * P].rearrange("p (h d) -> p h d", d=DC))
                last.then_inc(S("c_vm"), 1)

            def c_heads(n):
                def softmax(i):
                    m = 4 * n + i
                    mx = c_max[:, m % 4, :]
                    if m >= 2:
                        dve.wait_ge(S("c_t_mm"), 3 * (m - 1))
                    dve.wait_ge(S("c_s_mm"), 3 * m + 1)
                    o = bank("c_s0", m).rearrange("p (h k) -> p h k", k=P)
                    dve.tensor_reduce(mx[:, 0:4], o, X, ALU.max).then_inc(S("c_max"), 1)
                    dve.wait_ge(S("c_s_mm"), 3 * m + 2)
                    o0 = bank("c_s1", 2 * m)[:, 0:384].rearrange("p (h k) -> p h k", k=192)
                    dve.tensor_reduce(mx[:, 4:6], o0, X, ALU.max).then_inc(S("c_max"), 1)
                    dve.wait_ge(S("c_max"), 3 * m + 1)
                    tt(c_p0[:, m % 2], o, mx[:, 0:4].unsqueeze(2).to_broadcast([P, 4, P]), ALU.subtract)\
                        .then_inc(S("c_sub"), 1)
                    dve.wait_ge(S("c_s_mm"), 3 * m + 3)
                    o1 = bank("c_s1", 2 * m + 1)[:, 0:384].rearrange("p (h k) -> p h k", k=192)
                    dve.tensor_reduce(mx[:, 6:8], o1, X, ALU.max).then_inc(S("c_max"), 1)
                    dve.wait_ge(S("c_max"), 3 * m + 2)
                    tt(c_p1[:, m % 2, 0:2, 64:SEQ], o0, mx[:, 4:6].unsqueeze(2).to_broadcast([P, 2, 192]),
                       ALU.subtract).then_inc(S("c_sub"), 1)
                    dve.wait_ge(S("c_max"), 3 * m + 3)
                    tt(c_p1[:, m % 2, 2:4, 64:SEQ], o1, mx[:, 6:8].unsqueeze(2).to_broadcast([P, 2, 192]),
                       ALU.subtract).then_inc(S("c_sub"), 1)

                def turn_out(i):
                    m = 4 * n + i
                    if m >= 2:
                        dve.wait_ge(S("c_win_mm"), m - 1)
                    dve.wait_ge(S("c_t_mm"), 3 * m + 1)
                    dve.tensor_copy(c_pT[:, m % 2, 0, :], bank("c_t0", 3 * m)).then_inc(S("c_pT_dve"), 1)

                for i in range(5):
                    if i < 4:
                        softmax(i)
                    if i >= 1:
                        turn_out(i - 1)
                dve.wait_ge(S("c_win_mm"), 4 * (n + 1))
                r = c_rec[:, n % 2]
                r2 = c_rec[:, 2 + n % 2]
                for half, b in ((0, 6), (1, 7)):
                    acc = ps[:, b, 0:2 * VA].rearrange("p (s v) -> p s v", v=VA)
                    dve.tensor_scalar(r, acc[:, :, P:VA], 1e-6 if half == 0 else 0.0, None, ALU.add)\
                        .then_inc(S("c_den"), 1)
                    dve.wait_ge(S("c_den"), 2 * n + half + 1)
                    dve.reciprocal(r2, r).then_inc(S("c_rden"), 1)
                    dve.wait_ge(S("c_rden"), 2 * n + half + 1)
                    for s in range(2):
                        last = tt(c_cat[:, n % 2, s, half * P:(half + 1) * P].rearrange("p (h d) -> p h d", d=DC),
                                  acc[:, s, 0:P].rearrange("p (h d) -> p h d", d=DC),
                                  r2[:, s, :].unsqueeze(2).to_broadcast([P, HC, DC]), ALU.mult)
                    last.then_inc(S("c_cat"), 1)
                    if half == 0:
                        dve.wait_ge(S("c_cat"), 2 * n + 1)

            def c_add(n):
                g = n // NB
                if n % NB == 0:
                    dve.wait_ge(S("c_xz"), g + 1)
                dve.wait_ge(S("c_y_mm"), n + 1)
                xs = x[:, 2 * n:2 * n + 2, :].rearrange("p t f -> p (t f)")
                tt(xs, bank("c_y", n)[:, 0:SEQ], xs, ALU.add).then_inc(S("c_xsum" if n % NB < NB - 1 else "x_sum"), 1)

            if "C" in PH:
                skew([ln_stats(LN_C, x), c_rms, c_apply], G)
                skew([c_proj, c_heads, c_add], NB * G)

            def moe(n, u, key):
                def route(g):
                    k = n * G + g
                    chain = [ROUTE * k]

                    def link(ins):
                        chain[0] += 1
                        ins.then_inc(S("d_route"), 1)
                        dve.wait_ge(S("d_route"), chain[0])

                    v3 = lambda a: a.rearrange("p (t e) -> p t e", t=TG)
                    dve.wait_ge(S("d_exp"), k + 1)
                    link(dve.tensor_scalar(d_sc[:, g, 0, :], d_e[:, g, :], 1.0, None, ALU.add))
                    link(dve.reciprocal(d_sc[:, g, 1, :], d_sc[:, g, 0, :]))
                    sc, sfc = d_sc[:, g, 1, :], d_sfc[:, g, :]
                    link(tt(v3(sfc), v3(sc), bias_bc[:, :].unsqueeze(1).to_broadcast([P, TG, NE]), ALU.add))
                    s4 = sfc.rearrange("p (q e) -> p q e", e=4)
                    tp = d_top[:, g]
                    a, b, c, d = (s4[:, :, i] for i in range(4))
                    link(tt(tp[:, 0, :], a, b, ALU.max))
                    link(tt(tp[:, 1, :], a, b, ALU.min))
                    link(tt(tp[:, 2, :], c, d, ALU.max))
                    link(tt(tp[:, 3, :], c, d, ALU.min))
                    link(tt(tp[:, 4, :], tp[:, 0, :], tp[:, 2, :], ALU.max))
                    link(tt(tp[:, 5, :], tp[:, 0, :], tp[:, 2, :], ALU.min))
                    link(tt(tp[:, 6, :], tp[:, 1, :], tp[:, 3, :], ALU.max))
                    link(tt(tp[:, 7, :], tp[:, 5, :], tp[:, 6, :], ALU.max))
                    link(tt(tp[:, 0, :], tp[:, 4, :], tp[:, 7, :], ALU.add))
                    gs = tp[:, 0, :].rearrange("p (t q) -> p t q", q=2)
                    gm = tp[:, 1, :].rearrange("p (t q) -> p t q", q=2)
                    link(tt(gm[:, :, 0], gs[:, :, 0], gs[:, :, 1], ALU.is_ge))
                    link(tt(gm[:, :, 1], gs[:, :, 0], gs[:, :, 1], ALU.is_lt))
                    link(tt(s4, s4, tp[:, 1, :].unsqueeze(2).to_broadcast([P, 2 * TG, 4]), ALU.mult))
                    s_j = v3(sfc).unsqueeze(2).to_broadcast([P, TG, NE, NE])
                    s_e = v3(sfc).unsqueeze(3).to_broadcast([P, TG, NE, NE])
                    c0 = d_cmp[:, g % 2, 0, :].rearrange("p (t e j) -> p t e j", t=TG, e=NE)
                    c1 = d_cmp[:, g % 2, 1, :].rearrange("p (t e j) -> p t e j", t=TG, e=NE)
                    link(tt(c1, s_j, s_e, ALU.is_equal))
                    link(tt(c1, c1, lower[:, :, :].unsqueeze(1).to_broadcast([P, TG, NE, NE]), ALU.mult))
                    link(tt(c0, s_j, s_e, ALU.is_gt))
                    link(tt(d_cmp[:, g % 2, 0, :], d_cmp[:, g % 2, 0, :], d_cmp[:, g % 2, 1, :], ALU.add))
                    link(dve.tensor_reduce(d_rank[:, g, :], d_cmp[:, g % 2, 0, :].rearrange("p (q j) -> p q j", j=NE), X,
                                           ALU.add))
                    link(dve.scalar_tensor_tensor(out=d_w[:, g, :], in0=d_rank[:, g, :], scalar=1.5, in1=sc,
                                                  op0=ALU.is_lt, op1=ALU.mult))
                    link(dve.tensor_reduce(d_den[:, g, 0, :], v3(d_w[:, g, :]), X, ALU.add))
                    link(dve.tensor_scalar(d_den[:, g, 0, :], d_den[:, g, 0, :], 1e-20, None, ALU.add))
                    link(dve.reciprocal(d_den[:, g, 1, :], d_den[:, g, 0, :]))
                    link(tt(v3(d_gate[:, g, :]), v3(d_w[:, g, :]), d_den[:, g, 1, :].unsqueeze(2).to_broadcast([P, TG, NE]),
                            ALU.mult))
                    if g < 2:
                        link(dve.memset(d_parts[:, g % 2], 0.0))
                    elif g >= 2:
                        link(dve.memset(d_cmp[:, g % 2, 1, 0:1], 0.0))
                        dve.wait_ge(S("d_pT_mm"), k - 1)
                    part = [d_parts[:, g % 2, :, 32 * i:32 * i + NE] for i in range(3)]
                    rest = [d_rest[:, g % 2, i, :] for i in range(2)]
                    link(dve.tensor_copy(part[0], v3(d_gate[:, g, :])))
                    link(tt(v3(rest[0]), v3(d_gate[:, g, :]), part[0], ALU.subtract))
                    link(dve.tensor_copy(part[1], v3(rest[0])))
                    link(tt(v3(rest[1]), v3(rest[0]), part[1], ALU.subtract))
                    assert chain[0] == ROUTE * (k + 1), chain
                    dve.tensor_copy(part[2], v3(rest[1])).then_inc(S("d_gate"), 1)

                def gated(g):
                    for c in range(NF):
                        k = (n * G + g) * NF + c
                        dve.wait_ge(S("d_relu"), k + 1)
                        dve.wait_ge(S("d_b_mm"), k + 1)
                        if c == 0 and g >= 3:
                            dve.wait_ge(S("d_y_mm"), n * G + g - 2)
                        r2 = d_r2[:, g % 3, c, :]
                        tt(r2, d_r[:, k % 4, :], bank("d_b", k), ALU.mult).then_inc(S("d_gated"), 1)
                        dve.wait_ge(S("d_gated"), k + 1)
                        tt(r2, r2, d_r[:, k % 4, :], ALU.mult).then_inc(S("d_r2"), 1)

                def add(g):
                    dve.wait_ge(S("d_y_mm"), n * G + g + 1)
                    xg = x[:, TG * g:TG * g + TG, :].rearrange("p t f -> p (t f)")
                    tt(xg, bank(f"d_y{n}", g), xg, ALU.add).then_inc(S("x_sum"), 1)
                skew([ln_stats(u, x), ln_apply(u, x), route, gated, add], G)

            if "D" in PH:
                moe(0, LN_D0, "D")

            def z_init(g):
                dve.wait_ge(S("ln_rs"), LN_Z * G + g + 1)
                normalise(LN_Z, x, g, z, rstd).then_inc(S("z_in"), 1)

            def e_layer(l):
                def softmax(g):
                    n = l * G + g
                    if g == 0 and l == 0:
                        pass
                    dve.wait_ge(S("e_k_mm"), n + 1)
                    dve.tensor_reduce(e_km[:, g, :], bank("e_k", n).rearrange("p (b t) -> p b t", b=NB), X, ALU.max,
                                      negate=True).then_inc(S("e_kmax"), 1)
                    dve.wait_ge(S("e_q_mm"), n + 1)
                    o = bank("e_q", n).rearrange("p (h d) -> p h d", d=DE)
                    q3 = e_qe[:, g % 2, :].rearrange("p (h d) -> p h d", d=DE)
                    bc = lambda a: a.unsqueeze(2).to_broadcast([P, TG * HE, DE])
                    dve.tensor_reduce(e_qm[:, g, 0, :], o, X, ALU.max).then_inc(S("e_qmax"), 1)
                    dve.wait_ge(S("e_qmax"), n + 1)
                    if n >= 2:
                        dve.wait_ge(S("e_qT_mm"), n - 1)
                    tt(q3, o, bc(e_qm[:, g, 0, :]), ALU.subtract).then_inc(S("e_qsub"), 1)

                def q_norm(g):
                    n = l * G + g
                    q3 = e_qe[:, g % 2, :].rearrange("p (h d) -> p h d", d=DE)
                    bc = lambda a: a.unsqueeze(2).to_broadcast([P, TG * HE, DE])
                    dve.wait_ge(S("e_qexp"), n + 1)
                    dve.tensor_reduce(e_qm[:, g, 1, :], q3, X, ALU.add).then_inc(S("e_qsum"), 1)
                    dve.wait_ge(S("e_qsum"), n + 1)
                    dve.reciprocal(e_qm[:, g, 2, :], e_qm[:, g, 1, :]).then_inc(S("e_qrec"), 1)
                    dve.wait_ge(S("e_qrec"), n + 1)
                    tt(q3, q3, bc(e_qm[:, g, 2, :]), ALU.mult).then_inc(S("e_qn"), 1)
                    dve.wait_ge(S("e_kexp"), NB * (n + 1))
                    dve.reciprocal(e_kr[:, g, :], e_ks[:, g, :]).then_inc(S("e_krec"), 1)
                    dve.wait_ge(S("e_kT_mm"), n + 1)
                    if n >= 2:
                        dve.wait_ge(S("e_c_mm"), n - 1)
                    dve.tensor_copy(e_k[:, g % 2, :], bank("e_kT", n)).then_inc(S("e_k"), 1)

                def context(g):
                    n = l * G + g
                    dve.wait_ge(S("e_c_mm"), n + 1)
                    if n >= 2:
                        dve.wait_ge(S("e_m_mm"), n - 1)
                    tt(e_ctx[:, g % 2], bank("e_c", n)[:, 0:NB * P].rearrange("p (b d) -> p b d", d=P),
                       bd16[:, :, :].rearrange("p h d -> p (h d)").unsqueeze(1).to_broadcast([P, NB, P]),
                       ALU.mult).then_inc(S("e_ctx"), 1)

                def fold(g):
                    n = l * G + g
                    dve.wait_ge(S("e_m_mm"), n + 1)
                    dve.wait_ge(S("e_krec"), n + 1)
                    if n >= 2:
                        dve.wait_ge(S("e_y_mm"), n - 1)
                    tt(e_m[:, g % 2], bank("e_m", n)[:, 0:NB * P].rearrange("p (b d) -> p b d", d=P),
                       e_kr[:, g, :].unsqueeze(2).to_broadcast([P, NB, P]), ALU.mult).then_inc(S("e_m"), 1)

                def add1(g):
                    n = l * G + g
                    dve.wait_ge(S("e_zb"), n + 1)
                    dve.wait_ge(S("e_y_mm"), n + 1)
                    zg = z[:, TG * g:TG * g + TG, :].rearrange("p t f -> p (t f)")
                    tt(zg, bank("e_y", n), zg, ALU.add).then_inc(S("e_z1"), 1)

                def leaky(g):
                    n = l * G + g
                    for c in range(NF):
                        dve.wait_ge(S("e_hs"), NF * n + c + 1)
                        h = e_h[:, g % 3, c * TOK:(c + 1) * TOK]
                        tt(h, bank("e_u", NF * n + c), h, ALU.max).then_inc(S("e_h"), 1)

                def add2(g):
                    n = l * G + g
                    dve.wait_ge(S("e_d_mm"), n + 1)
                    zg = z[:, TG * g:TG * g + TG, :].rearrange("p t f -> p (t f)")
                    tt(zg, bank("e_d", n), zg, ALU.add).then_inc(S("e_z2"), 1)
                u = LN_E + 2 * l
                skew([ln_stats(u, z), ln_apply(u, z), softmax, q_norm, context, fold, add1,
                      ln_stats(u + 1, z), ln_apply(u + 1, z), leaky, add2], G)

            def e_add(g):
                dve.wait_ge(S("e_z2"), (DEPTH - 1) * G + g + 1)
                xg = x[:, TG * g:TG * g + TG, :].rearrange("p t f -> p (t f)")
                tt(xg, z[:, TG * g:TG * g + TG, :].rearrange("p t f -> p (t f)"), xg, ALU.add).then_inc(S("x_sum"), 1)

            if "E" in PH:
                skew([ln_stats(LN_Z, x), z_init], G)
                for l in range(DEPTH):
                    e_layer(l)
                skew([e_add], G)
            if "d" in PH:
                moe(1, LN_D1, "d")

        @block.scalar
        def _(act):
            def ln_out(u, w_col=None, b_col=None):
                def stage(g):
                    act.wait_ge(S("ln_T"), turned(u) * G + g + 1)
                    if w_col is None:
                        act.activation(xnT[:, g, :], bank(f"ln{u}", g), ACT.Copy).then_inc(S("ln_xT"), 1)
                    else:
                        act.activation(xnT[:, g, :], bank(f"ln{u}", g), ACT.Identity, bias=b_col, scale=w_col)\
                            .then_inc(S("ln_xT"), 1)
                return stage

            def a_query(g):
                act.wait_ge(S("a_u_mm"), g + 1)
                if g >= 2:
                    act.wait_ge(S("a_s_mm"), NB * (g - 1))
                act.activation(a_uT[:, g % 2, :], bank("a_u", g), ACT.Copy).then_inc(S("a_uT"), 1)

            def a_exp(g):
                for b in range(NB):
                    n = NB * g + b
                    act.wait_ge(S("a_nmax"), n + 1)
                    if g >= 2:
                        act.wait_ge(S("a_pT_mm"), NB * (g - 2) + b + 1)
                    o = bank("a_s", n)
                    for j, (c0, c1) in enumerate(((0, P), (P, 384))):
                        act.activation(a_p[:, g % 2, b, c0:c1], o[:, c0:c1], ACT.Exp, bias=a_nmax[:, 1, 2 * n + j:2 * n + j + 1],
                                       scale=P ** -0.5, accum_out=a_sum[:, 0, 2 * n + j:2 * n + j + 1])\
                            .then_inc(S("a_exp"), 1)

            def a_turned(g):
                act.wait_ge(S("a_pT_mm"), NB * g + 1)
                if g >= 2:
                    act.wait_ge(S("a_o_mm"), g - 1)
                act.activation(a_pT[:, g % 2, 0, :], bank("a_pT", NB * g)[:, 0:384], ACT.Copy).then_inc(S("a_pT0"), 1)

            act.wait_ge(S("prep_out"), PREP_OUT[-1])
            if "A" in PH:
                skew([None, ln_out(LN_A), a_query, a_exp, a_turned, None], G)

            def ffn(n, u, key):
                def gelu(g):
                    if g == 0:
                        act.wait_ge(S("x_sum"), G * PH.index(key))
                    if g >= 3:
                        act.wait_ge(S("f_y_mm"), n * G + g - 2)
                    for c in range(NF):
                        k = NF * (n * G + g) + c
                        act.wait_ge(S("f_h_mm"), k + 1)
                        act.activation(f_hT[:, g % 3, c * TOK:(c + 1) * TOK], bank(f"f_h{n}", NF * g + c),
                                       ACT.Gelu).then_inc(S("f_gelu"), 1)

                def square(g):
                    act.wait_ge(S("f_gelu"), NF * (n * G + g + 1))
                    if g >= 2:
                        act.wait_ge(S("f_ssq"), n * G + g - 1)
                    act.activation(f_sq[:, g % 2, :], f_hT[:, g % 3, :], ACT.Square).then_inc(S("f_sq"), 1)
                skew([None, None, ln_out(u), gelu, square], G)

            if "F" in PH:
                ffn(0, LN_F0, "F")

            def b_softmax(g):
                if g == 0:
                    act.wait_ge(S("x_sum"), G * PH.index("B"))

                def q_exp(j):
                    n = TG * g + j
                    act.wait_ge(S("b_qsub"), 2 * (n + 1))
                    qt = b_q[:, g % 2, j, :]
                    act.activation(qt, qt, ACT.Exp, scale=QD ** -0.5).then_inc(S("b_qexp"), 1)

                def k_exp(c):
                    n = NC_ * g + c
                    act.wait_ge(S("b_kmax"), n + 1)
                    if n >= 4:
                        act.wait_ge(S("b_kT_mm"), n - 3)
                    if c == 0 and g >= 2:
                        act.wait_ge(S("b_krec"), g - 1)
                    for b in range(NB):
                        act.activation(b_kTe[:, n % 4, b * SEQ:(b + 1) * SEQ], bank("b_k", n)[:, b * SEQ:(b + 1) * SEQ],
                                       ACT.Exp, bias=b_kmax[:, n, b:b + 1], accum_out=b_ksum[:, g % 2, b, c:c + 1])\
                            .then_inc(S("b_kexp"), 1)
                for c in range(NC_):
                    k_exp(c)
                    if c % 2 == 0:
                        q_exp(c // 2)

            def b_fold(g):
                for b in range(NB):
                    n = NB * g + b
                    if n >= 2:
                        act.wait_ge(S("b_g_mm"), n - 1)
                    for half in range(2):
                        act.wait_ge(S("b_m_mm"), 2 * n + half + 1)
                        act.activation(b_m[:, n % 2, 4 * half:4 * half + 4, :].rearrange("p c f -> p (c f)"),
                                       bank("b_m", 2 * n + half), ACT.Copy).then_inc(S("b_m"), 1)

            if "B" in PH:
                skew([None, ln_out(LN_B), b_softmax, None, b_fold], G)
            if "f" in PH:
                ffn(1, LN_F1, "f")

            def c_proj(n):
                if n == 0:
                    act.wait_ge(S("x_sum"), G * PH.index("C"))
                act.wait_ge(S("c_q_mm"), n + 1)
                if n >= 2:
                    act.wait_ge(S("c_l_mm"), 3 * 4 * (n - 1))
                act.activation(c_qT[:, n % 2].rearrange("p a t -> p (a t)"), bank("c_q", n), ACT.Copy).then_inc(S("c_qT"), 1)
                act.wait_ge(S("c_k_mm"), n + 1)
                if n >= 2:
                    act.wait_ge(S("c_km"), n - 1)
                act.activation(c_kT[:, n % 2, :], bank("c_k", n)[:, 0:SEQ], ACT.Copy).then_inc(S("c_kT"), 1)

            def c_heads(n):
                if n == 0:
                    act.wait_ge(S("c_zero"), 8)

                def square(i):
                    m = 4 * n + i
                    if m >= 2:
                        act.wait_ge(S("c_lin_mm"), m - 1)
                    for r in range(2):
                        act.wait_ge(S("c_l_mm"), 3 * m + r + 1)
                        act.activation(c_a0[:, m % 2, 2 * r:2 * r + 2, :].rearrange("p h q -> p (h q)"),
                                       bank("c_l0", 2 * m + r), ACT.Square, bias=ones[:, 0:1], scale=0.5)\
                            .then_inc(S("c_sqr"), 1)
                    act.wait_ge(S("c_l_mm"), 3 * m + 3)
                    act.activation(c_a1[:, m % 2].rearrange("p h q -> p (h q)"), bank("c_l1", m), ACT.Square,
                                   bias=ones[:, 0:1], scale=0.5).then_inc(S("c_sqr"), 1)

                def exp(i):
                    m = 4 * n + i
                    act.wait_ge(S("c_sub"), 3 * m + 1)
                    p0 = c_p0[:, m % 2].rearrange("p h k -> p (h k)")
                    act.activation(p0, p0, ACT.Exp, scale=DC ** -0.5).then_inc(S("c_exp"), 1)
                    act.wait_ge(S("c_sub"), 3 * m + 3)
                    p1 = c_p1[:, m % 2, :, 64:SEQ]
                    act.activation(p1, p1, ACT.Exp, scale=DC ** -0.5).then_inc(S("c_exp"), 1)

                def turn_out(i):
                    m = 4 * n + i
                    if m >= 2:
                        act.wait_ge(S("c_win_mm"), m - 1)
                    for r in range(2):
                        act.wait_ge(S("c_t_mm"), 3 * m + 2 + r)
                        act.activation(c_pT[:, m % 2, 1 + r, :], bank("c_t0", 3 * m + 1 + r), ACT.Copy)\
                            .then_inc(S("c_pT_act"), 1)

                for i in range(5):
                    if i < 4:
                        square(i)
                        exp(i)
                    if i >= 1:
                        turn_out(i - 1)

            def c_out(n):
                act.wait_ge(S("c_cT_mm"), n + 1)
                if n >= 1:
                    act.wait_ge(S("c_y_mm"), n)
                act.activation(c_catT.rearrange("p f t -> p (f t)"), bank("c_cT", n), ACT.Copy)\
                    .then_inc(S("c_catT"), 1)

            if "C" in PH:
                for g in range(G):
                    ln_out(LN_C)(g)
                skew([c_proj, c_heads, c_out], NB * G)

            def moe(n, u, key):
                def up(g):
                    if g == 0:
                        act.wait_ge(S("x_sum"), G * PH.index(key))
                    k = n * G + g
                    act.wait_ge(S("d_g_mm"), k + 1)
                    act.activation(d_e[:, g, :], bank(f"d_g{n}", g)[:, 0:TG * NE], ACT.Exp, scale=-1.0)\
                        .then_inc(S("d_exp"), 1)
                    if g >= 3:
                        act.wait_ge(S("d_y_mm"), k - 2)
                    for c in range(NF):
                        s = d_r2[:, g % 3, NF + c, :]
                        act.wait_ge(S("d_s_mm"), NF * k + c + 1)
                        act.activation(s, bank("d_s", NF * k + c), ACT.Relu).then_inc(S("d_srelu"), 1)
                        act.wait_ge(S("d_srelu"), NF * k + c + 1)
                        act.activation(s, s, ACT.Square).then_inc(S("d_sq"), 1)

                def experts(g):
                    act.wait_ge(S("d_pT_mm"), n * G + g + 1)
                    if g >= 2:
                        act.wait_ge(S("d_b_mm"), NF * (n * G + g - 1))
                    act.activation(d_partsT[0:96, g % 2, :], bank("d_pT", n * G + g).bitcast(BF16)[0:96, 0:TOK],
                                   ACT.Copy).then_inc(S("d_partsT"), 1)
                    for c in range(NF):
                        k = (n * G + g) * NF + c
                        act.wait_ge(S("d_u_mm"), k + 1)
                        if k >= 4:
                            act.wait_ge(S("d_r2"), k - 3)
                        act.activation(d_r[:, k % 4, :], bank("d_u", k), ACT.Relu).then_inc(S("d_relu"), 1)
                skew([None, ln_out(u), up, experts], G)

            if "D" in PH:
                moe(0, LN_D0, "D")

            def e_layer(l):
                def softmax(g):
                    n = l * G + g
                    if n == 0:
                        act.wait_ge(S("x_sum"), G * PH.index("E"))
                    act.wait_ge(S("e_kmax"), n + 1)
                    if n >= 2:
                        act.wait_ge(S("e_kT_mm"), n - 1)
                    if n >= G:
                        act.wait_ge(S("e_krec"), n - G + 1)
                    for b in range(NB):
                        act.activation(e_kTe[:, g % 2, b * SEQ:(b + 1) * SEQ], bank("e_k", n)[:, b * SEQ:(b + 1) * SEQ],
                                       ACT.Exp, bias=e_km[:, g, b:b + 1], accum_out=e_ks[:, g, b:b + 1])\
                            .then_inc(S("e_kexp"), 1)
                    act.wait_ge(S("e_qsub"), n + 1)
                    act.activation(e_qe[:, g % 2, :], e_qe[:, g % 2, :], ACT.Exp).then_inc(S("e_qexp"), 1)
                    act.wait_ge(S("e_v_mm"), n + 1)
                    if n >= 3:
                        act.wait_ge(S("e_c_mm"), n - 2)
                    act.activation(e_v[:, g % 3, :], bank("e_v", n), ACT.Copy).then_inc(S("e_v"), 1)

                def turn_out(g):
                    n = l * G + g
                    act.wait_ge(S("e_qT_mm"), n + 1)
                    if n >= G:
                        act.wait_ge(S("e_y_mm"), n - G + 1)
                    act.activation(e_qT[:, g, :], bank("e_qT", n), ACT.Copy).then_inc(S("e_qT"), 1)

                def slope(g):
                    n = l * G + g
                    if n >= 3:
                        act.wait_ge(S("e_d_mm"), n - 2)
                    for c in range(NF):
                        act.wait_ge(S("e_u_mm"), NF * n + c + 1)
                        act.activation(e_h[:, g % 3, c * TOK:(c + 1) * TOK], bank("e_u", NF * n + c), ACT.Copy,
                                       scale=0.01).then_inc(S("e_hs"), 1)
                u = LN_E + 2 * l
                skew([None, ln_out(u, col(0, l), col(1, l)), softmax, turn_out, None, None, None,
                      None, ln_out(u + 1, col(2, l), col(3, l)), slope], G)

            if "E" in PH:
                for l in range(DEPTH):
                    e_layer(l)
            if "d" in PH:
                moe(1, LN_D1, "d")

        @block.gpsimd
        def _(pool):
            chain = [0]

            def link(ins):
                chain[0] += 1
                ins.then_inc(S("pool_chain"), 1)
                pool.wait_ge(S("pool_chain"), chain[0])

            def select(o, pattern, base, mult, fill, op=ALU.is_ge):
                link(pool.affine_select(out=o, in_=o, pattern=pattern, compare_op=op, fill=fill, base=base,
                                        channel_multiplier=mult))

            link(pool.memset(ident[:, :], 0.0))
            select(ident[:, :], [[-1, P]], 0, 1, 1.0, ALU.not_equal)
            link(pool.memset(ones[:, :], 1.0))
            link(pool.memset(neg_half[:, :], -0.5))
            link(pool.memset(pos_half[:, :], 0.5))
            link(pool.memset(causal_bf, 0.0))
            select(causal_bf[:, 0:P], [[-1, P]], 0, 1, NEG)
            select(causal_bf[:, P:384], [[-1, SEQ]], P, 1, NEG)
            link(pool.memset(window_bf[:, :], 0.0))
            for c0, c1, off in ((0, P, 0), (P, 320, 64)):
                select(window_bf[:, c0:c1], [[-1, c1 - c0]], off, 1, NEG)
                select(window_bf[:, c0:c1], [[1, c1 - c0]], 64 - off, -1, NEG)
            for m, d, nh in ((head8, DC, HC), (head16, DE, HE)):
                link(pool.memset(m[:, :], 1.0))
                select(m[:, :], [[-d, nh]], 0, 1, 0.0)
                select(m[:, :], [[d, nh]], d - 1, -1, 0.0)
            link(pool.memset(lower[:, :, :], 1.0))
            select(lower[:, :, :], [[1, NE], [-1, NE]], -1, 0, 0.0)
            link(pool.memset(gate_sel[:, :, :], 0.0))
            for i in range(3):
                select(gate_sel[:, :, :].rearrange("p c (a m) -> p c a m", a=2), [[-2, NF], [-1, 2], [0, 64]], -32 * i, 1,
                       1.0, ALU.not_equal)
            pool.memset(st[:, 0, :], 0.0).then_inc(S("masks"), 1)

            def rsqrt(u):
                def stage(g):
                    ts = slice(TG * g, TG * g + TG)
                    pool.wait_ge(S("ln_ve"), u * G + g + 1)
                    pool.tensor_tensor(rstd[:, ts], var_eps[:, ts], neg_half[:, :], ALU.pow).then_inc(S("ln_rs"), 1)
                return stage

            if "A" in PH:
                skew([rsqrt(LN_A)], G)

            def ffn(n, u):
                def rms(g):
                    ts = slice(TG * g, TG * g + TG)
                    pool.wait_ge(S("s2_b"), S2[u] * G + g + 1)
                    pool.tensor_tensor(second[:, 2, ts], second[:, 1, ts], pos_half[:, :], ALU.pow).then_inc(S("s2_pow"), 1)

                def rms_h(g):
                    ts = slice(TG * g, TG * g + TG)
                    pool.wait_ge(S("f_ms"), n * G + g + 1)
                    pool.tensor_tensor(f_r[:, 1, ts], f_r[:, 0, ts], pos_half[:, :], ALU.pow).then_inc(S("f_pow"), 1)
                skew([rsqrt(u), rms, None, None, None, rms_h], G)

            if "F" in PH:
                ffn(0, LN_F0)

            def b_bias(g):
                pool.wait_ge(S("ln_xn"), LN_B * G + g + 1)
                xg = x[:, TG * g:TG * g + TG, :]
                pool.tensor_tensor(xg, xg, bout_bc[:, :].unsqueeze(1).to_broadcast([P, TG, P]), ALU.add)\
                    .then_inc(S("b_xb"), 1)

            def b_norm(g):
                for j in range(TG):
                    n = TG * g + j
                    pool.wait_ge(S("b_qrec"), n + 1)
                    qt = b_q[:, g % 2, j, :].rearrange("p (h d) -> p h d", d=QD)
                    pool.tensor_tensor(qt, qt, b_qrec[:, n % 4, :].unsqueeze(2).to_broadcast([P, QH, QD]), ALU.mult)\
                        .then_inc(S("b_qn"), 1)

            if "B" in PH:
                skew([rsqrt(LN_B), b_bias, b_norm], G)
            if "f" in PH:
                ffn(1, LN_F1)

            def c_rms(g):
                ts = slice(TG * g, TG * g + TG)
                pool.wait_ge(S("c_ms"), g + 1)
                pool.tensor_tensor(second[:, 2, ts], second[:, 0, ts], neg_half[:, :], ALU.pow).then_inc(S("s2_pow"), 1)

            def c_residual(g):
                pool.wait_ge(S("c_ln"), g + 1)
                xg = x[:, TG * g:TG * g + TG, :]
                pool.tensor_tensor(xg, xg, z[:, TG * g:TG * g + TG, :], ALU.add).then_inc(S("c_xz"), 1)

            def c_mask(n):
                for i in range(4):
                    m = 4 * n + i
                    for k, (a, need) in enumerate(((c_a0[:, m % 2, :, 0:P], 3 * m + 2), (c_a1[:, m % 2], 3 * m + 3))):
                        pool.wait_ge(S("c_sqr"), need)
                        pool.affine_select(out=a, in_=a, pattern=[[0, 4], [1, P]], compare_op=ALU.is_ge, fill=0.0,
                                           base=0, channel_multiplier=-1).then_inc(S("c_mask"), 1)

            if "C" in PH:
                pool.wait_ge(S("x_sum"), G * PH.index("C"))
                for i in range(4):
                    pool.memset(c_vm[:, i], 0.0).then_inc(S("c_clear"), 1)
                pool.wait_ge(S("c_clear"), 4)
                for i in range(4):
                    pool.memset(own_sums(i), 1.0).then_inc(S("c_zero"), 1)
                for i in range(2):
                    pool.memset(c_p1[:, i, :, 0:64], 0.0).then_inc(S("c_zero"), 1)
                    pool.memset(c_max[:, i, :], 0.0).then_inc(S("c_zero"), 1)
                skew([rsqrt(LN_C), c_rms, c_residual], G)
                for n in range(NB * G):
                    c_mask(n)
            if "D" in PH:
                skew([rsqrt(LN_D0)], G)

            def e_layer(l):
                def bias(g):
                    pool.wait_ge(S("ln_xn"), turned(LN_E + 2 * l) * G + g + 1)
                    zg = z[:, TG * g:TG * g + TG, :]
                    pool.tensor_tensor(zg, zg, bo_bc[:, l, :].unsqueeze(1).to_broadcast([P, TG, P]), ALU.add)\
                        .then_inc(S("e_zb"), 1)
                skew([rsqrt(LN_E + 2 * l), bias, None, None, None, None, None, rsqrt(LN_E + 2 * l + 1)], G)

            if "E" in PH:
                pool.wait_ge(S("e_bo_in"), 16)
                skew([rsqrt(LN_Z)], G)
                for l in range(DEPTH):
                    e_layer(l)
            if "d" in PH:
                skew([rsqrt(LN_D1)], G)


PREP_OUT = [1, 3, 4, 5, 6, 7, 9, 10, 11, 12, 13, 15, 16, 17, 18, 19]
S2 = {1: 0, 3: 1, 4: 2}
LN_PH = {1: 0, 2: 1, 3: 2, 4: 3, 5: 4, 6: 5, 19: 6}
ROUTE = 30
PHASES = "AFBfCDEd"

_INS = ['L0_attn_a_x', 'L0_attn_a_W_query', 'L0_attn_a_W_key', 'L0_attn_a_W_value', 'L0_attn_b_Wqkv', 'L0_attn_b_Wout',
        'L0_attn_b_bout', 'L0_ffn_w_up', 'L0_ffn_w_down', 'L1_attn_a_norm_w', 'L1_attn_a_Wq', 'L1_attn_a_Wk',
        'L1_attn_a_Wv', 'L1_attn_a_Wqf', 'L1_attn_a_Wkf', 'L1_attn_a_Wout', 'L1_attn_b_ln1_w', 'L1_attn_b_ln1_b',
        'L1_attn_b_wq', 'L1_attn_b_wk', 'L1_attn_b_wv', 'L1_attn_b_wo', 'L1_attn_b_bo', 'L1_attn_b_ln2_w',
        'L1_attn_b_ln2_b', 'L1_attn_b_w1', 'L1_attn_b_w2', 'L1_ffn_gate', 'L1_ffn_corr_bias', 'L1_ffn_w1', 'L1_ffn_w2',
        'L1_ffn_fc1_w', 'L1_ffn_fc2_w', 'L1_ffn_up_w', 'L1_ffn_down_w']


def kernel(**inputs):
    import numpy as _np
    import concourse.bacc as _bacc
    from concourse.bass_utils import run_bass_kernel_spmd as _run

    nc = _bacc.Bacc("TRN2", target_bir_lowering=False, num_devices=1)
    arrays, args = {}, {}
    for name in _INS:
        a = _np.ascontiguousarray(inputs[name])
        arrays[f"in_{name}"] = a
        args[name] = nc.dram_tensor(f"in_{name}", a.shape, mybir.dt.from_np(a.dtype), kind="ExternalInput").ap()
    out = nc.dram_tensor("out", inputs['L0_attn_a_x'].shape, F32, kind="ExternalOutput").ap()
    hybrid_program(nc, args, out)
    r = _run(nc, [arrays], core_ids=[0])
    return r.results[0]["out"]
```

```python
from contextlib import ExitStack

import concourse.bass as bass
from concourse import mybir

F32 = mybir.dt.float32
BF16 = mybir.dt.bfloat16
F32R = mybir.dt.float32r
ALU = mybir.AluOpType
ACT = mybir.ActivationFunctionType
X = mybir.AxisListType.X

P = 128
SEQ = 256
NEG = -1.0e30


def in_turn(*steps):
    def stage(g):
        if steps[g] is not None:
            steps[g]()
    return stage


def pipeline(phases, n):
    stages, base, before = [], 0, 1
    for key, own in phases:
        steps, lag, at = STEPS[key]
        base += max(0, before - lag) * (n - 1)
        before = lag
        stages += sorted(((base + at[name], lag, stage) for name, stage in own.items()), key=lambda s: s[0])
        base += steps
    for t in range(base + before * (n - 1)):
        for start, lag, stage in stages:
            g, late = divmod(t - start, lag)
            if late == 0 and 0 <= g < n:
                stage(g)


def hybrid_program(nc, w, out):
    x_dram = w["L0_attn_a_x"].rearrange("b (t p) d -> p (b t) d", p=P)
    out_dram = out.rearrange("b (t p) d -> p (b t) d", p=P)
    NT = x_dram.shape[1]
    TG = 4
    G = NT // TG
    TOK = TG * P
    NB = TG * P // SEQ
    DEPTH = w["L1_attn_b_wq"].shape[0]
    QH, QD = 16, 64
    INNER = QH * QD
    NC_ = INNER // P
    HC, DC = 16, 8
    HE, DE = 8, 16
    NE = w["L1_ffn_gate"].shape[0]
    FF = 512
    NF = FF // P
    VA = P + HC

    with ExitStack() as ctx:
        def sb(name, shape, dt=F32):
            return ctx.enter_context(nc.sbuf_tensor(name, shape, dt))

        x = sb("x", [P, NT, P])
        z = sb("z", [P, NT, P])
        xn = sb("xn", [P, NT, P])
        xnT = sb("xnT", [P, G, TOK])
        st = sb("st", [P, NT, 6])
        mv = sb("mv", [P, NT, 2])
        var_eps = sb("var_eps", [P, NT])
        rstd = sb("rstd", [P, NT])
        second = sb("second", [P, 3, NT])
        neg_half = sb("neg_half", [P, TG])
        pos_half = sb("pos_half", [P, TG])

        ident = sb("ident", [P, P])
        ident_bf = sb("ident_bf", [P, P], BF16)
        ones = sb("ones", [P, P])
        window_bf = sb("window_bf", [P, P + 192], BF16)
        head8 = sb("head8", [P, HC])
        head16 = sb("head16", [P, HE])
        bd16 = sb("bd16", [P, HE, DE])
        lower = sb("lower", [P, NE, NE])
        a_w = sb("a_w", [P, 2 * P])
        wupT = sb("wupT", [P, FF])
        wdnT = sb("wdnT", [P, NF, P])
        bout_bc = sb("bout_bc", [P, P])
        c_w = sb("c_w", [P, 4, P])
        wout_c = sb("wout_c", [P, 2, P])
        cols = sb("cols", [P, 25])
        gateT = sb("gateT", [P, NE])
        bias_bc = sb("bias_bc", [P, NE])
        gate_sel = sb("gate_sel", [P, NF, P], BF16)
        moe_up = sb("moe_up", [P, 2 * FF])
        moe_dn = sb("moe_dn", [P, 2 * NF, P])
        e_w4 = [sb(f"e_w4_{i}", [P, 4, P]) for i in range(2)]
        e_w1 = [sb(f"e_w1_{i}", [P, FF]) for i in range(2)]
        e_w2 = [sb(f"e_w2_{i}", [P, NF, P]) for i in range(2)]
        bo_bc = sb("bo_bc", [P, DEPTH, P])

        ARENA = 30436
        ROUNDED = HC * SEQ * 2 + 2 * 3 * SEQ
        with ExitStack() as shared:
            wqkv = shared.enter_context(nc.sbuf_tensor("wqkv", [P, 3 * INNER], F32))
            wvT = shared.enter_context(nc.sbuf_tensor("wvT", [P, NC_, P], F32))
            wout_b = shared.enter_context(nc.sbuf_tensor("wout_b", [P, NC_, P], F32))
            arena = shared.enter_context(nc.sbuf_tensor("arena", [P, ARENA], F32))
        rounded = sb("rounded", [P, 3 * INNER + 2 * NC_ * P + ROUNDED], F32R)

        PREP = 7500
        FFN = 3 * NF * TOK + 2 * NF * TOK + 2 * TOK + 3 * NT

        def carve(start=0):
            used = [start]

            def take(*dims):
                n = 1
                for d in dims:
                    n *= d
                a = arena[:, used[0]:used[0] + n]
                used[0] += n
                assert used[0] <= ARENA, used
                if len(dims) == 1:
                    return a
                names = "abcd"[:len(dims)]
                return a.rearrange(f"p ({' '.join(names)}) -> p {' '.join(names)}",
                                   **{c: d for c, d in zip(names[1:], dims[1:])})
            return take

        ps = ctx.enter_context(nc.psum_tensor("ps", [P, 8, 512], F32))
        sems = {}

        def S(name):
            if name not in sems:
                sems[name] = ctx.enter_context(nc.semaphore(name))
            return sems[name]

        ring = {"next": 0, "banks": list(range(8))}
        freed_by = {}
        where = {}

        def claim(pe, name, idx, sem, value):
            b = ring["banks"][ring["next"] % len(ring["banks"])]
            ring["next"] += 1
            if b in freed_by:
                pe.wait_ge(*freed_by[b])
            freed_by[b] = (S(sem), value)
            where[(name, idx)] = b
            return ps[:, b, :]

        def bank(name, idx):
            return ps[:, where[(name, idx)], :]

        def tiles(g):
            return range(TG * g, TG * g + TG)

        block = ctx.enter_context(nc.Block())

        take = carve()
        bd8 = take(HC, DC)
        s_aw = take(3, P)
        s_up0 = take(NF, P)
        s_dn0 = take(FF)
        s_gate = take(P)
        s_w1 = take(4, 64)
        s_w2 = take(8, 64)
        s_fc1 = take(P)
        s_fc2 = take(64)
        s_upw = take(NF, P)
        s_dnw = take(FF)
        s_cf = take(2, 16)
        s_rows = take(P)
        s_absum = take(2)
        s_thr = take(4)
        s_tern = take(2, FF)
        s_wt = take(2, FF)
        s_cfT = take(2, P)
        s_bd = take(P)
        s_wqT = take(P)
        s_w1T = take(FF)
        s_fc2T = take(P)

        causal_bf = arena[:, ARENA - 192:ARENA].bitcast(BF16)

        take = carve(PREP + FFN)
        a_uT = take(2, TOK)
        a_v = take(4, TG, P)
        a_p = take(2, NB, 384)
        a_pT = take(2, NB, 384)
        a_nmax = take(2, NT)
        a_sum = take(2, NT)

        f_hT, f_sq, f_ssq, f_r = [], [], [], []
        for at in (PREP, 0):
            take = carve(at)
            f_hT.append(take(3, NF * TOK))
            f_sq.append(take(2, NF * TOK))
            f_ssq.append(take(2, TOK))
            f_r.append(take(3, NT))

        take = carve()
        b_q = take(2, TG, INNER)
        b_k = take(2, TG, INNER)
        b_kTe = take(4, TOK)
        b_ctx = take(4, NC_, P)
        b_m = take(2, NC_, P)
        b_g = take(4, P)
        b_qmax = take(4, QH)
        b_qsum = take(4, QH)
        b_qrec = take(4, QH)
        b_kmax = take(NC_ * 4, NB)
        b_ksum = take(2, NB, NC_)
        b_krec = take(2, NB, NC_)

        take = carve()
        take(ROUNDED)
        c_pT = take(2, 3, 512)
        c_p1 = take(2, 4, SEQ)
        c_vm = take(4, HC * (VA + DC + 1))
        c_p0 = take(2, 4, P)
        c_a0 = take(2, 4, SEQ)
        c_a1 = take(2, 4, P)
        c_max = take(4, 8)
        c_rec = take(4, 2, HC)
        c_cat = take(2, 2, SEQ)
        c_catT = take(2, SEQ)

        cuts = [0, 3 * INNER, 3 * INNER + NC_ * P, 3 * INNER + 2 * NC_ * P]
        c_spread = rounded[:, cuts[0]:cuts[1]].rearrange("p (r t) -> p r t", t=2 * SEQ)
        pick_q = rounded[:, cuts[1]:cuts[2]].rearrange("p (a b) -> p a b", a=2)
        pick_k = rounded[:, cuts[2]:cuts[3]].rearrange("p (a b) -> p a b", a=2)
        c_km = rounded[:, cuts[3]:cuts[3] + 2 * HC * SEQ].rearrange("p (r h t) -> p r h t", r=2, h=HC)
        c_split = rounded[:, cuts[3] + 2 * HC * SEQ:cuts[3] + ROUNDED].rearrange("p (a t) -> p a t", a=2)
        quarter = a_w[:, 0:4]

        take = carve()
        d_r2 = take(3, 2 * NF, TOK)
        d_r = take(4, TOK)
        d_sc = take(G, 2, TG * NE)
        d_e = take(G, TG * NE)
        d_sfc = take(G, TG * NE)
        d_top = take(G, 8, TG * 2)
        d_cmp = take(2, 2, TG * NE * NE)
        d_rank = take(G, TG * NE)
        d_w = take(G, TG * NE)
        d_den = take(G, 2, TG)
        d_gate = take(G, TG * NE)
        d_rest = take(2, 2, TG * NE)
        d_parts = take(2, TG * 96 // 2).bitcast(BF16).rearrange("p r (t k) -> p r t k", k=96)
        d_partsT = take(2, TOK // 2).bitcast(BF16)

        take = carve()
        e_qe = take(2, TOK)
        e_qm = take(G, 3, TG * HE)
        e_qT = take(4, TOK)
        e_kTe = take(2, TOK)
        e_km = take(G, NB)
        e_ks = take(G, NB)
        e_kr = take(G, NB)
        e_k = take(2, TOK)
        e_v = take(3, TOK)
        e_ctx = take(2, NB, P)
        e_m = take(2, NB, P)
        e_h = take(3, NF * TOK)

        def value_blocks(i):
            return c_vm[:, i, 0:HC * VA].rearrange("p (h v) -> p h v", v=VA)

        def own_columns(i):
            return c_vm[:, i, 0:HC * (VA + DC)].rearrange("p (h v) -> p h v", v=VA + DC)[:, :, 0:DC]

        def own_sums(i):
            return c_vm[:, i, P:P + HC * (VA + 1)].rearrange("p (h v) -> p h v", v=VA + 1)[:, :, 0:1]

        WQP, WQ, WK, WV = range(4)

        def col(kind, l):
            c = kind * DEPTH + l
            return cols[:, c:c + 1]

        A_IN, F_IN, B_IN, C_IN, D_IN, E_IN = 3 * 16, 2 * 16, 3 * 16, (4 + 2 * HC + 5) * 16, 8 * 16, 6 * 16
        LN_A, LN_F0, LN_B, LN_F1, LN_C, LN_D0, LN_Z, LN_E = 0, 1, 2, 3, 4, 5, 6, 7
        LN_D1 = LN_E + 2 * DEPTH

        def ln_name_value(name, u, g):
            if u == LN_Z:
                return name + "_z", g + 1
            if LN_E < u < LN_D1 and (u - LN_E) % 2 == 1:
                return name + "_second", (u - LN_E) // 2 * G + g + 1
            n = u if u < LN_Z else LN_Z + (u - LN_E) // 2
            return name, n * G + g + 1

        def ln(name, u, g):
            name, value = ln_name_value(name, u, g)
            return S(name), value

        def by_sequence(start, heads, finish, opened=None):
            N = NB * G

            def steps(n):
                if n < N and start is not None:
                    start(n)
                if n == 1 and opened is not None:
                    opened()
                if n >= 1:
                    heads(n - 1)

            def group(g):
                for n in range(NB * g, NB * g + NB):
                    steps(n)

            def tail(g):
                if g == G - 1:
                    steps(N)
                    if finish is not None:
                        finish()
            return {"sequences": group, "last": tail}

        PH = PHASES
        LAST = len(PH) - 1

        @block.sync
        def _(sp):
            def load(dst, src, name):
                sp.dma_start(dst, src).then_inc(S(name), 16)

            for g in range(G):
                load(x[:, TG * g:TG * g + TG, :], x_dram[:, TG * g:TG * g + TG, :], f"x_in{g}")
                if g == 0:
                    for i, n in enumerate(("W_query", "W_key", "W_value")):
                        load(s_aw[:, i, :], w[f"L0_attn_a_{n}"], "a_in")
            load(s_up0, w["L0_ffn_w_up"].rearrange("(c p) d -> p c d", p=P), "f_in")
            load(s_dn0, w["L0_ffn_w_down"], "f_in")
            load(wqkv[:, :], w["L0_attn_b_Wqkv"], "b_in")
            load(wout_b[:, :, :], w["L0_attn_b_Wout"].rearrange("(c p) f -> p c f", p=P), "b_in")
            load(bout_bc[:, :], w["L0_attn_b_bout"].rearrange("(a d) -> a d", a=1).broadcast_to([P, P]), "b_in")
            load(c_w[:, WQ, :], w["L1_attn_a_Wq"], "c_in")
            load(c_w[:, WK, :], w["L1_attn_a_Wk"], "c_in")
            load(c_w[:, WV, :], w["L1_attn_a_Wv"], "c_in")
            load(wout_c[:, :, :], w["L1_attn_a_Wout"].rearrange("(c p) f -> p c f", p=P), "c_in")
            for i, n in enumerate(("Wqf", "Wkf")):
                for h in range(HC):
                    load(s_cf[h * DC:(h + 1) * DC, i, :], w[f"L1_attn_a_{n}"], "c_in")
            for i, n in enumerate(("ln1_w", "ln1_b", "ln2_w", "ln2_b")):
                load(s_rows[i * DEPTH:(i + 1) * DEPTH, :], w[f"L1_attn_b_{n}"], "c_in")
            load(s_rows[4 * DEPTH:4 * DEPTH + 1, :], w["L1_attn_a_norm_w"].rearrange("(a d) -> a d", a=1), "c_in")
            load(s_gate[0:NE, :], w["L1_ffn_gate"], "d_in")
            load(s_w1, w["L1_ffn_w1"].rearrange("e i l -> (e i) l").rearrange("(c p) l -> p c l", p=P), "d_in")
            load(s_w2[0:64, :, :], w["L1_ffn_w2"].rearrange("e l i -> l e i"), "d_in")
            load(s_fc1[0:64, :], w["L1_ffn_fc1_w"], "d_in")
            load(s_fc2, w["L1_ffn_fc2_w"], "d_in")
            load(s_upw, w["L1_ffn_up_w"].rearrange("(c p) d -> p c d", p=P), "d_in")
            load(s_dnw, w["L1_ffn_down_w"], "d_in")
            load(bias_bc[:, :], w["L1_ffn_corr_bias"].rearrange("(a d) -> a d", a=1).broadcast_to([P, NE]), "d_in")
            load(bo_bc[:, :, :], w["L1_attn_b_bo"].rearrange("(a l) d -> a l d", a=1).broadcast_to([P, DEPTH, P]), "e_bo_in")
            for l in range(DEPTH if "E" in PH else 0):
                if l >= 2:
                    sp.wait_ge(S("e_z2"), (l - 1) * G)
                for i, n in enumerate(("wq", "wk", "wv", "wo")):
                    load(e_w4[l % 2][:, i, :], w[f"L1_attn_b_{n}"][l], f"e_in{l % 2}")
                load(e_w1[l % 2][:, :], w["L1_attn_b_w1"][l], f"e_in{l % 2}")
                load(e_w2[l % 2][:, :, :], w["L1_attn_b_w2"][l].rearrange("(c p) f -> p c f", p=P), f"e_in{l % 2}")
            for g in range(G):
                sp.wait_ge(S("x_sum"), LAST * G + g + 1)
                sp.dma_start(out_dram[:, TG * g:TG * g + TG, :], x[:, TG * g:TG * g + TG, :]).then_inc(S("stored"), 16)
            sp.wait_ge(S("stored"), 16 * G)

        @block.tensor
        def _(pe):
            stages = []

            def phase(key, **own):
                stages.append((key, own))

            def mm(o, lhsT, rhs, start=True, stop=True):
                return pe.matmul(o, lhsT, rhs, start=start, stop=stop, skip_group_check=True)

            pe.wait_ge(S("masks"), 1)
            prep = [0]

            def prep_bank():
                prep[0] += 1
                return claim(pe, "prep", prep[0] - 1, "prep_out", PREP_OUT[prep[0] - 1])

            def prepare_query_key():
                pe.wait_ge(S("a_in"), A_IN)
                o = prep_bank()
                mm(o[:, 0:P], s_aw[:, 0, :], s_aw[:, 1, :])
                pe.transpose(o[:, P:2 * P], s_aw[:, 2, :], ident[:, :]).then_inc(S("prep_mm"), 1)

            def prepare_threshold():
                o = prep_bank()
                pe.wait_ge(S("f_abs"), 2)
                mm(o[:, 0:2], ones[:, :], s_absum).then_inc(S("prep_mm"), 1)

            def prepare_ternary():
                pe.wait_ge(S("f_tern"), 2)
                for i in range(2):
                    o = prep_bank()
                    for c in range(NF):
                        last = pe.transpose(o[:, c * P:(c + 1) * P], s_wt[:, i, c * P:(c + 1) * P], ident[:, :])
                    last.then_inc(S("prep_mm"), 1)

            def prepare_values_b():
                pe.wait_ge(S("b_in"), B_IN)
                for i in range(2):
                    o = prep_bank()
                    for c in range(4):
                        v0 = 2 * INNER + (4 * i + c) * P
                        last = pe.transpose(o[:, c * P:(c + 1) * P], wqkv[:, v0:v0 + P], ident[:, :])
                    last.then_inc(S("prep_mm"), 1)

            def prepare_features():
                pe.wait_ge(S("c_in"), C_IN)
                o = prep_bank()
                pe.transpose(o[0:16, 0:P], s_cf[:, 0, :], ident[:, :])
                pe.transpose(o[0:16, P:2 * P], s_cf[:, 1, :], ident[:, :])
                pe.transpose(o[:, 2 * P:2 * P + 25], s_rows[0:25, :], ident[0:25, 0:25]).then_inc(S("prep_mm"), 1)
                o = prep_bank()
                pe.wait_ge(S("prep_out"), PREP_OUT[6])
                mm(o[:, 0:P], s_cfT[0:16, 0, :], s_cfT[0:16, 1, :]).then_inc(S("prep_mm"), 1)

            def prepare_query_c():
                o = prep_bank()
                pe.wait_ge(S("c_scaled"), 3)
                pe.transpose(o[:, 0:P], c_w[:, WQ, :], ident[:, :]).then_inc(S("prep_mm"), 1)
                o = prep_bank()
                pe.wait_ge(S("prep_out"), PREP_OUT[8])
                mm(o[:, 0:P], s_wqT, s_bd).then_inc(S("prep_mm"), 1)

            def prepare_experts():
                pe.wait_ge(S("d_in"), D_IN)
                o = prep_bank()
                for c in range(4):
                    last = pe.transpose(o[0:64, c * P:(c + 1) * P], s_w1[:, c, :], ident[:, :])
                last.then_inc(S("prep_mm"), 1)
                o = prep_bank()
                pe.transpose(o[0:64, 0:P], s_fc2, ident[:, :])
                pe.transpose(o[:, P:P + NE], s_gate[0:NE, :], ident[0:NE, 0:NE]).then_inc(S("prep_mm"), 1)
                o = prep_bank()
                pe.wait_ge(S("prep_out"), PREP_OUT[11])
                mm(o, s_fc1[0:64, :], s_w1T[0:64, :]).then_inc(S("prep_mm"), 1)

            def prepare_shared():
                o = prep_bank()
                for c in range(NF):
                    last = pe.transpose(o[:, c * P:(c + 1) * P], s_upw[:, c, :], ident[:, :])
                last.then_inc(S("prep_mm"), 1)
                o = prep_bank()
                w2f = s_w2.rearrange("p e i -> p (e i)")
                for c in range(NF):
                    last = mm(o[:, c * P:(c + 1) * P], w2f[0:64, c * P:(c + 1) * P], s_fc2T[0:64, :])
                last.then_inc(S("prep_mm"), 1)
                o = prep_bank()
                for c in range(NF):
                    last = pe.transpose(o[:, c * P:(c + 1) * P], s_dnw[:, c * P:(c + 1) * P], ident[:, :])
                last.then_inc(S("prep_mm"), 1)

            prepare_query_key()

            def ln_transpose(u):
                def stage(g):
                    o = claim(pe, f"ln{u}", g, *ln_name_value("ln_xT", u, g))
                    pe.wait_ge(*ln("ln_xn", u, g))
                    for j, t in enumerate(tiles(g)):
                        last = pe.transpose(o[:, j * P:(j + 1) * P], xn[:, t, :], ident[:, :])
                    last.then_inc(ln("ln_T", u, g)[0], 1)
                return stage

            def a_proj(g):
                o = claim(pe, "a_u", g, "a_uT", g + 1)
                pe.wait_ge(*ln("ln_xT", LN_A, g))
                if g == 0:
                    pe.wait_ge(S("prep_out"), PREP_OUT[0])
                mm(o, a_w[:, 0:P], xnT[:, g, :]).then_inc(S("a_u_mm"), 1)
                o = claim(pe, "a_v", g, "a_v", g + 1)
                for j in range(TG):
                    last = mm(o[:, j * P:(j + 1) * P], xnT[:, g, j * P:(j + 1) * P], a_w[:, P:2 * P])
                last.then_inc(S("a_v_mm"), 1)

            def a_scores(g):
                for b in range(NB):
                    o = claim(pe, "a_s", NB * g + b, "a_exp", TG * g + 2 * b + 2)
                    mm(o[:, 0:384], ident_bf[:, :], causal_bf, True, False)
                    if b == 0:
                        pe.wait_ge(S("a_uT"), g + 1)
                    q0 = b * SEQ
                    mm(o[:, 0:P], a_uT[:, g % 2, q0:q0 + P], xnT[:, g, q0:q0 + P], False, False)
                    mm(o[:, P:384], a_uT[:, g % 2, q0 + P:q0 + SEQ], xnT[:, g, q0:q0 + SEQ],
                       False, True).then_inc(S("a_s_mm"), 1)

            def a_ptrans(g):
                for b in range(NB):
                    o = claim(pe, "a_pT", NB * g + b, f"a_pT{b}", g + 1)
                    pe.wait_ge(S("a_exp"), TG * g + 2 * b + 2)
                    for c in range(3):
                        last = pe.transpose(o[:, c * P:(c + 1) * P], a_p[:, g % 2, b, c * P:(c + 1) * P], ident[:, :])
                    last.then_inc(S("a_pT_mm"), 1)

            def a_out(g):
                o = claim(pe, "a_o", g, "x_sum", G * PH.index("A") + g + 1)
                pe.wait_ge(S("a_v"), g + 1)
                for b in range(NB):
                    pe.wait_ge(S(f"a_pT{b}"), g + 1)
                    v0, v1 = a_v[:, g, 2 * b, :], a_v[:, g, 2 * b + 1, :]
                    pT = a_pT[:, g % 2, b, :]
                    mm(o[:, 2 * b * P:(2 * b + 1) * P], pT[:, 0:P], v0)
                    mm(o[:, (2 * b + 1) * P:(2 * b + 2) * P], pT[:, P:2 * P], v0, True, False)
                    last = mm(o[:, (2 * b + 1) * P:(2 * b + 2) * P], pT[:, 2 * P:3 * P], v1, False, True)
                last.then_inc(S("a_o_mm"), 1)

            if "A" in PH:
                phase("A", prepare=in_turn(prepare_threshold, prepare_ternary, prepare_values_b, prepare_features), turn=ln_transpose(LN_A), project=a_proj, scores=a_scores, turn_p=a_ptrans, out=a_out)

            def ffn(n, u, key):
                def up(g):
                    for c in range(NF):
                        o = claim(pe, f"f_h{n}", NF * g + c, "f_gelu", n * NF * G + NF * g + c + 1)
                        if c == 0:
                            pe.wait_ge(*ln("ln_xT", u, g))
                            pe.wait_ge(S("prep_out"), PREP_OUT[3])
                        mm(o, wupT[:, c * P:(c + 1) * P], xnT[:, g, :]).then_inc(S("f_h_mm"), 1)

                def down(g):
                    o = claim(pe, f"f_ss{n}", g, "f_ms", n * G + g + 1)
                    pe.wait_ge(S("f_ssq"), n * G + g + 1)
                    for j in range(TG):
                        last = mm(o[:, j:j + 1], f_ssq[n][:, g % 2, j * P:(j + 1) * P], ones[:, 0:1])
                    last.then_inc(S("f_ss_mm"), 1)
                    o = claim(pe, f"f_y{n}", g, "x_sum", G * PH.index(key) + g + 1)
                    for j in range(TG):
                        for c in range(NF):
                            h0 = c * TOK + j * P
                            last = mm(o[:, j * P:(j + 1) * P], f_hT[n][:, g % 3, h0:h0 + P], wdnT[:, c, :],
                                      c == 0, c == NF - 1)
                    last.then_inc(S("f_y_mm"), 1)
                own = {"prepare": in_turn(prepare_query_c, prepare_experts, prepare_shared, None)} if n == 0 else {}
                phase("F", turn=ln_transpose(u), up=up, down=down, **own)

            if "F" in PH:
                ffn(0, LN_F0, "F")

            def b_qk(g):
                pe.wait_ge(*ln("ln_xT", LN_B, g))

                def q_tile(j):
                    for half in range(2):
                        o = claim(pe, "b_q", (TG * g + j) * 2 + half, "b_qsub", (TG * g + j) * 2 + half + 1)
                        mm(o, xnT[:, g, j * P:(j + 1) * P], wqkv[:, half * 512:half * 512 + 512]).then_inc(S("b_q_mm"), 1)

                def k_chunk(c):
                    n = NC_ * g + c
                    o = claim(pe, "b_k", n, "b_kexp", NB * (n + 1))
                    mm(o, wqkv[:, INNER + c * P:INNER + (c + 1) * P], xnT[:, g, :]).then_inc(S("b_k_mm"), 1)

                def k_turn(c):
                    n = NC_ * g + c
                    o = claim(pe, "b_kT", n, "b_k", n + 1)
                    pe.wait_ge(S("b_kexp"), NB * (n + 1))
                    for j in range(TG):
                        last = pe.transpose(o[:, j * P:(j + 1) * P], b_kTe[:, n % 4, j * P:(j + 1) * P], ident[:, :])
                    last.then_inc(S("b_kT_mm"), 1)

                for c in range(NC_ + 2):
                    if c < NC_:
                        k_chunk(c)
                        if c % 2 == 0:
                            q_tile(c // 2)
                    if c >= 2:
                        k_turn(c - 2)

            def b_context(g):
                for b in range(NB):
                    for half in range(2):
                        o = claim(pe, "b_c", (NB * g + b) * 2 + half, "b_ctx", (NB * g + b) * 4 + 2 * half + 2)
                        if b == 0 and half == 0:
                            pe.wait_ge(S("b_k"), NC_ * (g + 1))
                            pe.wait_ge(S("b_qn"), TG * (g + 1))
                        for c in range(4):
                            cc = (4 * half + c) * P
                            for s in range(2):
                                j = 2 * b + s
                                last = mm(o[:, c * P:(c + 1) * P], b_k[:, g % 2, j, cc:cc + P],
                                          b_q[:, g % 2, j, cc:cc + P], s == 0, s == 1)
                        last.then_inc(S("b_c_mm"), 1)

            def b_fold(g):
                for b in range(NB):
                    n = NB * g + b
                    for half in range(2):
                        o = claim(pe, "b_m", 2 * n + half, "b_m", 2 * n + half + 1)
                        pe.wait_ge(S("b_ctx"), 4 * n + 2 * half + 2)
                        for c in range(4):
                            cc = 4 * half + c
                            last = mm(o[:, c * P:(c + 1) * P], b_ctx[:, n % 4, cc, :], wout_b[:, cc, :])
                        last.then_inc(S("b_m_mm"), 1)
                for b in range(NB):
                    n = NB * g + b
                    o = claim(pe, "b_g", n, "b_g", n + 1)
                    pe.wait_ge(S("b_m"), 2 * n + 2)
                    for c in range(NC_):
                        last = mm(o[:, 0:P], wvT[:, c, :], b_m[:, n % 2, c, :], c == 0, c == NC_ - 1)
                    last.then_inc(S("b_g_mm"), 1)

            def b_out(g):
                o = claim(pe, "b_y", g, "x_sum", G * PH.index("B") + g + 1)
                pe.wait_ge(S("b_g"), NB * (g + 1))
                for j in range(TG):
                    last = mm(o[:, j * P:(j + 1) * P], xnT[:, g, j * P:(j + 1) * P], b_g[:, (NB * g + j // 2) % 4, :])
                last.then_inc(S("b_y_mm"), 1)

            if "B" in PH:
                phase("B", turn=ln_transpose(LN_B), heads=b_qk, context=b_context, fold=b_fold, out=b_out)
            if "f" in PH:
                ffn(1, LN_F1, "f")

            def c_proj(n):
                g, s0 = n // NB, (n % NB) * SEQ
                o = claim(pe, "c_q", n, "c_low", 2 * n + 1)
                pe.wait_ge(*ln("ln_xT", LN_C, g))
                mm(o[:, 0:SEQ], c_w[:, WQP, :], xnT[:, g, s0:s0 + SEQ])
                mm(o[:, SEQ:2 * SEQ], c_w[:, WQ, :], xnT[:, g, s0:s0 + SEQ]).then_inc(S("c_q_mm"), 1)
                o = claim(pe, "c_k", n, "c_low", 2 * n + 2)
                mm(o[:, 0:SEQ], c_w[:, WK, :], xnT[:, g, s0:s0 + SEQ]).then_inc(S("c_k_mm"), 1)
                if n == 0:
                    c_values(n)
                if n == 0:
                    for i in range(4):
                        c_spread_out(n, i)

            def c_values(n):
                g, s0 = n // NB, (n % NB) * SEQ
                o = claim(pe, "c_v", n, "c_vm", n + 1)
                for s in range(2):
                    last = mm(o[:, s * P:(s + 1) * P], xnT[:, g, s0 + s * P:s0 + (s + 1) * P], c_w[:, WV, :])
                last.then_inc(S("c_v_mm"), 1)


            def c_spread_out(n, i):
                m = 4 * n + i
                if m == 0:
                    pe.wait_ge(S("c_pick"), 5)
                for name, pick, cols_, freed in (("c_qs", pick_q, slice(0, 2 * SEQ), "c_spread"),
                                                 ("c_ks", pick_k, slice(2 * SEQ, 3 * SEQ), "c_km")):
                    o = claim(pe, name, m, freed, m + 1)[:, 0:cols_.stop - cols_.start]
                    if i == 0:
                        pe.wait_ge(S("c_low"), 2 * n + (1 if name == "c_qs" else 2))
                    for part in range(2):
                        last = mm(o, pick[:, part, i * P:(i + 1) * P],
                                  c_split[:, part, cols_], part == 0, part == 1)
                    last.then_inc(S("c_spread_mm"), 1)

            def c_heads(n):
                km = c_km[:, n % 2]

                def window_scores(i):
                    m = 4 * n + i
                    h0 = 4 * i
                    q = c_spread[:, m % 6, SEQ:2 * SEQ]
                    pe.wait_ge(S("c_km"), m + 1)
                    pe.wait_ge(S("c_spread"), m + 1)
                    o = claim(pe, "c_s0", m, "c_sub", 3 * m + 1)
                    mm(o, ident_bf[:, :], window_bf[:, 0:P].unsqueeze(1).to_broadcast([P, 4, P]), True, False)
                    mm(o, q[:, 0:P], km[:, h0:h0 + 4, 0:P], False, True).then_inc(S("c_s_mm"), 1)
                    for r in range(2):
                        o = claim(pe, "c_s1", 2 * m + r, "c_sub", 3 * m + 2 + r)
                        mm(o[:, 0:384], ident_bf[:, :], window_bf[:, P:320].unsqueeze(1).to_broadcast([P, 2, 192]), True, False)
                        mm(o[:, 0:384], q[:, P:SEQ], km[:, h0 + 2 * r:h0 + 2 * r + 2, 64:SEQ], False, True)\
                            .then_inc(S("c_s_mm"), 1)

                def linear_scores(i):
                    m = 4 * n + i
                    h0 = 4 * i
                    qp = c_spread[:, m % 6, 0:SEQ]
                    for r in range(2):
                        o = claim(pe, "c_l0", 2 * m + r, "c_sqr", 4 * m + 1 + r)
                        for k in range(2):
                            last = mm(o[:, k * SEQ:(k + 1) * SEQ], km[:, h0 + 2 * r + k, 0:P], qp)
                        last.then_inc(S("c_l_mm"), 1)
                    for r in range(2):
                        o = claim(pe, "c_l1", 2 * m + r, "c_sqr", 4 * m + 3 + r)
                        for k in range(2):
                            last = mm(o[:, k * SEQ:(k + 1) * SEQ], km[:, h0 + 2 * r + k, P:SEQ], qp)
                        last.then_inc(S("c_l_mm"), 1)

                def turn(i):
                    m = 4 * n + i
                    o = claim(pe, "c_t0", 3 * m, "c_pT_dve", m + 1)
                    pe.wait_ge(S("c_exp"), 2 * m + 2)
                    for k in range(4):
                        last = pe.transpose(o[:, k * P:(k + 1) * P], c_p0[:, m % 2, k, :], ident[:, :])
                    last.then_inc(S("c_t_mm"), 1)
                    for r in range(2):
                        o = claim(pe, "c_t0", 3 * m + 1 + r, "c_pT_act", 2 * m + r + 1)
                        for k in range(2):
                            for s in range(2):
                                last = pe.transpose(o[:, (2 * k + s) * P:(2 * k + s + 1) * P],
                                                    c_p1[:, m % 2, 2 * r + k, s * P:(s + 1) * P], ident[:, :])
                        last.then_inc(S("c_t_mm"), 1)

                for i in range(4):
                    m = 4 * n + i
                    window_scores(i)
                    if m > 0:
                        linear_values(m - 1)
                    linear_scores(i)
                    if m > 0:
                        window_values(m - 1)
                    turn(i)
                    if n + 1 < NB * G:
                        c_spread_out(n + 1, i)
                        if i == 2:
                            c_values(n + 1)
                    if n > 0 and i == 1:
                        c_turn_cat(n - 1)
                    if n > 0 and i == 2:
                        c_out(n - 1)

            lin, win = ps[:, 6, :], ps[:, 7, :]

            def linear_values(m):
                n, i = divmod(m, 4)
                v = [value_blocks((2 * n + s) % 4) for s in range(2)]
                if i == 0:
                    pe.wait_ge(S("c_vm"), n + 1)
                if i == 0 and n > 0:
                    pe.wait_ge(S("c_cat"), 2 * n)
                pe.wait_ge(S("c_mask"), 2 * m + 2)
                pe.wait_ge(S("c_sqr"), 4 * m + 4)
                for k in range(4):
                    h = 4 * i + k
                    first, end = h == 0, h == HC - 1
                    mm(lin[:, 0:VA], c_a0[:, m % 2, k, 0:P], v[0][:, h, :], first, end)
                    mm(lin[:, VA:2 * VA], c_a0[:, m % 2, k, P:SEQ], v[0][:, h, :], False, False)
                    last = mm(lin[:, VA:2 * VA], c_a1[:, m % 2, k, :], v[1][:, h, :], False, end)
                last.then_inc(S("c_lin_mm"), 1)

            def window_values(m):
                n, i = divmod(m, 4)
                v = [value_blocks((2 * n + s) % 4) for s in range(2)]
                pe.wait_ge(S("c_pT_dve"), m + 1)
                pe.wait_ge(S("c_pT_act"), 2 * m + 2)
                for k in range(4):
                    h = 4 * i + k
                    first, end = h == 0, h == HC - 1
                    pT = c_pT[:, m % 2]
                    mm(win[:, 0:VA], pT[:, 0, k * P:(k + 1) * P], v[0][:, h, :], first, end)
                    c1 = (k % 2) * SEQ
                    mm(win[:, VA:2 * VA], pT[:, 1 + k // 2, c1:c1 + P], v[0][:, h, :], False, False)
                    last = mm(win[:, VA:2 * VA], pT[:, 1 + k // 2, c1 + P:c1 + SEQ], v[1][:, h, :], False, end)
                last.then_inc(S("c_win_mm"), 1)

            def c_turn_cat(n):
                o = claim(pe, "c_cT", n, "c_catT", n + 1)
                pe.wait_ge(S("c_cat"), 2 * n + 2)
                for s in range(2):
                    for f in range(2):
                        last = pe.transpose(o[:, (2 * f + s) * P:(2 * f + s + 1) * P],
                                            c_cat[:, n % 2, s, f * P:(f + 1) * P], ident[:, :])
                last.then_inc(S("c_cT_mm"), 1)

            def c_out(n):
                if n % NB < NB - 1:
                    o = claim(pe, "c_y", n, "c_xsum", n // NB + 1)
                else:
                    o = claim(pe, "c_y", n, "x_sum", G * PH.index("C") + n // NB + 1)
                pe.wait_ge(S("c_catT"), n + 1)
                for s in range(2):
                    for f in range(2):
                        last = mm(o[:, s * P:(s + 1) * P], c_catT[:, f, s * P:(s + 1) * P], wout_c[:, f, :],
                                  f == 0, f == 1)
                last.then_inc(S("c_y_mm"), 1)

            def c_open():
                for b in (6, 7):
                    pe.wait_ge(*freed_by[b])
                ring["banks"] = list(range(6))

            def c_finish():
                n = NB * G - 1
                linear_values(4 * n + 3)
                window_values(4 * n + 3)
                c_turn_cat(n)
                c_out(n)
                ring["banks"] = list(range(8))
                for b in (6, 7):
                    freed_by[b] = (S("c_cat"), 2 * NB * G)

            if "C" in PH:
                phase("C", turn=ln_transpose(LN_C), **by_sequence(c_proj, c_heads, c_finish, c_open))

            def moe(n, u, key):
                def up(g):
                    pe.wait_ge(*ln("ln_xT", u, g))
                    o = claim(pe, f"d_g{n}", g, "d_exp", n * G + g + 1)
                    for j in range(TG):
                        last = mm(o[:, j * NE:(j + 1) * NE], xnT[:, g, j * P:(j + 1) * P], gateT[:, :])
                    last.then_inc(S("d_g_mm"), 1)
                    for c in range(NF):
                        k = n * G * NF + NF * g + c
                        o = claim(pe, "d_s", k, "d_srelu", k + 1)
                        mm(o, moe_up[:, FF + c * P:FF + (c + 1) * P], xnT[:, g, :]).then_inc(S("d_s_mm"), 1)

                def turn_gate(g):
                    k = n * G + g
                    o = claim(pe, "d_pT", k, "d_partsT", k + 1).bitcast(BF16)
                    pe.wait_ge(S("d_gate"), k + 1)
                    for j in range(TG):
                        last = pe.transpose(o[0:96, j * P:(j + 1) * P], d_parts[:, g % 2, j, :], ident_bf[:, :])
                    last.then_inc(S("d_pT_mm"), 1)

                def experts(g):
                    for c in range(NF):
                        k = n * G * NF + NF * g + c
                        o = claim(pe, "d_u", k, "d_relu", k + 1)
                        mm(o, moe_up[:, c * P:(c + 1) * P], xnT[:, g, :]).then_inc(S("d_u_mm"), 1)
                        o = claim(pe, "d_b", k, "d_r2", k + 1)
                        if c == 0:
                            pe.wait_ge(S("d_partsT"), n * G + g + 1)
                        mm(o, gate_sel[0:96, c, :], d_partsT[0:96, g % 2, :]).then_inc(S("d_b_mm"), 1)

                def down(g):
                    o = claim(pe, f"d_y{n}", g, "x_sum", G * PH.index(key) + g + 1)
                    pe.wait_ge(S("d_sq"), (n * G + g + 1) * NF)
                    pe.wait_ge(S("d_r2"), (n * G + g + 1) * NF)
                    for j in range(TG):
                        for c in range(2 * NF):
                            last = mm(o[:, j * P:(j + 1) * P], d_r2[:, g % 3, c, j * P:(j + 1) * P], moe_dn[:, c, :],
                                      c == 0, c == 2 * NF - 1)
                    last.then_inc(S("d_y_mm"), 1)
                phase("D", turn=ln_transpose(u), up=up, turn_gate=turn_gate, experts=experts, down=down)

            if "D" in PH:
                moe(0, LN_D0, "D")

            def e_layer(l):
                w4, w1, w2 = e_w4[l % 2], e_w1[l % 2], e_w2[l % 2]

                def qkv(g):
                    n = l * G + g
                    if g == 0:
                        pe.wait_ge(S(f"e_in{l % 2}"), E_IN * (l // 2 + 1))
                    pe.wait_ge(*ln("ln_xT", LN_E + 2 * l, g))
                    o = claim(pe, "e_k", n, "e_kexp", NB * (n + 1))
                    mm(o, w4[:, 1, :], xnT[:, g, :]).then_inc(S("e_k_mm"), 1)
                    o = claim(pe, "e_q", n, "e_qsub", n + 1)
                    for j in range(TG):
                        last = mm(o[:, j * P:(j + 1) * P], xnT[:, g, j * P:(j + 1) * P], w4[:, 0, :])
                    last.then_inc(S("e_q_mm"), 1)
                    o = claim(pe, "e_v", n, "e_v", n + 1)
                    for j in range(TG):
                        last = mm(o[:, j * P:(j + 1) * P], xnT[:, g, j * P:(j + 1) * P], w4[:, 2, :])
                    last.then_inc(S("e_v_mm"), 1)

                def turn_k(g):
                    n = l * G + g
                    o = claim(pe, "e_kT", n, "e_k", n + 1)
                    pe.wait_ge(S("e_kexp"), NB * (n + 1))
                    for j in range(TG):
                        last = pe.transpose(o[:, j * P:(j + 1) * P], e_kTe[:, g % 2, j * P:(j + 1) * P], ident[:, :])
                    last.then_inc(S("e_kT_mm"), 1)

                def turn_q(g):
                    n = l * G + g
                    o = claim(pe, "e_qT", n, "e_qT", n + 1)
                    pe.wait_ge(S("e_qn"), n + 1)
                    for j in range(TG):
                        last = pe.transpose(o[:, j * P:(j + 1) * P], e_qe[:, g % 2, j * P:(j + 1) * P], ident[:, :])
                    last.then_inc(S("e_qT_mm"), 1)

                def context(g):
                    n = l * G + g
                    o = claim(pe, "e_c", n, "e_ctx", n + 1)
                    pe.wait_ge(S("e_k"), n + 1)
                    pe.wait_ge(S("e_v"), n + 1)
                    for b in range(NB):
                        for s in range(2):
                            j = (2 * b + s) * P
                            last = mm(o[:, b * P:(b + 1) * P], e_v[:, g % 3, j:j + P], e_k[:, g % 2, j:j + P], s == 0, s == 1)
                    last.then_inc(S("e_c_mm"), 1)

                def fold(g):
                    n = l * G + g
                    o = claim(pe, "e_m", n, "e_m", n + 1)
                    pe.wait_ge(S("e_ctx"), n + 1)
                    for b in range(NB):
                        last = mm(o[:, b * P:(b + 1) * P], e_ctx[:, g % 2, b, :], w4[:, 3, :])
                    last.then_inc(S("e_m_mm"), 1)

                def out_(g):
                    n = l * G + g
                    o = claim(pe, "e_y", n, "e_z1", n + 1)
                    pe.wait_ge(S("e_m"), n + 1)
                    pe.wait_ge(S("e_qT"), n + 1)
                    for j in range(TG):
                        last = mm(o[:, j * P:(j + 1) * P], e_qT[:, g, j * P:(j + 1) * P], e_m[:, g % 2, j // 2, :])
                    last.then_inc(S("e_y_mm"), 1)

                def up(half):
                    def stage(g):
                        n = l * G + g
                        pe.wait_ge(*ln("ln_xT", LN_E + 2 * l + 1, g))
                        for c in (2 * half, 2 * half + 1):
                            o = claim(pe, "e_u", NF * n + c, "e_h", NF * n + c + 1)
                            mm(o, w1[:, c * P:(c + 1) * P], xnT[:, g, :]).then_inc(S("e_u_mm"), 1)
                    return stage

                def down(half):
                    def stage(g):
                        n = l * G + g
                        o = claim(pe, "e_d", n, "e_z2", n + 1) if half == 0 else bank("e_d", n)
                        pe.wait_ge(S("e_h"), NF * (n + 1))
                        for j in (2 * half, 2 * half + 1):
                            for c in range(NF):
                                h0 = c * TOK + j * P
                                last = mm(o[:, j * P:(j + 1) * P], e_h[:, g % 3, h0:h0 + P], w2[:, c, :],
                                          c == 0, c == NF - 1)
                        if half == 1:
                            last.then_inc(S("e_d_mm"), 1)
                    return stage

                phase("E", turn_1=ln_transpose(LN_E + 2 * l), qkv=qkv, turn_k=turn_k, turn_q=turn_q, context=context,
                              fold=fold, out=out_, turn_2=ln_transpose(LN_E + 2 * l + 1), up_a=up(0), up_b=up(1),
                              down_a=down(0), down_b=down(1))

            if "E" in PH:
                phase("Z")
                for l in range(DEPTH):
                    e_layer(l)
                phase("X")
            if "d" in PH:
                moe(1, LN_D1, "d")
            pipeline(stages, G)

        @block.vector
        def _(dve):
            stages = []

            def phase(key, **own):
                stages.append((key, own))

            own = [0]

            def next_own():
                own[0] += 1
                return own[0]

            def tt(o, a, b, op):
                return dve.tensor_tensor(o, a, b, op)

            def ln_stats(u, src):
                def stage(g):
                    if src is x and u == 0:
                        dve.wait_ge(S(f"x_in{g}"), 16)
                    if src is x and u > 0:
                        dve.wait_ge(S("x_sum"), G * LN_PH[u] + g + 1)
                    if src is z:
                        if (u - LN_E) % 2 == 1:
                            dve.wait_ge(S("e_z1"), ((u - LN_E) // 2) * G + g + 1)
                        elif u > LN_E:
                            dve.wait_ge(S("e_z2"), ((u - LN_E) // 2 - 1) * G + g + 1)
                        else:
                            dve.wait_ge(S("z_in"), g + 1)
                    for t in tiles(g):
                        last = dve.bn_stats(st[:, t, :], src[:, t, :])
                    last.then_inc(S("dve_own"), 1)
                    dve.wait_ge(S("dve_own"), next_own())
                    for t in tiles(g):
                        last = dve.bn_aggr(mv[:, t, :], st[:, t, :])
                    last.then_inc(S("dve_own"), 1)
                    dve.wait_ge(S("dve_own"), next_own())
                    dve.tensor_scalar(var_eps[:, TG * g:TG * g + TG], mv[:, TG * g:TG * g + TG, 1], 1e-5, None,
                                      ALU.add).then_inc(ln("ln_ve", u, g)[0], 1)
                return stage

            def normalise(u, src, g, dst, scale):
                for t in tiles(g):
                    last = dve.tensor_scalar(dst[:, t, :], src[:, t, :], mv[:, t, 0:1], scale[:, t:t + 1],
                                             ALU.subtract, ALU.mult)
                return last

            def ln_apply(u, src):
                def stage(g):
                    dve.wait_ge(*ln("ln_rs", u, g))
                    normalise(u, src, g, xn, rstd).then_inc(ln("ln_xn", u, g)[0], 1)
                return stage

            dve.wait_ge(S("masks"), 1)
            dve.tensor_copy(ident_bf[:, :], ident[:, :]).then_inc(S("ident_bf"), 1)
            n_out = [0]

            def evac(dst, src):
                n_out[0] += 1
                dve.tensor_copy(dst, src).then_inc(S("prep_out"), 1)

            def prep(i):
                dve.wait_ge(S("prep_mm"), i + 1)
                return bank("prep", i)

            def prepare_query_key():
                o = prep(0)
                evac(a_w[:, :], o[:, 0:2 * P])

            def prepare_threshold():
                dve.wait_ge(S("f_in"), F_IN)
                flat_up = s_up0.rearrange("p c d -> p (c d)")
                dve.tensor_reduce(s_absum[:, 0:1], flat_up, X, ALU.add, apply_absolute_value=True).then_inc(S("f_abs"), 1)
                dve.tensor_reduce(s_absum[:, 1:2], s_dn0, X, ALU.add, apply_absolute_value=True).then_inc(S("f_abs"), 1)
                o = prep(1)
                half_mean = 0.5 / (P * FF)
                dve.tensor_scalar(s_thr[:, 0:2], o[:, 0:2], half_mean, None, ALU.mult).then_inc(S("prep_out"), 1)
                dve.tensor_scalar(s_thr[:, 2:4], o[:, 0:2], -half_mean, None, ALU.mult).then_inc(S("prep_out"), 1)
                n_out[0] += 2
                dve.wait_ge(S("prep_out"), n_out[0])
                for i, src in enumerate((flat_up, s_dn0)):
                    dve.tensor_scalar(s_tern[:, i, :], src, s_thr[:, 2 + i:3 + i], None, ALU.is_lt).then_inc(S("dve_own"), 1)
                    dve.wait_ge(S("dve_own"), next_own())
                    dve.scalar_tensor_tensor(out=s_wt[:, i, :], in0=src, scalar=s_thr[:, i:i + 1], in1=s_tern[:, i, :],
                                             op0=ALU.is_gt, op1=ALU.subtract).then_inc(S("f_tern"), 1)

            def prepare_ternary():
                o = prep(2)
                evac(wupT[:, :], o)
                o = prep(3)
                evac(wdnT[:, :, :].rearrange("p c f -> p (c f)"), o)

            def prepare_values_b():
                for i in range(2):
                    o = prep(4 + i)
                    evac(wvT[:, 4 * i:4 * i + 4, :].rearrange("p c f -> p (c f)"), o)

            def prepare_features():
                dve.wait_ge(S("masks"), 2)
                dve.tensor_copy(bd8, head8[:, :].unsqueeze(2).to_broadcast([P, HC, DC])).then_inc(S("dve_const"), 1)
                dve.tensor_copy(bd16[:, :, :], head16[:, :].unsqueeze(2).to_broadcast([P, HE, DE])).then_inc(S("dve_const"), 1)
                dve.wait_ge(S("dve_const"), 2)
                o = prep(6)
                evac(s_cfT[0:16, :, :].rearrange("p c f -> p (c f)"), o[0:16, 0:2 * P])
                evac(cols[:, :], o[:, 2 * P:2 * P + 25])
                dve.wait_ge(S("prep_out"), n_out[0])
                for i in (WQ, WK, WV):
                    dve.tensor_scalar(c_w[:, i, :], c_w[:, i, :], cols[:, 24:25], None, ALU.mult).then_inc(S("c_scaled"), 1)
                o = prep(7)
                tt(s_bd, o[:, 0:P], bd8.rearrange("p h d -> p (h d)"), ALU.mult).then_inc(S("prep_out"), 1)
                n_out[0] += 1

            def prepare_query_c():
                o = prep(8)
                evac(s_wqT, o[:, 0:P])
                o = prep(9)
                evac(c_w[:, WQP, :], o[:, 0:P])

            def prepare_experts():
                o = prep(10)
                evac(s_w1T[0:64, :], o[0:64, :])
                o = prep(11)
                evac(s_fc2T[0:64, :], o[0:64, 0:P])
                evac(gateT[:, :], o[:, P:P + NE])

            def prepare_shared():
                o = prep(12)
                evac(moe_up[:, 0:FF], o)
                o = prep(13)
                evac(moe_up[:, FF:2 * FF], o)
                o = prep(14)
                evac(moe_dn[:, 0:NF, :].rearrange("p c f -> p (c f)"), o)
                o = prep(15)
                evac(moe_dn[:, NF:2 * NF, :].rearrange("p c f -> p (c f)"), o)
                assert n_out[0] == PREP_OUT[-1], n_out

            prepare_query_key()

            def a_values(g):
                dve.wait_ge(S("a_v_mm"), g + 1)
                dve.tensor_copy(a_v[:, g, :, :].rearrange("p t f -> p (t f)"), bank("a_v", g)).then_inc(S("a_v"), 1)

            def a_max(g):
                for b in range(NB):
                    n = NB * g + b
                    dve.wait_ge(S("a_s_mm"), n + 1)
                    o = bank("a_s", n)
                    dve.tensor_reduce(a_nmax[:, 0, 2 * n:2 * n + 1], o[:, 0:P], X, ALU.max).then_inc(S("a_max"), 1)
                    dve.tensor_reduce(a_nmax[:, 0, 2 * n + 1:2 * n + 2], o[:, P:384], X, ALU.max).then_inc(S("a_max"), 1)
                    dve.wait_ge(S("a_max"), 2 * n + 2)
                    dve.tensor_scalar(a_nmax[:, 1, 2 * n:2 * n + 2], a_nmax[:, 0, 2 * n:2 * n + 2], -P ** -0.5, None,
                                      ALU.mult).then_inc(S("a_nmax"), 1)

            def a_turned(g):
                dve.wait_ge(S("a_exp"), TG * (g + 1))
                dve.reciprocal(a_sum[:, 1, TG * g:TG * g + TG], a_sum[:, 0, TG * g:TG * g + TG]).then_inc(S("a_rec"), 1)
                dve.wait_ge(S("a_pT_mm"), NB * g + 2)
                dve.tensor_copy(a_pT[:, g % 2, 1, :], bank("a_pT", NB * g + 1)[:, 0:384]).then_inc(S("a_pT1"), 1)

            def a_add(g):
                dve.wait_ge(S("a_o_mm"), g + 1)
                dve.wait_ge(S("a_rec"), g + 1)
                o = bank("a_o", g)
                for j, t in enumerate(tiles(g)):
                    last = dve.scalar_tensor_tensor(out=x[:, t, :], in0=o[:, j * P:(j + 1) * P], scalar=a_sum[:, 1, t:t + 1],
                                                    in1=x[:, t, :], op0=ALU.mult, op1=ALU.add)
                last.then_inc(S("x_sum"), 1)

            if "A" in PH:
                phase("A", prepare=in_turn(prepare_threshold, prepare_ternary, prepare_values_b, prepare_features), stats=ln_stats(LN_A, x), apply=ln_apply(LN_A, x), evacuate=a_values, max=a_max, turned=a_turned, add=a_add)

            def c_blank(g):
                if g == 0:
                    dve.wait_ge(S("x_sum"), G * PH.index("f"))
                if g < 2:
                    dve.tensor_scalar((pick_q, pick_k)[g].rearrange("p a (b c) -> p (a b) c", c=P),
                                      ones[:, :].unsqueeze(1).to_broadcast([P, 8, P]), 0.0, None, ALU.mult)\
                        .then_inc(S("c_blank"), 1)
                dve.memset(c_vm[:, g], 0.0).then_inc(S("c_clear"), 1)

            def ffn(n, u, key):
                def rms_in(g):
                    ts = slice(TG * g, TG * g + TG)
                    dve.wait_ge(*ln("ln_rs", u, g))
                    tt(second[:, 0, ts], mv[:, ts, 1], rstd[:, ts], ALU.mult).then_inc(S("dve_own"), 1)
                    dve.wait_ge(S("dve_own"), next_own())
                    tt(second[:, 1, ts], second[:, 0, ts], rstd[:, ts], ALU.mult).then_inc(S("s2_b"), 1)

                def apply(g):
                    ts = slice(TG * g, TG * g + TG)
                    dve.wait_ge(S("s2_pow"), S2[u] * G + g + 1)
                    dve.tensor_scalar(second[:, 0, ts], second[:, 2, ts], 1e-8, None, ALU.add).then_inc(S("dve_own"), 1)
                    dve.wait_ge(S("dve_own"), next_own())
                    dve.reciprocal(second[:, 1, ts], second[:, 0, ts]).then_inc(S("dve_own"), 1)
                    dve.wait_ge(S("dve_own"), next_own())
                    tt(second[:, 0, ts], second[:, 1, ts], rstd[:, ts], ALU.mult).then_inc(S("dve_own"), 1)
                    dve.wait_ge(S("dve_own"), next_own())
                    normalise(u, x, g, xn, second[:, 0, :]).then_inc(ln("ln_xn", u, g)[0], 1)

                def squares(g):
                    k = n * G + g
                    dve.wait_ge(S("f_sq"), k + 1)
                    dve.tensor_reduce(f_ssq[n][:, g % 2, :], f_sq[n][:, g % 2, :].rearrange("p (c t) -> p t c", c=NF), X,
                                      ALU.add).then_inc(S("f_ssq"), 1)

                def mean_square(g):
                    k = n * G + g
                    dve.wait_ge(S("f_ss_mm"), k + 1)
                    dve.tensor_scalar(f_r[n][:, 0, TG * g:TG * g + TG], bank(f"f_ss{n}", g)[:, 0:TG], 1.0 / FF, None,
                                      ALU.mult).then_inc(S("f_ms"), 1)

                def add(g):
                    k = n * G + g
                    ts = slice(TG * g, TG * g + TG)
                    dve.wait_ge(S("f_pow"), k + 1)
                    dve.tensor_scalar(f_r[n][:, 0, ts], f_r[n][:, 1, ts], 1e-8, None, ALU.add).then_inc(S("dve_own"), 1)
                    dve.wait_ge(S("dve_own"), next_own())
                    dve.reciprocal(f_r[n][:, 2, ts], f_r[n][:, 0, ts]).then_inc(S("dve_own"), 1)
                    dve.wait_ge(S("dve_own"), next_own())
                    dve.wait_ge(S("f_y_mm"), k + 1)
                    o = bank(f"f_y{n}", g)
                    for j, t in enumerate(tiles(g)):
                        last = dve.scalar_tensor_tensor(out=x[:, t, :], in0=o[:, j * P:(j + 1) * P],
                                                        scalar=f_r[n][:, 2, t:t + 1], in1=x[:, t, :],
                                                        op0=ALU.mult, op1=ALU.add)
                    last.then_inc(S("x_sum"), 1)
                own = {"blank": c_blank} if n == 1 else \
                    {"prepare": in_turn(prepare_query_c, prepare_experts, prepare_shared, None)}
                phase("F", stats=ln_stats(u, x), second_scale=rms_in, apply=apply, squares=squares, mean_square=mean_square, add=add, **own)

            if "F" in PH:
                ffn(0, LN_F0, "F")

            def b_softmax(g):
                if g == 0:
                    dve.wait_ge(S("x_sum"), G * PH.index("B"))
                    dve.memset(b_ctx, 0.0).then_inc(S("dve_own"), 1)
                    dve.wait_ge(S("dve_own"), next_own())

                def q_tile(j):
                    n = TG * g + j
                    r = n % 4
                    if g >= 2 and j == 0:
                        dve.wait_ge(S("b_c_mm"), 2 * NB * (g - 1))
                    for half in range(2):
                        hs = slice(half * 8, half * 8 + 8)
                        dve.wait_ge(S("b_q_mm"), 2 * n + half + 1)
                        o = bank("b_q", 2 * n + half).rearrange("p (h d) -> p h d", d=QD)
                        dve.tensor_reduce(b_qmax[:, r, hs], o, X, ALU.max).then_inc(S("dve_own"), 1)
                        dve.wait_ge(S("dve_own"), next_own())
                        tt(b_q[:, g % 2, j, half * 512:half * 512 + 512].rearrange("p (h d) -> p h d", d=QD), o,
                           b_qmax[:, r, hs].unsqueeze(2).to_broadcast([P, 8, QD]), ALU.subtract).then_inc(S("b_qsub"), 1)

                def q_sum(j):
                    n = TG * g + j
                    r = n % 4
                    dve.wait_ge(S("b_qexp"), n + 1)
                    dve.tensor_reduce(b_qsum[:, r, :], b_q[:, g % 2, j, :].rearrange("p (h d) -> p h d", d=QD), X,
                                      ALU.add).then_inc(S("dve_own"), 1)
                    dve.wait_ge(S("dve_own"), next_own())
                    if n >= 4:
                        dve.wait_ge(S("b_qn"), n - 3)
                    dve.reciprocal(b_qrec[:, r, :], b_qsum[:, r, :]).then_inc(S("b_qrec"), 1)

                def k_max(c):
                    n = NC_ * g + c
                    dve.wait_ge(S("b_k_mm"), n + 1)
                    dve.tensor_reduce(b_kmax[:, n, :], bank("b_k", n).rearrange("p (b t) -> p b t", b=NB), X, ALU.max,
                                      negate=True).then_inc(S("b_kmax"), 1)

                for c in range(NC_ + 2):
                    if c < NC_:
                        k_max(c)
                        if c % 2 == 0:
                            q_tile(c // 2)
                    if c >= 2:
                        if c % 2 == 0:
                            q_sum(c // 2 - 1)
                dve.wait_ge(S("b_kexp"), NB * NC_ * (g + 1))
                dve.reciprocal(b_krec[:, g % 2, :, :], b_ksum[:, g % 2, :, :]).then_inc(S("b_krec"), 1)

            def b_context(g):
                dve.wait_ge(S("b_krec"), g + 1)
                for b in range(NB):
                    n = NB * g + b
                    if n >= 4:
                        dve.wait_ge(S("b_m_mm"), 2 * (n - 3))
                    for half in range(2):
                        dve.wait_ge(S("b_c_mm"), 2 * n + half + 1)
                        cs = slice(4 * half, 4 * half + 4)
                        for q in range(2):
                            r = slice(64 * q, 64 * q + 64)
                            src = bank("b_c", 2 * n + half).rearrange("p (c d) -> p c d", d=P)
                            tt(b_ctx[r, n % 4, cs, r], src[r, :, r],
                               b_krec[r, g % 2, b, cs].unsqueeze(2).to_broadcast([64, 4, 64]),
                               ALU.mult).then_inc(S("b_ctx"), 1)

            def b_fold(g):
                for b in range(NB):
                    n = NB * g + b
                    dve.wait_ge(S("b_g_mm"), n + 1)
                    dve.tensor_copy(b_g[:, n % 4, :], bank("b_g", n)[:, 0:P]).then_inc(S("b_g"), 1)

            def b_add(g):
                dve.wait_ge(S("b_xb"), g + 1)
                dve.wait_ge(S("b_y_mm"), g + 1)
                xg = x[:, TG * g:TG * g + TG, :].rearrange("p t f -> p (t f)")
                tt(xg, bank("b_y", g), xg, ALU.add).then_inc(S("x_sum"), 1)

            if "B" in PH:
                phase("B", stats=ln_stats(LN_B, x), apply=ln_apply(LN_B, x), heads=b_softmax, mask=b_context, fold=b_fold, add=b_add)
            if "f" in PH:
                ffn(1, LN_F1, "f")

            def c_rms(g):
                ts = slice(TG * g, TG * g + TG)
                k = S2[LN_C] * G + g
                dve.wait_ge(*ln("ln_rs", LN_C, g))
                tt(second[:, 0, ts], mv[:, ts, 1], rstd[:, ts], ALU.mult).then_inc(S("dve_own"), 1)
                dve.wait_ge(S("dve_own"), next_own())
                tt(second[:, 1, ts], second[:, 0, ts], rstd[:, ts], ALU.mult).then_inc(S("s2_b"), 1)
                dve.wait_ge(S("s2_b"), k + 1)
                dve.tensor_scalar(second[:, 0, ts], second[:, 1, ts], 1e-6, None, ALU.add).then_inc(S("c_ms"), 1)
                normalise(LN_C, x, g, z, rstd).then_inc(S("c_ln"), 1)

            def c_apply(g):
                dve.wait_ge(S("s2_pow"), S2[LN_C] * G + g + 1)
                dve.wait_ge(S("c_ln"), g + 1)
                for t in tiles(g):
                    last = dve.tensor_scalar(xn[:, t, :], z[:, t, :], second[:, 2, t:t + 1], None, ALU.mult)
                last.then_inc(ln("ln_xn", LN_C, g)[0], 1)

            def c_proj(n):
                for k, (name, c0, c1) in enumerate((("c_q", 0, 2 * SEQ), ("c_k", 2 * SEQ, 3 * SEQ))):
                    dve.wait_ge(S("c_high"), 2 * n + k + 1)
                    if n >= 1:
                        dve.wait_ge(S("c_spread_mm"), 8 * n)
                    tt(c_split[:, 1, c0:c1], bank(name, n)[:, 0:c1 - c0], c_split[:, 0, c0:c1], ALU.subtract)\
                        .then_inc(S("c_low"), 1)
                if n == 0:
                    c_values(n)
                if n == 0:
                    for i in range(4):
                        c_keys(n, i)

            def c_values(n):
                dve.wait_ge(S("c_v_mm"), n + 1)
                if n == 0:
                    dve.wait_ge(S("c_zero"), 6)
                if n >= 2:
                    dve.wait_ge(S("c_win_mm"), 4 * (n - 1))
                for s in range(2):
                    last = dve.tensor_copy(own_columns((2 * n + s) % 4),
                                           bank("c_v", n)[:, s * P:(s + 1) * P].rearrange("p (h d) -> p h d", d=DC))
                last.then_inc(S("c_vm"), 1)

            def c_keys(n, i):
                m = 4 * n + i
                dve.wait_ge(S("c_spread_mm"), 2 * m + 2)
                if m >= 8:
                    dve.wait_ge(S("c_l_mm"), 4 * (m - 7))
                for k in range(4):
                    last = dve.tensor_scalar(c_km[:, n % 2, 4 * i + k, :], bank("c_ks", m)[:, 0:SEQ],
                                             quarter[:, k:k + 1], None, ALU.mult)
                last.then_inc(S("c_km"), 1)

            def c_heads(n):
                def softmax(i):
                    m = 4 * n + i
                    mx = c_max[:, m % 4, :]
                    if m >= 2:
                        dve.wait_ge(S("c_t_mm"), 3 * (m - 1))
                    dve.wait_ge(S("c_s_mm"), 3 * m + 1)
                    o = bank("c_s0", m).rearrange("p (h k) -> p h k", k=P)
                    dve.tensor_reduce(mx[:, 0:4], o, X, ALU.max).then_inc(S("c_max"), 1)
                    dve.wait_ge(S("c_s_mm"), 3 * m + 2)
                    o0 = bank("c_s1", 2 * m)[:, 0:384].rearrange("p (h k) -> p h k", k=192)
                    dve.tensor_reduce(mx[:, 4:6], o0, X, ALU.max).then_inc(S("c_max"), 1)
                    dve.wait_ge(S("c_max"), 3 * m + 1)
                    tt(c_p0[:, m % 2], o, mx[:, 0:4].unsqueeze(2).to_broadcast([P, 4, P]), ALU.subtract)\
                        .then_inc(S("c_sub"), 1)
                    dve.wait_ge(S("c_s_mm"), 3 * m + 3)
                    o1 = bank("c_s1", 2 * m + 1)[:, 0:384].rearrange("p (h k) -> p h k", k=192)
                    dve.tensor_reduce(mx[:, 6:8], o1, X, ALU.max).then_inc(S("c_max"), 1)
                    dve.wait_ge(S("c_max"), 3 * m + 2)
                    tt(c_p1[:, m % 2, 0:2, 64:SEQ], o0, mx[:, 4:6].unsqueeze(2).to_broadcast([P, 2, 192]),
                       ALU.subtract).then_inc(S("c_sub"), 1)
                    dve.wait_ge(S("c_max"), 3 * m + 3)
                    tt(c_p1[:, m % 2, 2:4, 64:SEQ], o1, mx[:, 6:8].unsqueeze(2).to_broadcast([P, 2, 192]),
                       ALU.subtract).then_inc(S("c_sub"), 1)

                def turn_out(i):
                    m = 4 * n + i
                    if m >= 2:
                        dve.wait_ge(S("c_win_mm"), m - 1)
                    dve.wait_ge(S("c_t_mm"), 3 * m + 1)
                    dve.tensor_copy(c_pT[:, m % 2, 0, :], bank("c_t0", 3 * m)).then_inc(S("c_pT_dve"), 1)

                for i in range(4):
                    softmax(i)
                    turn_out(i)
                    if n > 0 and i == 0:
                        c_divide(n - 1)
                    if n + 1 < NB * G:
                        c_keys(n + 1, i)
                        if i == 2:
                            c_values(n + 1)
                    if n > 0 and i == 2:
                        c_add(n - 1)

            def c_divide(n):
                dve.wait_ge(S("c_win_mm"), 4 * (n + 1))
                r = c_rec[:, n % 2]
                r2 = c_rec[:, 2 + n % 2]
                for half, b in ((0, 6), (1, 7)):
                    acc = ps[:, b, 0:2 * VA].rearrange("p (s v) -> p s v", v=VA)
                    dve.tensor_scalar(r, acc[:, :, P:VA], 1e-6 if half == 0 else 0.0, None, ALU.add)\
                        .then_inc(S("dve_own"), 1)
                    dve.wait_ge(S("dve_own"), next_own())
                    dve.reciprocal(r2, r).then_inc(S("dve_own"), 1)
                    dve.wait_ge(S("dve_own"), next_own())
                    for s in range(2):
                        last = tt(c_cat[:, n % 2, s, half * P:(half + 1) * P].rearrange("p (h d) -> p h d", d=DC),
                                  acc[:, s, 0:P].rearrange("p (h d) -> p h d", d=DC),
                                  r2[:, s, :].unsqueeze(2).to_broadcast([P, HC, DC]), ALU.mult)
                    last.then_inc(S("c_cat"), 1)
                    if half == 0:
                        dve.wait_ge(S("c_cat"), 2 * n + 1)

            def c_add(n):
                g = n // NB
                if n % NB == 0:
                    dve.wait_ge(S("c_xz"), g + 1)
                dve.wait_ge(S("c_y_mm"), n + 1)
                xs = x[:, 2 * n:2 * n + 2, :].rearrange("p t f -> p (t f)")
                tt(xs, bank("c_y", n)[:, 0:SEQ], xs, ALU.add).then_inc(S("c_xsum" if n % NB < NB - 1 else "x_sum"), 1)

            if "C" in PH:
                def c_finish():
                    c_divide(NB * G - 1)
                    c_add(NB * G - 1)

                phase("C", stats=ln_stats(LN_C, x), second_scale=c_rms, apply=c_apply, **by_sequence(c_proj, c_heads, c_finish))

            def moe(n, u, key):
                def route(g):
                    k = n * G + g
                    def link(ins):
                        ins.then_inc(S("dve_own"), 1)
                        dve.wait_ge(S("dve_own"), next_own())

                    v3 = lambda a: a.rearrange("p (t e) -> p t e", t=TG)
                    dve.wait_ge(S("d_exp"), k + 1)
                    link(dve.tensor_scalar(d_sc[:, g, 0, :], d_e[:, g, :], 1.0, None, ALU.add))
                    link(dve.reciprocal(d_sc[:, g, 1, :], d_sc[:, g, 0, :]))
                    sc, sfc = d_sc[:, g, 1, :], d_sfc[:, g, :]
                    link(tt(v3(sfc), v3(sc), bias_bc[:, :].unsqueeze(1).to_broadcast([P, TG, NE]), ALU.add))
                    s4 = sfc.rearrange("p (q e) -> p q e", e=4)
                    tp = d_top[:, g]
                    a, b, c, d = (s4[:, :, i] for i in range(4))
                    link(tt(tp[:, 0, :], a, b, ALU.max))
                    link(tt(tp[:, 1, :], a, b, ALU.min))
                    link(tt(tp[:, 2, :], c, d, ALU.max))
                    link(tt(tp[:, 3, :], c, d, ALU.min))
                    link(tt(tp[:, 4, :], tp[:, 0, :], tp[:, 2, :], ALU.max))
                    link(tt(tp[:, 5, :], tp[:, 0, :], tp[:, 2, :], ALU.min))
                    link(tt(tp[:, 6, :], tp[:, 1, :], tp[:, 3, :], ALU.max))
                    link(tt(tp[:, 7, :], tp[:, 5, :], tp[:, 6, :], ALU.max))
                    link(tt(tp[:, 0, :], tp[:, 4, :], tp[:, 7, :], ALU.add))
                    gs = tp[:, 0, :].rearrange("p (t q) -> p t q", q=2)
                    gm = tp[:, 1, :].rearrange("p (t q) -> p t q", q=2)
                    link(tt(gm[:, :, 0], gs[:, :, 0], gs[:, :, 1], ALU.is_ge))
                    link(tt(gm[:, :, 1], gs[:, :, 0], gs[:, :, 1], ALU.is_lt))
                    link(tt(s4, s4, tp[:, 1, :].unsqueeze(2).to_broadcast([P, 2 * TG, 4]), ALU.mult))
                    s_j = v3(sfc).unsqueeze(2).to_broadcast([P, TG, NE, NE])
                    s_e = v3(sfc).unsqueeze(3).to_broadcast([P, TG, NE, NE])
                    c0 = d_cmp[:, g % 2, 0, :].rearrange("p (t e j) -> p t e j", t=TG, e=NE)
                    c1 = d_cmp[:, g % 2, 1, :].rearrange("p (t e j) -> p t e j", t=TG, e=NE)
                    link(tt(c1, s_j, s_e, ALU.is_equal))
                    link(tt(c1, c1, lower[:, :, :].unsqueeze(1).to_broadcast([P, TG, NE, NE]), ALU.mult))
                    link(tt(c0, s_j, s_e, ALU.is_gt))
                    link(tt(d_cmp[:, g % 2, 0, :], d_cmp[:, g % 2, 0, :], d_cmp[:, g % 2, 1, :], ALU.add))
                    link(dve.tensor_reduce(d_rank[:, g, :], d_cmp[:, g % 2, 0, :].rearrange("p (q j) -> p q j", j=NE), X,
                                           ALU.add))
                    link(dve.scalar_tensor_tensor(out=d_w[:, g, :], in0=d_rank[:, g, :], scalar=1.5, in1=sc,
                                                  op0=ALU.is_lt, op1=ALU.mult))
                    link(dve.tensor_reduce(d_den[:, g, 0, :], v3(d_w[:, g, :]), X, ALU.add))
                    link(dve.tensor_scalar(d_den[:, g, 0, :], d_den[:, g, 0, :], 1e-20, None, ALU.add))
                    link(dve.reciprocal(d_den[:, g, 1, :], d_den[:, g, 0, :]))
                    link(tt(v3(d_gate[:, g, :]), v3(d_w[:, g, :]), d_den[:, g, 1, :].unsqueeze(2).to_broadcast([P, TG, NE]),
                            ALU.mult))
                    if g < 2:
                        link(dve.memset(d_parts[:, g % 2], 0.0))
                    else:
                        dve.wait_ge(S("d_pT_mm"), k - 1)
                    part = [d_parts[:, g % 2, :, 32 * i:32 * i + NE] for i in range(3)]
                    rest = [d_rest[:, g % 2, i, :] for i in range(2)]
                    link(dve.tensor_copy(part[0], v3(d_gate[:, g, :])))
                    link(tt(v3(rest[0]), v3(d_gate[:, g, :]), part[0], ALU.subtract))
                    link(dve.tensor_copy(part[1], v3(rest[0])))
                    link(tt(v3(rest[1]), v3(rest[0]), part[1], ALU.subtract))
                    dve.tensor_copy(part[2], v3(rest[1])).then_inc(S("d_gate"), 1)

                def gated(g):
                    for c in range(NF):
                        k = (n * G + g) * NF + c
                        dve.wait_ge(S("d_rsq"), k + 1)
                        dve.wait_ge(S("d_b_mm"), k + 1)
                        if c == 0 and g >= 3:
                            dve.wait_ge(S("d_y_mm"), n * G + g - 2)
                        r2 = d_r2[:, g % 3, c, :]
                        tt(r2, bank("d_b", k), d_r[:, k % 4, :], ALU.mult).then_inc(S("d_r2"), 1)

                def add(g):
                    dve.wait_ge(S("d_y_mm"), n * G + g + 1)
                    xg = x[:, TG * g:TG * g + TG, :].rearrange("p t f -> p (t f)")
                    tt(xg, bank(f"d_y{n}", g), xg, ALU.add).then_inc(S("x_sum"), 1)
                phase("D", stats=ln_stats(u, x), apply=ln_apply(u, x), route=route, gate=gated, add=add)

            if "D" in PH:
                moe(0, LN_D0, "D")

            def z_init(g):
                dve.wait_ge(*ln("ln_rs", LN_Z, g))
                normalise(LN_Z, x, g, z, rstd).then_inc(S("z_in"), 1)

            def e_layer(l):
                def softmax(g):
                    n = l * G + g
                    dve.wait_ge(S("e_k_mm"), n + 1)
                    dve.tensor_reduce(e_km[:, g, :], bank("e_k", n).rearrange("p (b t) -> p b t", b=NB), X, ALU.max,
                                      negate=True).then_inc(S("e_kmax"), 1)
                    dve.wait_ge(S("e_q_mm"), n + 1)
                    o = bank("e_q", n).rearrange("p (h d) -> p h d", d=DE)
                    q3 = e_qe[:, g % 2, :].rearrange("p (h d) -> p h d", d=DE)
                    bc = lambda a: a.unsqueeze(2).to_broadcast([P, TG * HE, DE])
                    dve.tensor_reduce(e_qm[:, g, 0, :], o, X, ALU.max).then_inc(S("dve_own"), 1)
                    dve.wait_ge(S("dve_own"), next_own())
                    if n >= 2:
                        dve.wait_ge(S("e_qT_mm"), n - 1)
                    tt(q3, o, bc(e_qm[:, g, 0, :]), ALU.subtract).then_inc(S("e_qsub"), 1)

                def q_norm(g):
                    n = l * G + g
                    q3 = e_qe[:, g % 2, :].rearrange("p (h d) -> p h d", d=DE)
                    bc = lambda a: a.unsqueeze(2).to_broadcast([P, TG * HE, DE])
                    dve.wait_ge(S("e_qexp"), n + 1)
                    dve.tensor_reduce(e_qm[:, g, 1, :], q3, X, ALU.add).then_inc(S("dve_own"), 1)
                    dve.wait_ge(S("dve_own"), next_own())
                    dve.reciprocal(e_qm[:, g, 2, :], e_qm[:, g, 1, :]).then_inc(S("e_qrec"), 1)
                    dve.wait_ge(S("e_kexp"), NB * (n + 1))
                    dve.reciprocal(e_kr[:, g, :], e_ks[:, g, :]).then_inc(S("e_krec"), 1)

                def context(g):
                    n = l * G + g
                    dve.wait_ge(S("e_c_mm"), n + 1)
                    if n >= 2:
                        dve.wait_ge(S("e_m_mm"), n - 1)
                    tt(e_ctx[:, g % 2], bank("e_c", n)[:, 0:NB * P].rearrange("p (b d) -> p b d", d=P),
                       bd16[:, :, :].rearrange("p h d -> p (h d)").unsqueeze(1).to_broadcast([P, NB, P]),
                       ALU.mult).then_inc(S("e_ctx"), 1)

                def add1(g):
                    n = l * G + g
                    dve.wait_ge(S("e_zb"), n + 1)
                    dve.wait_ge(S("e_y_mm"), n + 1)
                    zg = z[:, TG * g:TG * g + TG, :].rearrange("p t f -> p (t f)")
                    tt(zg, bank("e_y", n), zg, ALU.add).then_inc(S("e_z1"), 1)

                def leaky(half):
                    def stage(g):
                        n = l * G + g
                        for c in (2 * half, 2 * half + 1):
                            dve.wait_ge(S("e_hs"), NF * n + c + 1)
                            h = e_h[:, g % 3, c * TOK:(c + 1) * TOK]
                            tt(h, bank("e_u", NF * n + c), h, ALU.max).then_inc(S("e_h"), 1)
                    return stage

                def add2(g):
                    n = l * G + g
                    dve.wait_ge(S("e_d_mm"), n + 1)
                    zg = z[:, TG * g:TG * g + TG, :].rearrange("p t f -> p (t f)")
                    tt(zg, bank("e_d", n), zg, ALU.add).then_inc(S("e_z2"), 1)
                u = LN_E + 2 * l
                phase("E", stats_1=ln_stats(u, z), apply_1=ln_apply(u, z), softmax=softmax, q_norm=q_norm,
                              mask=context, add_1=add1, stats_2=ln_stats(u + 1, z),
                              apply_2=ln_apply(u + 1, z), leaky_a=leaky(0), leaky_b=leaky(1), add_2=add2)

            def e_add(g):
                dve.wait_ge(S("e_z2"), (DEPTH - 1) * G + g + 1)
                xg = x[:, TG * g:TG * g + TG, :].rearrange("p t f -> p (t f)")
                tt(xg, z[:, TG * g:TG * g + TG, :].rearrange("p t f -> p (t f)"), xg, ALU.add).then_inc(S("x_sum"), 1)

            if "E" in PH:
                phase("Z", stats=ln_stats(LN_Z, x), apply=z_init)
                for l in range(DEPTH):
                    e_layer(l)
                phase("X", add=e_add)
            if "d" in PH:
                moe(1, LN_D1, "d")
            pipeline(stages, G)

        @block.scalar
        def _(act):
            stages = []

            def phase(key, **own):
                stages.append((key, own))

            def ln_out(u, w_col=None, b_col=None):
                def stage(g):
                    act.wait_ge(*ln("ln_T", u, g))
                    if u == LN_E and g == 0:
                        act.wait_ge(S("prep_out"), PREP_OUT[6])
                    if w_col is None:
                        act.activation(xnT[:, g, :], bank(f"ln{u}", g), ACT.Copy).then_inc(ln("ln_xT", u, g)[0], 1)
                    else:
                        act.activation(xnT[:, g, :], bank(f"ln{u}", g), ACT.Identity, bias=b_col, scale=w_col)\
                            .then_inc(ln("ln_xT", u, g)[0], 1)
                return stage

            def a_query(g):
                act.wait_ge(S("a_u_mm"), g + 1)
                if g >= 2:
                    act.wait_ge(S("a_s_mm"), NB * (g - 1))
                act.activation(a_uT[:, g % 2, :], bank("a_u", g), ACT.Copy).then_inc(S("a_uT"), 1)

            def a_exp(g):
                for b in range(NB):
                    n = NB * g + b
                    act.wait_ge(S("a_nmax"), n + 1)
                    if g >= 2:
                        act.wait_ge(S("a_pT_mm"), NB * (g - 2) + b + 1)
                    o = bank("a_s", n)
                    for j, (c0, c1) in enumerate(((0, P), (P, 384))):
                        act.activation(a_p[:, g % 2, b, c0:c1], o[:, c0:c1], ACT.Exp, bias=a_nmax[:, 1, 2 * n + j:2 * n + j + 1],
                                       scale=P ** -0.5, accum_out=a_sum[:, 0, 2 * n + j:2 * n + j + 1])\
                            .then_inc(S("a_exp"), 1)

            def a_turned(g):
                act.wait_ge(S("a_pT_mm"), NB * g + 1)
                if g >= 2:
                    act.wait_ge(S("a_o_mm"), g - 1)
                act.activation(a_pT[:, g % 2, 0, :], bank("a_pT", NB * g)[:, 0:384], ACT.Copy).then_inc(S("a_pT0"), 1)

            if "A" in PH:
                phase("A", turned_x=ln_out(LN_A), evacuate=a_query, exp=a_exp, turned=a_turned)

            def ffn(n, u, key):
                def gelu(g):
                    if g == 0 and n == 1:
                        act.wait_ge(S("x_sum"), G * PH.index(key))
                    if g >= 3:
                        act.wait_ge(S("f_y_mm"), n * G + g - 2)
                    for c in range(NF):
                        k = NF * (n * G + g) + c
                        act.wait_ge(S("f_h_mm"), k + 1)
                        act.activation(f_hT[n][:, g % 3, c * TOK:(c + 1) * TOK], bank(f"f_h{n}", NF * g + c),
                                       ACT.Gelu).then_inc(S("f_gelu"), 1)

                def square(g):
                    act.wait_ge(S("f_gelu"), NF * (n * G + g + 1))
                    if g >= 2:
                        act.wait_ge(S("f_ssq"), n * G + g - 1)
                    act.activation(f_sq[n][:, g % 2, :], f_hT[n][:, g % 3, :], ACT.Square).then_inc(S("f_sq"), 1)
                phase("F", turned_x=ln_out(u), gelu=gelu, square=square)

            if "F" in PH:
                ffn(0, LN_F0, "F")

            def b_softmax(g):
                if g == 0:
                    act.wait_ge(S("x_sum"), G * PH.index("B"))

                def q_exp(j):
                    n = TG * g + j
                    act.wait_ge(S("b_qsub"), 2 * (n + 1))
                    qt = b_q[:, g % 2, j, :]
                    act.activation(qt, qt, ACT.Exp, scale=QD ** -0.5).then_inc(S("b_qexp"), 1)

                def k_exp(c):
                    n = NC_ * g + c
                    act.wait_ge(S("b_kmax"), n + 1)
                    if n >= 4:
                        act.wait_ge(S("b_kT_mm"), n - 3)
                    if c == 0 and g >= 2:
                        act.wait_ge(S("b_krec"), g - 1)
                    for b in range(NB):
                        act.activation(b_kTe[:, n % 4, b * SEQ:(b + 1) * SEQ], bank("b_k", n)[:, b * SEQ:(b + 1) * SEQ],
                                       ACT.Exp, bias=b_kmax[:, n, b:b + 1], accum_out=b_ksum[:, g % 2, b, c:c + 1])\
                            .then_inc(S("b_kexp"), 1)

                def k_turned(c):
                    n = NC_ * g + c
                    if g >= 2 and c == 0:
                        act.wait_ge(S("b_c_mm"), 2 * NB * (g - 1))
                    act.wait_ge(S("b_kT_mm"), n + 1)
                    act.activation(b_k[:, g % 2, :, c * P:(c + 1) * P],
                                   bank("b_kT", n).rearrange("p (t f) -> p t f", f=P), ACT.Copy).then_inc(S("b_k"), 1)

                for c in range(NC_ + 2):
                    if c < NC_:
                        k_exp(c)
                        if c % 2 == 0:
                            q_exp(c // 2)
                    if c >= 2:
                        k_turned(c - 2)

            def b_fold(g):
                for b in range(NB):
                    n = NB * g + b
                    if n >= 2:
                        act.wait_ge(S("b_g_mm"), n - 1)
                    for half in range(2):
                        act.wait_ge(S("b_m_mm"), 2 * n + half + 1)
                        act.activation(b_m[:, n % 2, 4 * half:4 * half + 4, :].rearrange("p c f -> p (c f)"),
                                       bank("b_m", 2 * n + half), ACT.Copy).then_inc(S("b_m"), 1)

            if "B" in PH:
                phase("B", turned_x=ln_out(LN_B), heads=b_softmax, fold=b_fold)
            if "f" in PH:
                ffn(1, LN_F1, "f")

            def c_proj(n):
                if n == 0:
                    act.wait_ge(S("x_sum"), G * PH.index("C"))
                act.wait_ge(S("c_q_mm"), n + 1)
                if n >= 1:
                    act.wait_ge(S("c_spread_mm"), 8 * n)
                act.activation(c_split[:, 0, 0:2 * SEQ], bank("c_q", n), ACT.Copy).then_inc(S("c_high"), 1)
                act.wait_ge(S("c_k_mm"), n + 1)
                act.activation(c_split[:, 0, 2 * SEQ:3 * SEQ], bank("c_k", n)[:, 0:SEQ], ACT.Copy)\
                    .then_inc(S("c_high"), 1)
                if n == 0:
                    for i in range(4):
                        c_queries(n, i)

            def c_queries(n, i):
                m = 4 * n + i
                act.wait_ge(S("c_spread_mm"), 2 * m + 1)
                if m >= 6:
                    act.wait_ge(S("c_l_mm"), 4 * (m - 5))
                act.activation(c_spread[:, m % 6, :], bank("c_qs", m), ACT.Copy).then_inc(S("c_spread"), 1)

            def c_heads(n):
                if n == 0:
                    act.wait_ge(S("c_zero"), 6)

                def square(i):
                    m = 4 * n + i
                    if m >= 2:
                        act.wait_ge(S("c_lin_mm"), m - 1)
                    for r in range(2):
                        act.wait_ge(S("c_l_mm"), 4 * m + r + 1)
                        act.activation(c_a0[:, m % 2, 2 * r:2 * r + 2, :].rearrange("p h q -> p (h q)"),
                                       bank("c_l0", 2 * m + r), ACT.Square, bias=ones[:, 0:1], scale=0.5)\
                            .then_inc(S("c_sqr"), 1)
                    for r in range(2):
                        act.wait_ge(S("c_l_mm"), 4 * m + r + 3)
                        act.activation(c_a1[:, m % 2, 2 * r:2 * r + 2, :],
                                       bank("c_l1", 2 * m + r).rearrange("p (h q) -> p h q", q=SEQ)[:, :, P:SEQ],
                                       ACT.Square, bias=ones[:, 0:1], scale=0.5).then_inc(S("c_sqr"), 1)

                def exp(i):
                    m = 4 * n + i
                    act.wait_ge(S("c_sub"), 3 * m + 1)
                    p0 = c_p0[:, m % 2].rearrange("p h k -> p (h k)")
                    act.activation(p0, p0, ACT.Exp, scale=DC ** -0.5).then_inc(S("c_exp"), 1)
                    act.wait_ge(S("c_sub"), 3 * m + 3)
                    p1 = c_p1[:, m % 2, :, 64:SEQ]
                    act.activation(p1, p1, ACT.Exp, scale=DC ** -0.5).then_inc(S("c_exp"), 1)

                def turn_out(i):
                    m = 4 * n + i
                    if m >= 2:
                        act.wait_ge(S("c_win_mm"), m - 1)
                    for r in range(2):
                        act.wait_ge(S("c_t_mm"), 3 * m + 2 + r)
                        act.activation(c_pT[:, m % 2, 1 + r, :], bank("c_t0", 3 * m + 1 + r), ACT.Copy)\
                            .then_inc(S("c_pT_act"), 1)

                for i in range(4):
                    exp(i)
                    square(i)
                    turn_out(i)
                    if n + 1 < NB * G:
                        c_queries(n + 1, i)
                    if n > 0 and i == 1:
                        c_out(n - 1)

            def c_out(n):
                act.wait_ge(S("c_cT_mm"), n + 1)
                if n >= 1:
                    act.wait_ge(S("c_y_mm"), n)
                act.activation(c_catT.rearrange("p f t -> p (f t)"), bank("c_cT", n), ACT.Copy)\
                    .then_inc(S("c_catT"), 1)

            if "C" in PH:
                phase("C", turned_x=ln_out(LN_C), **by_sequence(c_proj, c_heads, lambda: c_out(NB * G - 1)))

            def moe(n, u, key):
                def up(g):
                    if g == 0:
                        act.wait_ge(S("x_sum"), G * PH.index(key))
                    k = n * G + g
                    act.wait_ge(S("d_g_mm"), k + 1)
                    act.activation(d_e[:, g, :], bank(f"d_g{n}", g)[:, 0:TG * NE], ACT.Exp, scale=-1.0)\
                        .then_inc(S("d_exp"), 1)
                    if g >= 3:
                        act.wait_ge(S("d_y_mm"), k - 2)
                    for c in range(NF):
                        s = d_r2[:, g % 3, NF + c, :]
                        act.wait_ge(S("d_s_mm"), NF * k + c + 1)
                        act.activation(s, bank("d_s", NF * k + c), ACT.Relu).then_inc(S("d_srelu"), 1)
                        act.wait_ge(S("d_srelu"), NF * k + c + 1)
                        act.activation(s, s, ACT.Square).then_inc(S("d_sq"), 1)

                def gates_out(g):
                    act.wait_ge(S("d_pT_mm"), n * G + g + 1)
                    if g >= 2:
                        act.wait_ge(S("d_b_mm"), NF * (n * G + g - 1))
                    act.activation(d_partsT[0:96, g % 2, :], bank("d_pT", n * G + g).bitcast(BF16)[0:96, 0:TOK],
                                   ACT.Copy).then_inc(S("d_partsT"), 1)

                def experts(g):
                    for c in range(NF):
                        k = (n * G + g) * NF + c
                        act.wait_ge(S("d_u_mm"), k + 1)
                        if k >= 4:
                            act.wait_ge(S("d_r2"), k - 3)
                        act.activation(d_r[:, k % 4, :], bank("d_u", k), ACT.Relu).then_inc(S("d_relu"), 1)
                        act.wait_ge(S("d_relu"), k + 1)
                        act.activation(d_r[:, k % 4, :], d_r[:, k % 4, :], ACT.Square).then_inc(S("d_rsq"), 1)
                phase("D", turned_x=ln_out(u), shared=up, gates_out=gates_out, experts=experts)

            if "D" in PH:
                moe(0, LN_D0, "D")

            def e_layer(l):
                def softmax(g):
                    n = l * G + g
                    if n == 0:
                        act.wait_ge(S("x_sum"), G * PH.index("E"))
                    act.wait_ge(S("e_kmax"), n + 1)
                    if n >= 2:
                        act.wait_ge(S("e_kT_mm"), n - 1)
                    if n >= G:
                        act.wait_ge(S("e_krec"), n - G + 1)
                    for b in range(NB):
                        act.activation(e_kTe[:, g % 2, b * SEQ:(b + 1) * SEQ], bank("e_k", n)[:, b * SEQ:(b + 1) * SEQ],
                                       ACT.Exp, bias=e_km[:, g, b:b + 1], accum_out=e_ks[:, g, b:b + 1])\
                            .then_inc(S("e_kexp"), 1)
                    act.wait_ge(S("e_qsub"), n + 1)
                    act.activation(e_qe[:, g % 2, :], e_qe[:, g % 2, :], ACT.Exp).then_inc(S("e_qexp"), 1)
                    act.wait_ge(S("e_v_mm"), n + 1)
                    if n >= 3:
                        act.wait_ge(S("e_c_mm"), n - 2)
                    act.activation(e_v[:, g % 3, :], bank("e_v", n), ACT.Copy).then_inc(S("e_v"), 1)

                def k_out(g):
                    n = l * G + g
                    act.wait_ge(S("e_kT_mm"), n + 1)
                    if n >= 2:
                        act.wait_ge(S("e_c_mm"), n - 1)
                    act.activation(e_k[:, g % 2, :], bank("e_kT", n), ACT.Copy).then_inc(S("e_k"), 1)

                def turn_out(g):
                    n = l * G + g
                    act.wait_ge(S("e_qT_mm"), n + 1)
                    if n >= G:
                        act.wait_ge(S("e_y_mm"), n - G + 1)
                    act.activation(e_qT[:, g, :], bank("e_qT", n), ACT.Copy).then_inc(S("e_qT"), 1)

                def divide_k(g):
                    n = l * G + g
                    act.wait_ge(S("e_m_mm"), n + 1)
                    act.wait_ge(S("e_krec"), n + 1)
                    if n >= 2:
                        act.wait_ge(S("e_y_mm"), n - 1)
                    for b in range(NB):
                        last = act.activation(e_m[:, g % 2, b, :], bank("e_m", n)[:, b * P:(b + 1) * P], ACT.Copy,
                                              scale=e_kr[:, g, b:b + 1])
                    last.then_inc(S("e_m"), 1)

                def slope(half):
                    def stage(g):
                        n = l * G + g
                        if n >= 3:
                            act.wait_ge(S("e_d_mm"), n - 2)
                        for c in (2 * half, 2 * half + 1):
                            act.wait_ge(S("e_u_mm"), NF * n + c + 1)
                            act.activation(e_h[:, g % 3, c * TOK:(c + 1) * TOK], bank("e_u", NF * n + c), ACT.Copy,
                                           scale=0.01).then_inc(S("e_hs"), 1)
                    return stage
                u = LN_E + 2 * l
                phase("E", out_1=ln_out(u, col(0, l), col(1, l)), exp=softmax, k_out=k_out, scale=divide_k, q_out=turn_out,
                              out_2=ln_out(u + 1, col(2, l), col(3, l)), slope_a=slope(0), slope_b=slope(1))

            if "E" in PH:
                phase("Z")
                for l in range(DEPTH):
                    e_layer(l)
                phase("X")
            if "d" in PH:
                moe(1, LN_D1, "d")
            pipeline(stages, G)

        @block.gpsimd
        def _(pool):
            stages = []

            def phase(key, **own):
                stages.append((key, own))

            chain = [0]

            def link(ins):
                chain[0] += 1
                ins.then_inc(S("pool_chain"), 1)
                pool.wait_ge(S("pool_chain"), chain[0])

            def select(o, pattern, base, mult, fill, op=ALU.is_ge):
                link(pool.affine_select(out=o, in_=o, pattern=pattern, compare_op=op, fill=fill, base=base,
                                        channel_multiplier=mult))

            link(pool.memset(ident[:, :], 0.0))
            select(ident[:, :], [[-1, P]], 0, 1, 1.0, ALU.not_equal)
            link(pool.memset(ones[:, :], 1.0))
            link(pool.memset(causal_bf, 0.0))
            select(causal_bf[:, 0:P], [[-1, P]], 0, 1, NEG)
            select(causal_bf[:, P:384], [[-1, SEQ]], P, 1, NEG)
            pool.memset(neg_half[:, :], -0.5).then_inc(S("masks"), 1)
            link(pool.memset(window_bf[:, :], 0.0))
            for c0, c1, off in ((0, P, 0), (P, 320, 64)):
                select(window_bf[:, c0:c1], [[-1, c1 - c0]], off, 1, NEG)
                select(window_bf[:, c0:c1], [[1, c1 - c0]], 64 - off, -1, NEG)
            for m, d, nh in ((head8, DC, HC), (head16, DE, HE)):
                link(pool.memset(m[:, :], 1.0))
                select(m[:, :], [[-d, nh]], 0, 1, 0.0)
                select(m[:, :], [[d, nh]], d - 1, -1, 0.0)
            link(pool.memset(lower[:, :, :], 1.0))
            select(lower[:, :, :], [[1, NE], [-1, NE]], -1, 0, 0.0)
            link(pool.memset(gate_sel[:, :, :], 0.0))
            for i in range(3):
                select(gate_sel[:, :, :].rearrange("p c (a m) -> p c a m", a=2), [[-2, NF], [-1, 2], [0, 64]], -32 * i, 1,
                       1.0, ALU.not_equal)
            pool.memset(pos_half[:, :], 0.5).then_inc(S("masks"), 1)

            def rsqrt(u):
                def stage(g):
                    ts = slice(TG * g, TG * g + TG)
                    pool.wait_ge(*ln("ln_ve", u, g))
                    pool.tensor_tensor(rstd[:, ts], var_eps[:, ts], neg_half[:, :], ALU.pow).then_inc(ln("ln_rs", u, g)[0], 1)
                return stage

            if "A" in PH:
                phase("A", rsqrt=rsqrt(LN_A))

            def ffn(n, u):
                def rms(g):
                    ts = slice(TG * g, TG * g + TG)
                    pool.wait_ge(S("s2_b"), S2[u] * G + g + 1)
                    pool.tensor_tensor(second[:, 2, ts], second[:, 1, ts], pos_half[:, :], ALU.pow).then_inc(S("s2_pow"), 1)

                def rms_h(g):
                    ts = slice(TG * g, TG * g + TG)
                    pool.wait_ge(S("f_ms"), n * G + g + 1)
                    pool.tensor_tensor(f_r[n][:, 1, ts], f_r[n][:, 0, ts], pos_half[:, :], ALU.pow).then_inc(S("f_pow"), 1)
                own = {"constants": c_constants} if n == 1 else {}
                phase("F", rsqrt=rsqrt(u), second_root=rms, root=rms_h, **own)

            if "F" in PH:
                ffn(0, LN_F0)

            def b_bias(g):
                pool.wait_ge(*ln("ln_xn", LN_B, g))
                xg = x[:, TG * g:TG * g + TG, :]
                pool.tensor_tensor(xg, xg, bout_bc[:, :].unsqueeze(1).to_broadcast([P, TG, P]), ALU.add)\
                    .then_inc(S("b_xb"), 1)

            def b_norm(g):
                for j in range(TG):
                    n = TG * g + j
                    pool.wait_ge(S("b_qrec"), n + 1)
                    qt = b_q[:, g % 2, j, :].rearrange("p (h d) -> p h d", d=QD)
                    pool.tensor_tensor(qt, qt, b_qrec[:, n % 4, :].unsqueeze(2).to_broadcast([P, QH, QD]), ALU.mult)\
                        .then_inc(S("b_qn"), 1)

            if "B" in PH:
                phase("B", rsqrt=rsqrt(LN_B), bias=b_bias, heads=b_norm)
            def c_constants(g):
                if g == 0:
                    pool.wait_ge(S("x_sum"), G * PH.index("f"))
                if g < 2:
                    pick_rows(g)
                if g == 2:
                    link(pool.memset(quarter, 1.0))
                    select(quarter, [[-32, 4]], 0, 1, 0.0)
                    pool.affine_select(out=quarter, in_=quarter, pattern=[[32, 4]], compare_op=ALU.is_ge, fill=0.0,
                                       base=31, channel_multiplier=-1).then_inc(S("c_pick"), 1)
                if g == 3:
                    for i in range(4):
                        pool.wait_ge(S("c_clear"), i + 1)
                        pool.memset(own_sums(i), 1.0).then_inc(S("c_zero"), 1)
                    for i in range(2):
                        pool.memset(c_p1[:, i, :, 0:64], 0.0).then_inc(S("c_zero"), 1)

            def pick_rows(i):
                pick, rows = ((pick_q, (slice(0, 2), slice(2, 4))), (pick_k, (slice(0, 4, 2), slice(1, 4, 2))))[i]
                pool.wait_ge(S("c_blank"), i + 1)
                for part in range(2):
                    o = pick[:, part, :].rearrange("p (h j d) -> p h j d", h=HC, j=4)[:, :, rows[part], :]
                    pool.affine_select(out=o, in_=o, pattern=[[-DC, HC], [0, 2], [-1, DC]], compare_op=ALU.not_equal,
                                       fill=1.0, base=0, channel_multiplier=1).then_inc(S("c_pick"), 1)

            if "f" in PH:
                ffn(1, LN_F1)

            def c_rms(g):
                ts = slice(TG * g, TG * g + TG)
                pool.wait_ge(S("c_ms"), g + 1)
                pool.tensor_tensor(second[:, 2, ts], second[:, 0, ts], neg_half[:, :], ALU.pow).then_inc(S("s2_pow"), 1)

            def c_residual(g):
                pool.wait_ge(S("c_ln"), g + 1)
                xg = x[:, TG * g:TG * g + TG, :]
                pool.tensor_tensor(xg, xg, z[:, TG * g:TG * g + TG, :], ALU.add).then_inc(S("c_xz"), 1)

            def c_mask(n):
                for i in range(4):
                    m = 4 * n + i
                    for k, (a, need) in enumerate(((c_a0[:, m % 2, :, 0:P], 4 * m + 2), (c_a1[:, m % 2], 4 * m + 4))):
                        pool.wait_ge(S("c_sqr"), need)
                        pool.affine_select(out=a, in_=a, pattern=[[0, 4], [1, P]], compare_op=ALU.is_ge, fill=0.0,
                                           base=0, channel_multiplier=-1).then_inc(S("c_mask"), 1)

            if "C" in PH:
                phase("C", rsqrt=rsqrt(LN_C), second_root=c_rms, residual=c_residual, **by_sequence(None, c_mask, None))
            if "D" in PH:
                phase("D", rsqrt=rsqrt(LN_D0))

            def e_layer(l):
                def bias(g):
                    if l == 0 and g == 0:
                        pool.wait_ge(S("e_bo_in"), 16)
                    pool.wait_ge(*ln("ln_xn", LN_E + 2 * l, g))
                    zg = z[:, TG * g:TG * g + TG, :]
                    pool.tensor_tensor(zg, zg, bo_bc[:, l, :].unsqueeze(1).to_broadcast([P, TG, P]), ALU.add)\
                        .then_inc(S("e_zb"), 1)
                def divide(g):
                    n = l * G + g
                    pool.wait_ge(S("e_qrec"), n + 1)
                    q3 = e_qe[:, g % 2, :].rearrange("p (h d) -> p h d", d=DE)
                    pool.tensor_tensor(q3, q3, e_qm[:, g, 2, :].unsqueeze(2).to_broadcast([P, TG * HE, DE]), ALU.mult)\
                        .then_inc(S("e_qn"), 1)
                phase("E", divide=divide, rsqrt_1=rsqrt(LN_E + 2 * l), bias=bias, rsqrt_2=rsqrt(LN_E + 2 * l + 1))

            if "E" in PH:
                phase("Z", rsqrt=rsqrt(LN_Z))
                for l in range(DEPTH):
                    e_layer(l)
                phase("X")
            if "d" in PH:
                phase("D", rsqrt=rsqrt(LN_D1))
            pipeline(stages, G)


PREP_OUT = [1, 3, 4, 5, 6, 7, 9, 10, 11, 12, 13, 15, 16, 17, 18, 19]
S2 = {1: 0, 3: 1, 4: 2}
LN_PH = {1: 0, 2: 1, 3: 2, 4: 3, 5: 4, 6: 5, 19: 6}
STEPS = {
    "A": (14, 2, {"stats": 0, "rsqrt": 1, "apply": 2, "turn": 3, "turned_x": 4, "project": 5, "evacuate": 6,
                  "prepare": 6, "scores": 7, "max": 8, "exp": 9, "turn_p": 10, "turned": 11, "out": 12,
                  "add": 13}),
    "F": (15, 2, {"stats": 0, "rsqrt": 0, "prepare": 0, "second_scale": 1, "second_root": 1, "apply": 3,
                  "turn": 4, "turned_x": 5, "up": 7, "gelu": 8, "square": 9, "blank": 9, "squares": 10,
                  "constants": 11, "down": 11, "mean_square": 12, "root": 13, "add": 14}),
    "B": (10, 3, {"stats": 0, "rsqrt": 1, "apply": 2, "turn": 3, "bias": 3, "turned_x": 4, "heads": 5,
                  "context": 6, "mask": 7, "fold": 7, "out": 8, "add": 9}),
    "C": (10, 2, {"stats": 0, "rsqrt": 1, "second_scale": 2, "second_root": 3, "residual": 3, "apply": 4,
                  "turn": 5, "turned_x": 5, "sequences": 6, "last": 7}),
    "D": (11, 2, {"stats": 0, "rsqrt": 1, "apply": 2, "turn": 3, "turned_x": 3, "up": 4, "shared": 4, "route": 5,
                  "turn_gate": 6, "gates_out": 6, "experts": 7, "gate": 7, "down": 9, "add": 9}),
    "Z": (3, 5, {"stats": 0, "rsqrt": 1, "apply": 2}),
    "E": (29, 5, {"stats_1": 0, "rsqrt_1": 2, "apply_1": 3, "turn_1": 4, "bias": 4, "out_1": 5, "qkv": 6,
                  "softmax": 7, "exp": 8, "turn_k": 9, "q_norm": 9, "k_out": 10, "divide": 10, "turn_q": 12,
                  "context": 12, "q_out": 13, "mask": 13, "fold": 14, "scale": 15, "out": 16, "add_1": 17,
                  "stats_2": 18, "rsqrt_2": 19, "apply_2": 20, "turn_2": 21, "out_2": 22, "up_a": 23,
                  "slope_a": 24, "up_b": 24, "leaky_a": 25, "slope_b": 25, "leaky_b": 25, "down_a": 27,
                  "down_b": 27, "add_2": 28}),
    "X": (1, 5, {"add": 0}),
}
PHASES = "AFBfCDEd"

_INS = ['L0_attn_a_x', 'L0_attn_a_W_query', 'L0_attn_a_W_key', 'L0_attn_a_W_value', 'L0_attn_b_Wqkv', 'L0_attn_b_Wout',
        'L0_attn_b_bout', 'L0_ffn_w_up', 'L0_ffn_w_down', 'L1_attn_a_norm_w', 'L1_attn_a_Wq', 'L1_attn_a_Wk',
        'L1_attn_a_Wv', 'L1_attn_a_Wqf', 'L1_attn_a_Wkf', 'L1_attn_a_Wout', 'L1_attn_b_ln1_w', 'L1_attn_b_ln1_b',
        'L1_attn_b_wq', 'L1_attn_b_wk', 'L1_attn_b_wv', 'L1_attn_b_wo', 'L1_attn_b_bo', 'L1_attn_b_ln2_w',
        'L1_attn_b_ln2_b', 'L1_attn_b_w1', 'L1_attn_b_w2', 'L1_ffn_gate', 'L1_ffn_corr_bias', 'L1_ffn_w1', 'L1_ffn_w2',
        'L1_ffn_fc1_w', 'L1_ffn_fc2_w', 'L1_ffn_up_w', 'L1_ffn_down_w']


def kernel(**inputs):
    import numpy as _np
    import concourse.bacc as _bacc
    from concourse.bass_utils import run_bass_kernel_spmd as _run

    nc = _bacc.Bacc("TRN2", target_bir_lowering=False, num_devices=1)
    arrays, args = {}, {}
    for name in _INS:
        a = _np.ascontiguousarray(inputs[name])
        arrays[f"in_{name}"] = a
        args[name] = nc.dram_tensor(f"in_{name}", a.shape, mybir.dt.from_np(a.dtype), kind="ExternalInput").ap()
    out = nc.dram_tensor("out", inputs['L0_attn_a_x'].shape, F32, kind="ExternalOutput").ap()
    hybrid_program(nc, args, out)
    r = _run(nc, [arrays], core_ids=[0])
    return r.results[0]["out"]
```
